# Optimizing a Trainium2 kernel written in Bass

```python
import numpy as np
import jax
import jax.numpy as jnp

def _softmax(x, axis=-1):
    return jax.nn.softmax(x, axis=axis)

def _gelu(x):
    return jax.nn.gelu(x, approximate=True)

def _silu(x):
    return jax.nn.silu(x)

def _sigmoid(x):
    return jax.nn.sigmoid(x)

def _layernorm(x, axis=-1, eps=1e-05):
    m = jnp.mean(x, axis=axis, keepdims=True)
    v = jnp.var(x, axis=axis, keepdims=True)
    return (x - m) / jnp.sqrt(v + eps)

def _scatter_add(tgt, idx, src, axis=0):
    return tgt.at[idx].add(src)

def _segment_sum(src, seg, n):
    return jax.ops.segment_sum(src, seg, n)
kernel_name = 'mk_sandwich_d2_jaxref_r8_72d48a'

def setup_inputs(seed: int=0):
    np.random.seed(seed)
    _w = jnp.asarray

    def _L0_attn_setup():
        import jax, jax.numpy as jnp
        import numpy as np
        DIM = 128
        DEPTH = 6
        HEADS = 8
        FF_MULT = 4
        LN_EPS = 1e-05
        LEAKY_SLOPE = 0.01

        def _layernorm(x, w, b):
            m = jnp.mean(x, axis=-1, keepdims=True)
            v = jnp.mean(jnp.square(x - m), axis=-1, keepdims=True)
            return (x - m) * jax.lax.rsqrt(v + LN_EPS) * w + b

        def _linear_attn(q, k, v):
            q = jax.nn.softmax(q, axis=-1)
            k = jax.nn.softmax(k, axis=-2)
            context = jnp.einsum('bhnd,bhne->bhde', k, v)
            return jnp.einsum('bhnd,bhde->bhne', q, context)
        key = jax.random.key(seed)
        ks = jax.random.split(key, 12)
        b, t = (2, 512)
        s = 0.02
        return {'x': jax.random.normal(ks[0], (b, t, DIM), dtype=jnp.float32), 'ln1_w': jnp.ones((DEPTH, DIM), jnp.float32), 'ln1_b': jnp.zeros((DEPTH, DIM), jnp.float32), 'wq': jax.random.normal(ks[1], (DEPTH, DIM, DIM), jnp.float32) * s, 'wk': jax.random.normal(ks[2], (DEPTH, DIM, DIM), jnp.float32) * s, 'wv': jax.random.normal(ks[3], (DEPTH, DIM, DIM), jnp.float32) * s, 'wo': jax.random.normal(ks[4], (DEPTH, DIM, DIM), jnp.float32) * s, 'bo': jnp.zeros((DEPTH, DIM), jnp.float32), 'ln2_w': jnp.ones((DEPTH, DIM), jnp.float32), 'ln2_b': jnp.zeros((DEPTH, DIM), jnp.float32), 'w1': jax.random.normal(ks[5], (DEPTH, DIM, FF_MULT * DIM), jnp.float32) * s, 'w2': jax.random.normal(ks[6], (DEPTH, FF_MULT * DIM, DIM), jnp.float32) * s}
    _L0_attn_in = _L0_attn_setup()

    def _L0_ffn_setup():
        import jax, jax.numpy as jnp
        import numpy as np
        import math
        BETA = 0.9
        THRESHOLD = 1.0
        NUM_STEPS = 5
        ALPHA = 2.0

        @jax.custom_vjp
        def spike_fn(u):
            return (u > 0).astype(u.dtype)

        def _spike_fwd(u):
            return (spike_fn(u), u)

        def _spike_bwd(u, g):
            s = jnp.pi / 2.0 * ALPHA * u
            return (g * (ALPHA / 2.0) / (1.0 + s * s),)
        spike_fn.defvjp(_spike_fwd, _spike_bwd)
        key = jax.random.key(seed)
        k1, k2, k3 = jax.random.split(key, 3)
        n_embd = 128
        x = jax.random.normal(k1, (4, 256, n_embd), dtype=jnp.float32)
        W_fc = jax.random.normal(k2, (4 * n_embd, n_embd), dtype=jnp.float32) / math.sqrt(n_embd)
        W_proj = jax.random.normal(k3, (n_embd, 4 * n_embd), dtype=jnp.float32) / math.sqrt(4 * n_embd)
        return {'x': x, 'W_fc': W_fc, 'W_proj': W_proj}
    _L0_ffn_in = _L0_ffn_setup()

    def _L1_attn_setup():
        import jax, jax.numpy as jnp
        import numpy as np
        import math
        D_MODEL = 128
        D_STATE = 64
        DT_MIN, DT_MAX = (0.001, 0.1)
        key = jax.random.key(seed)
        ks = jax.random.split(key, 8)
        x = jax.random.normal(ks[0], (2, 512, D_MODEL), dtype=jnp.float32)
        lim = 1.0 / math.sqrt(D_MODEL)
        Win = jax.random.uniform(ks[1], (D_MODEL, D_MODEL), minval=-lim, maxval=lim, dtype=jnp.float32)
        bin_ = jax.random.uniform(ks[2], (D_MODEL,), minval=-lim, maxval=lim, dtype=jnp.float32)
        Wout = jax.random.uniform(ks[3], (D_MODEL, D_MODEL), minval=-lim, maxval=lim, dtype=jnp.float32)
        bout = jax.random.uniform(ks[4], (D_MODEL,), minval=-lim, maxval=lim, dtype=jnp.float32)
        A_log = jnp.broadcast_to(jnp.log(jnp.arange(1, D_STATE + 1, dtype=jnp.float32)), (D_MODEL, D_STATE))
        B = 0.1 * jax.random.normal(ks[5], (D_MODEL, D_STATE), dtype=jnp.float32)
        C = 0.1 * jax.random.normal(ks[6], (D_MODEL, D_STATE), dtype=jnp.float32)
        Dp = jnp.ones((D_MODEL,), dtype=jnp.float32)
        log_dt = jax.random.uniform(ks[7], (D_MODEL,), dtype=jnp.float32) * (math.log(DT_MAX) - math.log(DT_MIN)) + math.log(DT_MIN)
        dt = jnp.exp(log_dt)
        return {'x': x, 'Win': Win, 'bin_': bin_, 'A_log': A_log, 'B': B, 'C': C, 'Dp': Dp, 'dt': dt, 'Wout': Wout, 'bout': bout}
    _L1_attn_in = _L1_attn_setup()

    def _L1_ffn_setup():
        import jax, jax.numpy as jnp
        import numpy as np
        DIM = 128

        def _reference_tuple_inner(x, W_r, W_k, W_v, mu_r, mu_k):
            B, T, C = x.shape
            x_prev = jnp.concatenate([jnp.zeros((B, 1, C), x.dtype), x[:, :-1, :]], axis=1)
            xr = mu_r * x + (1.0 - mu_r) * x_prev
            xk = mu_k * x + (1.0 - mu_k) * x_prev
            r = jax.nn.sigmoid(jnp.einsum('btc,dc->btd', xr, W_r))
            k = jnp.einsum('btc,dc->btd', xk, W_k)
            k_act = jnp.square(jax.nn.relu(k))
            out = r * jnp.einsum('btc,dc->btd', k_act, W_v)
            new_state = x[:, -1, :]
            return (out, new_state)
        key = jax.random.key(seed)
        ks = jax.random.split(key, 6)
        B, T, C = (8, 256, DIM)
        x = jax.random.normal(ks[0], (B, T, C), dtype=jnp.float32)
        s = 1.0 / np.sqrt(C)
        W_r = jax.random.uniform(ks[1], (C, C), jnp.float32, -s, s)
        W_k = jax.random.uniform(ks[2], (C, C), jnp.float32, -s, s)
        W_v = jax.random.uniform(ks[3], (C, C), jnp.float32, -s, s)
        mu_r = jax.random.uniform(ks[4], (C,), jnp.float32)
        mu_k = jax.random.uniform(ks[5], (C,), jnp.float32)
        return {'x': x, 'W_r': W_r, 'W_k': W_k, 'W_v': W_v, 'mu_r': mu_r, 'mu_k': mu_k}
    _L1_ffn_in = _L1_ffn_setup()
    _d = {'L0_attn_x': _L0_attn_in['x'], 'L0_attn_ln1_w': _L0_attn_in['ln1_w'], 'L0_attn_ln1_b': _L0_attn_in['ln1_b'], 'L0_attn_wq': _L0_attn_in['wq'], 'L0_attn_wk': _L0_attn_in['wk'], 'L0_attn_wv': _L0_attn_in['wv'], 'L0_attn_wo': _L0_attn_in['wo'], 'L0_attn_bo': _L0_attn_in['bo'], 'L0_attn_ln2_w': _L0_attn_in['ln2_w'], 'L0_attn_ln2_b': _L0_attn_in['ln2_b'], 'L0_attn_w1': _L0_attn_in['w1'], 'L0_attn_w2': _L0_attn_in['w2'], 'L0_ffn_W_fc': _L0_ffn_in['W_fc'], 'L0_ffn_W_proj': _L0_ffn_in['W_proj'], 'L1_attn_Win': _L1_attn_in['Win'], 'L1_attn_bin_': _L1_attn_in['bin_'], 'L1_attn_A_log': _L1_attn_in['A_log'], 'L1_attn_B': _L1_attn_in['B'], 'L1_attn_C': _L1_attn_in['C'], 'L1_attn_Dp': _L1_attn_in['Dp'], 'L1_attn_dt': _L1_attn_in['dt'], 'L1_attn_Wout': _L1_attn_in['Wout'], 'L1_attn_bout': _L1_attn_in['bout'], 'L1_ffn_W_r': _L1_ffn_in['W_r'], 'L1_ffn_W_k': _L1_ffn_in['W_k'], 'L1_ffn_W_v': _L1_ffn_in['W_v'], 'L1_ffn_mu_r': _L1_ffn_in['mu_r'], 'L1_ffn_mu_k': _L1_ffn_in['mu_k']}
    _x0 = _d['L0_attn_x']
    _d['L0_attn_x'] = jax.random.normal(jax.random.fold_in(jax.random.key(seed), 1), (8, 512, 128), dtype=_x0.dtype)
    del _x0
    return _d

def reference(L0_attn_x, L0_attn_ln1_w, L0_attn_ln1_b, L0_attn_wq, L0_attn_wk, L0_attn_wv, L0_attn_wo, L0_attn_bo, L0_attn_ln2_w, L0_attn_ln2_b, L0_attn_w1, L0_attn_w2, L0_ffn_W_fc, L0_ffn_W_proj, L1_attn_Win, L1_attn_bin_, L1_attn_A_log, L1_attn_B, L1_attn_C, L1_attn_Dp, L1_attn_dt, L1_attn_Wout, L1_attn_bout, L1_ffn_W_r, L1_ffn_W_k, L1_ffn_W_v, L1_ffn_mu_r, L1_ffn_mu_k):

    def _L0_attn_ref(x, ln1_w, ln1_b, wq, wk, wv, wo, bo, ln2_w, ln2_b, w1, w2):
        import jax, jax.numpy as jnp
        import numpy as np
        DIM = 128
        DEPTH = 6
        HEADS = 8
        FF_MULT = 4
        LN_EPS = 1e-05
        LEAKY_SLOPE = 0.01

        def _layernorm(x, w, b):
            m = jnp.mean(x, axis=-1, keepdims=True)
            v = jnp.mean(jnp.square(x - m), axis=-1, keepdims=True)
            return (x - m) * jax.lax.rsqrt(v + LN_EPS) * w + b

        def _linear_attn(q, k, v):
            q = jax.nn.softmax(q, axis=-1)
            k = jax.nn.softmax(k, axis=-2)
            context = jnp.einsum('bhnd,bhne->bhde', k, v)
            return jnp.einsum('bhnd,bhde->bhne', q, context)
        b, t, e = x.shape
        h, dh = (HEADS, e // HEADS)
        for i in range(DEPTH):
            xn = _layernorm(x, ln1_w[i], ln1_b[i])
            q = (xn @ wq[i]).reshape(b, t, h, dh).transpose(0, 2, 1, 3)
            k = (xn @ wk[i]).reshape(b, t, h, dh).transpose(0, 2, 1, 3)
            v = (xn @ wv[i]).reshape(b, t, h, dh).transpose(0, 2, 1, 3)
            attn = _linear_attn(q, k, v)
            attn = attn.transpose(0, 2, 1, 3).reshape(b, t, e)
            x = attn @ wo[i] + bo[i] + x
            xn = _layernorm(x, ln2_w[i], ln2_b[i])
            hdn = xn @ w1[i]
            hdn = jnp.where(hdn >= 0, hdn, LEAKY_SLOPE * hdn)
            x = hdn @ w2[i] + x
        return x

    def _L0_ffn_ref(x, W_fc, W_proj):
        import jax, jax.numpy as jnp
        import numpy as np
        import math
        BETA = 0.9
        THRESHOLD = 1.0
        NUM_STEPS = 5
        ALPHA = 2.0

        @jax.custom_vjp
        def spike_fn(u):
            return (u > 0).astype(u.dtype)

        def _spike_fwd(u):
            return (spike_fn(u), u)

        def _spike_bwd(u, g):
            s = jnp.pi / 2.0 * ALPHA * u
            return (g * (ALPHA / 2.0) / (1.0 + s * s),)
        spike_fn.defvjp(_spike_fwd, _spike_bwd)
        h = jnp.square(jax.nn.relu(jnp.einsum('bsd,fd->bsf', x, W_fc)))
        y = jnp.einsum('bsf,df->bsd', h, W_proj)

        def step(mem, _):
            reset = jax.lax.stop_gradient(spike_fn(mem - THRESHOLD))
            mem_new = BETA * mem + y - reset * THRESHOLD
            spk = spike_fn(mem_new - THRESHOLD)
            return (mem_new, spk)
        mem0 = jnp.zeros_like(y)
        _, spks = jax.lax.scan(step, mem0, None, length=NUM_STEPS)
        return jnp.sum(spks, axis=0) / NUM_STEPS

    def _L1_attn_ref(x, Win, bin_, A_log, B, C, Dp, dt, Wout, bout):
        import jax, jax.numpy as jnp
        import numpy as np
        import math
        D_MODEL = 128
        D_STATE = 64
        DT_MIN, DT_MAX = (0.001, 0.1)
        b, L, d = x.shape
        x = x @ Win.T + bin_
        u = jnp.transpose(x, (0, 2, 1))
        A = -jnp.exp(-A_log)
        logdA = A * dt[:, None]
        dB = B * dt[:, None]
        t = jnp.arange(L, dtype=x.dtype)
        powers = jnp.exp(logdA[:, :, None] * t)
        k = jnp.einsum('dn,dnl->dl', C * dB, powers)
        n_fft = 2 * L
        k_f = jnp.fft.rfft(k, n=n_fft)
        u_f = jnp.fft.rfft(u, n=n_fft)
        y = jnp.fft.irfft(u_f * k_f[None], n=n_fft)[..., :L]
        y = y + u * Dp[:, None]
        y = jnp.transpose(y, (0, 2, 1))
        return y @ Wout.T + bout

    def _L1_ffn_ref(x, W_r, W_k, W_v, mu_r, mu_k):
        import jax, jax.numpy as jnp
        import numpy as np
        DIM = 128

        def _reference_tuple_inner(x, W_r, W_k, W_v, mu_r, mu_k):
            B, T, C = x.shape
            x_prev = jnp.concatenate([jnp.zeros((B, 1, C), x.dtype), x[:, :-1, :]], axis=1)
            xr = mu_r * x + (1.0 - mu_r) * x_prev
            xk = mu_k * x + (1.0 - mu_k) * x_prev
            r = jax.nn.sigmoid(jnp.einsum('btc,dc->btd', xr, W_r))
            k = jnp.einsum('btc,dc->btd', xk, W_k)
            k_act = jnp.square(jax.nn.relu(k))
            out = r * jnp.einsum('btc,dc->btd', k_act, W_v)
            new_state = x[:, -1, :]
            return (out, new_state)
        return _reference_tuple_inner(x, W_r, W_k, W_v, mu_r, mu_k)[0]
    x = L0_attn_x
    x = x + _layernorm(_L0_attn_ref(_layernorm(x, axis=-1), L0_attn_ln1_w, L0_attn_ln1_b, L0_attn_wq, L0_attn_wk, L0_attn_wv, L0_attn_wo, L0_attn_bo, L0_attn_ln2_w, L0_attn_ln2_b, L0_attn_w1, L0_attn_w2), axis=-1)
    x = x + _layernorm(_L0_ffn_ref(_layernorm(x, axis=-1), L0_ffn_W_fc, L0_ffn_W_proj), axis=-1)
    x = x + _layernorm(_L1_attn_ref(_layernorm(x, axis=-1), L1_attn_Win, L1_attn_bin_, L1_attn_A_log, L1_attn_B, L1_attn_C, L1_attn_Dp, L1_attn_dt, L1_attn_Wout, L1_attn_bout), axis=-1)
    x = x + _layernorm(_L1_ffn_ref(_layernorm(x, axis=-1), L1_ffn_W_r, L1_ffn_W_k, L1_ffn_W_v, L1_ffn_mu_r, L1_ffn_mu_k), axis=-1)
    return x

_drawn_inputs = setup_inputs


def setup_inputs(seed=0):
    import zlib

    import numpy as np

    out = dict(_drawn_inputs(seed))
    spreads = {'L0_attn_ln1_w': (1.0, 0.6),
     'L0_attn_ln1_b': (0.0, 0.362),
     'L0_attn_bo': (0.0, 0.1),
     'L0_attn_ln2_w': (1.0, 0.2),
     'L0_attn_ln2_b': (0.0, 0.306),
     'L1_attn_Dp': (1.0, 0.2)}
    factors = {'L0_attn_wq': 8.0, 'L0_attn_wk': 8.0, 'L1_attn_A_log': 4.316}
    for name, (base, spread) in spreads.items():
        noise = np.random.default_rng([zlib.crc32(name.encode()), seed]).standard_normal(out[name].shape)
        drawn = base * np.exp(spread * noise) if base else spread * noise
        out[name] = jnp.asarray(drawn.astype(out[name].dtype))
    for name, factor in factors.items():
        out[name] = (out[name] * factor).astype(out[name].dtype)
    return out
```

```python
import numpy as np
import concourse.bass as bass
from concourse import mybir
from contextlib import ExitStack

FP32 = mybir.dt.float32
F32R = mybir.dt.float32r
BF16 = mybir.dt.bfloat16
ALU = mybir.AluOpType
ACT = mybir.ActivationFunctionType
AX = mybir.AxisListType

P = 128
BATCH = 8
SEQ = 512
TILES = SEQ // P
LAYERS = 6
HEADS = 8
DH = P // HEADS
FB = 4
STATES = 64
BINS = 2 * SEQ // P
GROUP = 4
PAIRS = P // 2
EPS = 1e-5
LEAK = 0.01
BETA = 0.9
STEPS = 5
ITEMS = LAYERS * BATCH


def some(value):
    return not isinstance(value, int) or value > 0


def alone(eng, passed, value):
    if not isinstance(value, int):
        eng.sem_inc(passed, 1)


SHARED = [
    [("i_st", 8), ("v1_st", 48), ("siv_st", 8), ("cxv_st", 8), ("dxv_st", 8)],
    [("v2_st", 48), ("sxv_st", 8), ("cov_st", 8), ("dov_st", 8)],
    [("i_var", 8), ("var1", 48), ("s_iv", 8), ("c_xv", 8), ("d_xv", 8)],
    [("var2", 48), ("s_xv", 8), ("c_ov", 8), ("d_ov", 8)],
    [("i_ve", 8), ("p1_ve", 48), ("si_ve", 8), ("cx_ve", 8), ("dx_ve", 8)],
    [("p2_ve", 48), ("sx_ve", 8), ("co_ve", 8), ("do_ve", 8)],
    [("i_rstd", 8), ("rstd1", 48), ("s_ir", 8), ("c_rs", 8), ("d_xs", 8)],
    [("rstd2", 48), ("s_xrs", 8), ("c_or", 8), ("d_os", 8)],
    [("si_r", 8), ("dx_r", 8)],
    [("si_mr", 8), ("dx_mr", 8)],
    [("sc_r", 8), ("co_r", 8), ("do_r", 8)],
    [("sc_mr", 8), ("co_mr", 8), ("do_mr", 8)],
    [("x2T_ps", 48), ("s_xT_ps", 8), ("c_xT_ps", 8), ("d_xT_ps", 8)],
    [("k_ps2", 48), ("c_f_ps", 8), ("d_k_ps", 8)],
    [("q_ps", 48), ("s_cnt", 8), ("d_r_ps", 8)],
    [("y_ps", 192), ("s_y_ps", 32), ("c_u_ps", 8), ("d_v_ps", 8)],
    [("h_ps", 192), ("s_h_ps", 32)],
    [("ha", 192), ("s_relu", 32), ("d_relu", 8)],
    [("q_fm", 48), ("s_sq", 32), ("d_sq", 8)],
    [("x2h", 48), ("s_hi", 8), ("c_xT", 8), ("d_xT", 8)],
]


def seq(t, b):
    return t[:, bass.ds(b * SEQ, SEQ)]


def tile(t, b, j):
    return t[:, bass.ds(b * SEQ + j * P, P)]


def per_tile(col):
    return col.unsqueeze(2).broadcast_to([P, TILES, P])


def tiles(ap):
    return ap.rearrange("p (j c) -> p j c", c=P)


def heads(ap):
    return ap.rearrange("p (a d) -> p a d", d=DH)


def pipeline(eng, lag, step):
    for n in range(lag):
        step(n, lambda k, n=n: n - k >= 0)
    with eng.Fori(lag, BATCH) as n:
        step(n, lambda k: True)
    for n in range(BATCH, BATCH + lag):
        step(n, lambda k, n=n: n - k < BATCH)


def layers(eng, step, prepare):

    def layer(first, slot, nxt):
        step(first, 0, slot, 1 - slot)
        step(first + 1, 1, slot, 1 - slot)
        if isinstance(first, int) and first == 0:
            step(2, 2, slot, slot)
        start = 3 if isinstance(first, int) and first == 0 else 2
        with eng.Fori(start, BATCH - 1) as b:
            step(first + b, b, slot, slot)
        step(first + BATCH - 1, BATCH - 1, slot, slot)
        if nxt is not None:
            prepare(*nxt)

    layer(0, 0, (1, 1, 1))
    with eng.Fori(0, (LAYERS - 2) // 2) as r:
        layer(r * (2 * BATCH) + BATCH, 1, (r * 2 + 2, 0, r + 2))
        layer(r * (2 * BATCH) + 2 * BATCH, 0, (r * 2 + 3, 1, r + 2))
    layer((LAYERS - 1) * BATCH, (LAYERS - 1) % 2, None)
    last = (LAYERS - 1) % 2
    step(ITEMS, 0, last, last)
    step(ITEMS + 1, 1, last, last)


def before(b, k):
    return (b - k) % BATCH if isinstance(b, int) else b - k


def build(nc, x, qkv, wo, w1, w2, lnc, bo, fcT, proj, winT, woutT, alog, bmat, cmat, dtr, dp, bins_,
          bouts, wrT, wkT, wvT, mu, ident, cent, hmask, iota, fwd, fwdx, inv, out):
    ctx = ExitStack()
    with ctx:
        def sb(name, shape, dt=FP32):
            return ctx.enter_context(nc.sbuf_tensor(name, [P, *shape] if len(shape) == 1 else shape, dt))

        def sem(name):
            return ctx.enter_context(nc.semaphore(name))

        X = sb("X", [BATCH * SEQ])
        XI = sb("XI", [BATCH * SEQ])
        ID = sb("ID", [P])
        CENT = sb("CENT", [P])
        HMASK = sb("HMASK", [P])
        IOTA = sb("IOTA", [P])
        EIGHTH = sb("EIGHTH", [1, P])
        MHALF = sb("MHALF", [TILES])
        IDB = sb("IDB", [P], BF16)
        QKV = [sb(f"QKV{s}", [3 * P]) for s in range(2)]
        WO = [sb(f"WO{s}", [P]) for s in range(2)]
        W1 = [sb(f"W1{s}", [FB * P]) for s in range(2)]
        W2 = [sb(f"W2{s}", [FB * P]) for s in range(2)]
        LNC = [sb(f"LNC{s}", [4]) for s in range(2)]
        BO = [sb(f"BO{s}", [1, P]) for s in range(2)]
        QKH = [sb(f"QKH{s}", [2 * P], F32R) for s in range(2)]
        QKL = [sb(f"QKL{s}", [2 * P], F32R) for s in range(2)]
        WV = [sb(f"WV{s}", [P]) for s in range(2)]
        W1H = [sb(f"W1H{s}", [FB * P], F32R) for s in range(2)]
        W1L = [sb(f"W1L{s}", [FB * P], F32R) for s in range(2)]
        BIAS = [sb(f"BIAS{s}", [2 + FB]) for s in range(2)]
        BM = [sb(f"BM{s}", [P]) for s in range(2)]
        LNP = [sb(f"LNP{i}", [P]) for i in range(2)]
        MBV = sb("MBV", [P])
        ST1, MV1, VE1, R1 = sb("ST1", [24]), sb("MV1", [8]), sb("VE1", [4]), sb("R1", [4])
        ST2, MV2, VE2, R2 = sb("ST2", [24]), sb("MV2", [8]), sb("VE2", [4]), sb("R2", [4])
        XR = sb("XR", [SEQ])
        XTF = sb("XTF", [SEQ])
        XTH, XTL = sb("XTH", [SEQ], F32R), sb("XTL", [SEQ], F32R)
        QF, QB = sb("QF", [SEQ]), sb("QB", [SEQ])
        QMX, QSM, QRC = sb("QMX", [32]), sb("QSM", [32]), sb("QRC", [32])
        QS = sb("QS", [SEQ])
        NKM, KSM, KRC = sb("NKM", [1]), sb("KSM", [1]), sb("KRC", [1])
        EK, EKT = sb("EK", [SEQ]), sb("EKT", [SEQ])
        GT, CT, MM = sb("GT", [P]), sb("CT", [P]), sb("MM", [P])
        NM1, ST3, MV3, VE3, R3, NM3 = sb("NM1", [4]), sb("ST3", [24]), sb("MV3", [8]), sb("VE3", [4]), sb("R3", [4]), sb("NM3", [4])
        XR2 = sb("XR2", [SEQ])
        X2H, X2L = sb("X2H", [SEQ], F32R), sb("X2L", [SEQ], F32R)
        HA = [sb(f"HA{i}", [SEQ]) for i in range(2)]
        HL = [sb(f"HL{i}", [SEQ]) for i in range(2)]
        FCT = sb("FCT", [FB * P])
        FCH, FCL = sb("FCH", [FB * P], F32R), sb("FCL", [FB * P], F32R)
        PROJ = sb("PROJ", [FB * P])
        SPK = [sb(f"SPK{i}", [SEQ], BF16) for i in range(STEPS)]
        YM, ACC, MEM = sb("YM", [SEQ]), sb("ACC", [SEQ]), sb("MEM", [SEQ])
        SH = sb("SH", [1 + SEQ])
        FWD = sb("FWD", [TILES * BINS * P])
        FWDX = sb("FWDX", [TILES * 2 * P])
        INV = sb("INV", [BINS * SEQ])
        BIG = sb("BIG", [PAIRS * P])
        E2 = BIG
        UALL = BIG[:, 0:BATCH * SEQ]
        YF = BIG[:, BATCH * SEQ:BATCH * SEQ + BINS * SEQ]
        ALOG, BMAT, CMAT, DTR = (sb(n, [PAIRS]) for n in ("ALOG", "BMAT", "CMAT", "DTR"))
        LA, CDB = sb("LA", [PAIRS]), sb("CDB", [PAIRS])
        E1 = sb("E1", [PAIRS * TILES])
        CE1 = sb("CE1", [PAIRS * 2 * TILES])
        DP = sb("DP", [1, P])
        KTM = sb("KTM", [TILES * P])
        KRE, KIM, KRE2 = sb("KRE", [TILES * P]), sb("KIM", [TILES * P]), sb("KRE2", [P])
        WINT, WOUTT, BIN, BOUT = (sb(n, [P]) for n in ("WINT", "WOUTT", "BIN", "BOUT"))
        WINC = sb("WINC", [P])
        WRT, WKT, WVT, MU = sb("WRT", [P]), sb("WKT", [P]), sb("WVT", [P]), sb("MU", [2])

        PS = [ctx.enter_context(nc.psum_tensor(f"PS{i}", [P, SEQ], FP32)) for i in range(8)]
        pXT, pQ, pK, pX2, pH, pY, pW = PS[0], PS[1], PS[2], PS[3], PS[4:6], PS[6], PS[7]

        signals = {name: sem(name) for name in (
            "bias_out bias_ps bm_out bm_ps c_in c_m c_o_ps c_ps c_u c_x c_xr c_yT c_y_ps c_yf c_z c_zo cdb ce1 "
            "ce1_zero ct d_diff d_mix d_out d_rv d_sig d_zn d_zo dve_passed e1 e1_arg e2 e2_arg eighth ek ekT_ps "
            "ek_tm fc_hi fc_out fc_ps g_ps gt hl k_out k_ps k_rec kf kf_ps kmax ktm la la_exp late_in lnp m_ps "
            "m_ready mbv out_ps p_const pool_passed q_blk q_exp q_nrm q_rec q_sub q_sum qmax qs resid1 resid2 "
            "s_acc s_cr s_cv s_lo s_mem s_spk s_x1 s_x2 s_xr s_y1 s_zc s_zi sc_ve scv_st sh0 sp_passed ssm_in "
            "stored w1_hi w1_out w1_ps w_ready win_out win_ps wqk_hi wqkv_out wqkv_ps x2 x2l xT_ps xTf xTl x_in "
            "xi_init xr xr2 ").split()}
        starts = {}
        for row in SHARED:
            first, total = sem(row[0][0]), 0
            for name, counts in row:
                signals[name], starts[name] = first, total
                total += counts
        s = {"w_in": [sem("w_in0"), sem("w_in1")], **signals}
        at = starts

        block = ctx.enter_context(nc.Block())

        @block.sync
        def _(sp):
            for b in range(BATCH):
                sp.dma_start(tiles(X[:, b * SEQ:(b + 1) * SEQ]),
                             x[b].rearrange("(j p) c -> p j c", p=P)).then_inc(s["x_in"], 16)

            def load(l, slot):
                sp.dma_start(QKV[slot][:, :], qkv[bass.ds(l, 1)].rearrange("a p n -> (a p) n")).then_inc(s["w_in"][slot], 16)
                sp.dma_start(LNC[slot][:, :], lnc[bass.ds(l, 1)].rearrange("a p n -> (a p) n")).then_inc(s["w_in"][slot], 16)
                sp.dma_start(W1[slot][:, :], w1[bass.ds(l, 1)].rearrange("a p n -> (a p) n")).then_inc(s["w_in"][slot], 16)
                sp.dma_start(WO[slot][:, :], wo[bass.ds(l, 1)].rearrange("a p n -> (a p) n")).then_inc(s["w_in"][slot], 16)
                sp.dma_start(tiles(W2[slot][:, :]),
                             w2[bass.ds(l, 1)].rearrange("a (f p) n -> (a p) f n", p=P)).then_inc(s["w_in"][slot], 16)
                sp.dma_start(BO[slot][:, :], bo[bass.ds(l, 1)]).then_inc(s["w_in"][slot], 16)

            sp.dma_start(CENT[:, :], cent).then_inc(s["c_in"], 16)
            sp.dma_start(ID[:, :], ident).then_inc(s["c_in"], 16)
            sp.dma_start(HMASK[:, :], hmask).then_inc(s["c_in"], 16)
            load(0, 0)
            for t, d in ((IOTA, iota), (ALOG, alog), (BMAT, bmat), (CMAT, cmat), (DTR, dtr), (DP, dp)):
                sp.dma_start(t[:, :], d).then_inc(s["ssm_in"], 16)
            sp.dma_start(FWD[:, :].rearrange("p (j f) -> p j f", j=TILES), fwd.rearrange("(j p) f -> p j f", p=P)).then_inc(s["ssm_in"], 16)
            sp.dma_start(FWDX[:, :].rearrange("p (j f) -> p j f", j=TILES), fwdx.rearrange("(j p) f -> p j f", p=P)).then_inc(s["ssm_in"], 16)
            load(1, 1)
            sp.dma_start(INV[:, :].rearrange("p (k t) -> p k t", k=BINS), inv.rearrange("(k p) t -> p k t", p=P)).then_inc(s["late_in"], 16)
            sp.dma_start(FCT[:, :], fcT).then_inc(s["late_in"], 16)
            sp.dma_start(tiles(PROJ[:, :]), proj.rearrange("(f p) n -> p f n", p=P)).then_inc(s["late_in"], 16)
            for t, d in ((WINT, winT), (WOUTT, woutT), (WRT, wrT), (WKT, wkT), (WVT, wvT), (MU, mu)):
                sp.dma_start(t[:, :], d).then_inc(s["late_in"], 16)
            sp.dma_start(BIN[:, :], bins_.broadcast_to([P, P])).then_inc(s["late_in"], 16)
            sp.dma_start(BOUT[:, :], bouts.broadcast_to([P, P])).then_inc(s["late_in"], 16)

            with sp.Fori(0, (LAYERS - 2) // 2) as r:
                sp.wait_ge(s["resid2"], r * (2 * BATCH) + BATCH)
                alone(sp, s["sp_passed"], r * (2 * BATCH) + BATCH)
                sp.wait_ge(s["w_ready"], r * 2 + 2)
                alone(sp, s["sp_passed"], r * 2 + 2)
                load(r * 2 + 2, 0)
                sp.wait_ge(s["resid2"], r * (2 * BATCH) + 2 * BATCH)
                alone(sp, s["sp_passed"], r * (2 * BATCH) + 2 * BATCH)
                sp.wait_ge(s["w_ready"], r * 2 + 3)
                alone(sp, s["sp_passed"], r * 2 + 3)
                load(r * 2 + 3, 1)

            with sp.Fori(0, BATCH) as b:
                sp.wait_ge(s["d_out"], b + 1)
                alone(sp, s["sp_passed"], b + 1)
                sp.dma_start(out[bass.ds(b, 1)].rearrange("a (j p) c -> (a p) j c", p=P), tiles(seq(X, b))).then_inc(s["stored"], 16)
            sp.wait_ge(s["stored"], 16 * BATCH)

        W_LOADS = 6 * 16
        SSM_LOADS = 8 * 16
        LATE_LOADS = 11 * 16

        @block.tensor
        def _(pe):
            def mm(o, l, r, start=True, stop=True):
                return nc.tensor.matmul(o, l, r, start=start, stop=stop, skip_group_check=True)

            def split3(o, lh, ll, rh, rl):
                mm(o, ll, rh, True, False)
                mm(o, lh, rl, False, False)
                return mm(o, lh, rh, False, True)

            def transposes(o, i):
                for j in range(TILES):
                    last = nc.tensor.transpose(o[:, j * P:(j + 1) * P], i[:, j * P:(j + 1) * P], ID[:, :])
                return last

            def prepare(l, slot, times):
                pe.wait_ge(s["w_in"][slot], times * W_LOADS)
                pe.wait_ge(s["lnp"], l + 1)
                if some(l):
                    pe.wait_ge(s["bm_out"], l)
                mm(pW[:, 0:3 * P], LNP[0][:, :], QKV[slot][:, :]).then_inc(s["wqkv_ps"], 1)
                pe.wait_ge(s["wqkv_out"], 2 * (l + 1))
                mm(pW[:, :], LNP[1][:, :], W1[slot][:, :]).then_inc(s["w1_ps"], 1)
                pe.wait_ge(s["w1_out"], l + 1)
                mm(pW[:, 0:1], QKV[slot][:, 0:P], LNC[slot][:, 1:2])
                mm(pW[:, 1:2], QKV[slot][:, 2 * P:3 * P], LNC[slot][:, 1:2])
                for f in range(FB):
                    last = mm(pW[:, 2 + f:3 + f], W1[slot][:, f * P:(f + 1) * P], LNC[slot][:, 3:4])
                last.then_inc(s["bias_ps"], 1)
                pe.wait_ge(s["mbv"], l + 1)
                mm(pW[:, 0:P], MBV[:, :], WO[slot][:, :], True, False)
                mm(pW[:, 0:P], EIGHTH[0:1, :], BO[slot][0:1, :], False, True).then_inc(s["bm_ps"], 1)
                pe.wait_ge(s["w_ready"], l + 1)

            pe.wait_ge(s["c_in"], 3 * 16)
            pe.wait_ge(s["eighth"], 1)
            prepare(0, 0, 1)

            pe.wait_ge(s["ssm_in"], SSM_LOADS)
            pe.wait_ge(s["ce1"], 1)
            for i in range(PAIRS):
                if i % 4 == 0:
                    pe.wait_ge(s["e2"], i // 4 + 1)
                last = mm(pH[0][:, i * 8:i * 8 + 8], E2[:, i * P:(i + 1) * P], CE1[:, i * 8:i * 8 + 8])
            last.then_inc(s["k_ps"], 1)
            pe.wait_ge(s["ktm"], 1)
            for half, bank in ((0, pH[1]), (1, pY)):
                for k in range(TILES):
                    for j in range(TILES):
                        lhs = FWD[:, j * BINS * P + half * SEQ + k * P:][:, 0:P]
                        if half == 1 and k == 0:
                            lhs = FWDX[:, j * 2 * P:j * 2 * P + P]
                        last = mm(bank[:, k * P:(k + 1) * P], lhs, KTM[:, j * P:(j + 1) * P], j == 0, j == TILES - 1)
                last.then_inc(s["kf_ps"], 1)
            for j in range(TILES):
                last = mm(pX2[:, 0:P], FWDX[:, j * 2 * P + P:(j + 1) * 2 * P], KTM[:, j * P:(j + 1) * P], j == 0, j == TILES - 1)
            last.then_inc(s["kf_ps"], 1)
            pe.wait_ge(s["kf"], 3)

            def step(n, b, front, back):
                static = isinstance(n, int)
                has_n = not static or n < ITEMS
                has_o = not static or 1 <= n <= ITEMS
                m = n - 2
                has_m = not static or 2 <= n
                wa, wf = front, back
                k0 = m * FB

                def h(f):
                    if not has_m:
                        return
                    if some(k0 + f - 1):
                        pe.wait_ge(s["ha"], k0 + f - 1)
                    o = slice(f * P, (f + 1) * P)
                    split3(pH[f % 2][:, :], W1H[wf][:, o], W1L[wf][:, o], X2H[:, :], X2L[:, :]).then_inc(s["h_ps"], 1)

                def y(f):
                    if not has_m:
                        return
                    pe.wait_ge(s["hl"], k0 + f + 1)
                    if f == 0:
                        if some(m):
                            pe.wait_ge(s["resid2"], m)
                    for j in range(TILES):
                        last = mm(pY[:, j * P:(j + 1) * P], HL[f % 2][:, j * P:(j + 1) * P],
                                  W2[wf][:, f * P:(f + 1) * P], f == 0 and j == 0, f == FB - 1)
                    last.then_inc(s["y_ps"], 1)

                if has_m:
                    pe.wait_ge(s["xr2"], m + 1)
                    transposes(pX2, XR2).then_inc(s["x2T_ps"], 1)
                if has_o:
                    if some(n):
                        pe.wait_ge(s["m_ready"], n)
                    if some(n):
                        pe.wait_ge(s["qs"], n)
                    for j in range(TILES):
                        last = mm(pQ[:, j * P:(j + 1) * P], QS[:, j * P:(j + 1) * P], MM[:, :])
                    last.then_inc(s["out_ps"], 1)
                if has_n:
                    pe.wait_ge(s["xr"], n + 1)
                    if some(n):
                        pe.wait_ge(s["ek_tm"], n)
                    transposes(pXT, XR).then_inc(s["xT_ps"], 1)
                if has_m:
                    pe.wait_ge(s["x2l"], m + 1)
                h(0)
                h(1)
                h(2)
                if has_n:
                    pe.wait_ge(s["xTl"], n + 1)
                    split3(pK[:, :], QKH[wa][:, P:2 * P], QKL[wa][:, P:2 * P], XTH[:, :], XTL[:, :]).then_inc(s["k_ps2"], 1)
                    if some(n):
                        pe.wait_ge(s["resid1"], n)
                    split3(pQ[:, :], QKH[wa][:, 0:P], QKL[wa][:, 0:P], XTH[:, :], XTL[:, :]).then_inc(s["q_ps"], 1)
                y(0)
                h(3)
                y(1)
                if has_n:
                    pe.wait_ge(s["ek"], n + 1)
                    transposes(pXT, EK).then_inc(s["ekT_ps"], 1)
                y(2)
                if has_n:
                    pe.wait_ge(s["ek_tm"], n + 1)
                    for j in range(TILES):
                        last = mm(pK[:, 0:P], XR[:, j * P:(j + 1) * P], EKT[:, j * P:(j + 1) * P], j == 0, j == TILES - 1)
                    last.then_inc(s["g_ps"], 1)
                y(3)
                if has_n:
                    pe.wait_ge(s["gt"], n + 1)
                    mm(pK[:, P:2 * P], WV[wa][:, :], GT[:, :]).then_inc(s["c_ps"], 1)
                    pe.wait_ge(s["ct"], n + 1)
                    mm(pK[:, 2 * P:3 * P], CT[:, :], WO[wa][:, :]).then_inc(s["m_ps"], 1)

            pe.wait_ge(s["w_ready"], 1)
            layers(pe, step, prepare)

            pe.wait_ge(s["late_in"], LATE_LOADS)
            pe.wait_ge(s["x2"], 1)
            mm(pW[:, :], CENT[:, :], FCT[:, :]).then_inc(s["fc_ps"], 1)
            pe.wait_ge(s["fc_out"], 1)
            mm(pW[:, 0:P], CENT[:, :], WINT[:, :]).then_inc(s["win_ps"], 1)
            pe.wait_ge(s["win_out"], 1)

            def spiking(n, live):
                if live(2):
                    i = n - 2
                    pe.wait_ge(s["s_xr"], i + 1)
                    if some(i):
                        pe.wait_ge(s["s_lo"], i)
                    transposes(pX2, XR2).then_inc(s["s_xT_ps"], 1)
                    pe.wait_ge(s["s_lo"], i + 1)
                    for f in range(FB):
                        o = slice(f * P, (f + 1) * P)
                        k = i * FB + f
                        if some(k - 1):
                            pe.wait_ge(s["s_relu"], at["s_relu"] + k - 1)
                        split3(pH[f % 2][:, :], FCH[:, o], FCL[:, o], X2H[:, :], X2L[:, :]).then_inc(s["s_h_ps"], 1)
                        if f >= 1:
                            proj_block(i, f - 1)
                    proj_block(i, FB - 1)
                if live(3):
                    i = n - 3
                    if some(i):
                        pe.wait_ge(s["s_zc"], i)
                    for t in range(STEPS):
                        pe.wait_ge(s["s_spk"], i * STEPS + t + 1)
                        last = mm(pQ[:, :], IDB[:, :], SPK[t][:, :], t == 0, t == STEPS - 1)
                    last.then_inc(s["s_cnt"], 1)

            def proj_block(i, f):
                pe.wait_ge(s["s_sq"], at["s_sq"] + i * FB + f + 1)
                if f == 0:
                    if some(i):
                        pe.wait_ge(s["s_y1"], i)
                for j in range(TILES):
                    last = mm(pY[:, j * P:(j + 1) * P], HL[f % 2][:, j * P:(j + 1) * P],
                              PROJ[:, f * P:(f + 1) * P], f == 0 and j == 0, f == FB - 1)
                last.then_inc(s["s_y_ps"], 1)

            pipeline(pe, 5, spiking)

            def ssm_in(n, live):
                if live(1):
                    i = n - 1
                    pe.wait_ge(s["c_xr"], i + 1)
                    if some(i):
                        pe.wait_ge(s["c_xT"], at["c_xT"] + i)
                    transposes(pX2, XR2).then_inc(s["c_xT_ps"], 1)
                    pe.wait_ge(s["c_xT"], at["c_xT"] + i + 1)
                    if some(i):
                        pe.wait_ge(s["c_u"], i)
                    for j in range(TILES):
                        last = mm(pY[:, j * P:(j + 1) * P], XTF[:, j * P:(j + 1) * P], WINC[:, :])
                    last.then_inc(s["c_u_ps"], 1)

            pipeline(pe, 2, ssm_in)

            def out_proj(g, i):
                item = g * GROUP + i
                pe.wait_ge(s["c_yT"], item + 1)
                if some(item):
                    pe.wait_ge(s["c_z"], item)
                for j in range(TILES):
                    last = mm(pXT[:, j * P:(j + 1) * P], XTF[:, j * P:(j + 1) * P], WOUTT[:, :])
                last.then_inc(s["c_o_ps"], 1)

            with pe.Fori(0, BATCH // GROUP) as g:
                pe.wait_ge(s["c_u"], BATCH)
                u4 = UALL[:, bass.ds(g * (GROUP * SEQ), GROUP * SEQ)].rearrange("p (b j d) -> p j b d", b=GROUP, j=TILES)
                for k in range(TILES):
                    for half in range(2):
                        bank = PS[4 + (k % 2) * 2 + half]
                        if k >= 2:
                            if some(g * TILES + k - 1):
                                pe.wait_ge(s["c_yf"], g * TILES + k - 1)
                        for j in range(TILES):
                            lhs = FWD[:, j * BINS * P + half * SEQ + k * P:][:, 0:P]
                            last = mm(bank[:, :].rearrange("p (b d) -> p b d", b=GROUP), lhs, u4[:, j], j == 0, j == TILES - 1)
                    last.then_inc(s["c_f_ps"], 1)
                pe.wait_ge(s["c_yf"], (g + 1) * TILES)
                for i in range(GROUP):
                    if i >= 2:
                        if some(g * GROUP + i - 1):
                            pe.wait_ge(s["c_yT"], g * GROUP + i - 1)
                    bank = PS[2 + i % 2]
                    for k in range(BINS):
                        last = mm(bank[:, :], YF[:, k * SEQ + i * P:k * SEQ + (i + 1) * P],
                                  INV[:, k * SEQ:(k + 1) * SEQ], k == 0, k == BINS - 1)
                    last.then_inc(s["c_y_ps"], 1)
                    if i >= 1:
                        out_proj(g, i - 1)
                out_proj(g, GROUP - 1)

            def mix(n, live):
                if live(1):
                    i = n - 1
                    pe.wait_ge(s["d_zn"], i + 1)
                    if some(i):
                        pe.wait_ge(s["d_xT"], at["d_xT"] + i)
                    transposes(pX2, XR2).then_inc(s["d_xT_ps"], 1)
                if live(2):
                    i = n - 2
                    pe.wait_ge(s["d_mix"], i + 1)
                    if some(i):
                        pe.wait_ge(s["d_relu"], at["d_relu"] + i)
                    mm(pK[:, :], WKT[:, :], HA[1][:, :]).then_inc(s["d_k_ps"], 1)
                    if some(i):
                        pe.wait_ge(s["d_sig"], i)
                    for j in range(TILES):
                        last = mm(pQ[:, j * P:(j + 1) * P], HA[0][:, j * P:(j + 1) * P], WRT[:, :])
                    last.then_inc(s["d_r_ps"], 1)
                    pe.wait_ge(s["d_sq"], at["d_sq"] + i + 1)
                    if some(i):
                        pe.wait_ge(s["d_rv"], i)
                    for j in range(TILES):
                        last = mm(pY[:, j * P:(j + 1) * P], HL[0][:, j * P:(j + 1) * P], WVT[:, :])
                    last.then_inc(s["d_v_ps"], 1)

            pipeline(pe, 3, mix)

        @block.gpsimd
        def _(pool):
            pool.memset(MHALF[:, :], -0.5).then_inc(s["p_const"], 1)
            pool.memset(CE1[:, :], 0.0).then_inc(s["ce1_zero"], 1)
            pool.wait_ge(s["p_const"], 1)
            own = [0]

            def rstd(mv, ve, r, eps, summed, count):
                pool.tensor_scalar(ve[:, :], mv[:, :].rearrange("p (j t) -> p j t", t=2)[:, :, 1], eps, 1.0,
                                   ALU.add, ALU.mult).then_inc(summed, 1)
                pool.wait_ge(summed, count)
                return pool.tensor_tensor(r[:, :], ve[:, :], MHALF[:, :], ALU.pow)

            def mean_rstd(mv, r, nm, powered, r_count, scaled, count):
                pool.wait_ge(powered, r_count)
                pool.tensor_tensor(nm[:, :], mv[:, :].rearrange("p (j t) -> p j t", t=2)[:, :, 0], r[:, :],
                                   ALU.mult).then_inc(scaled, 1)
                pool.wait_ge(scaled, count)
                alone(pool, s["pool_passed"], count)
                return pool.tensor_scalar(nm[:, :], nm[:, :], -1.0, 0.0, ALU.mult, ALU.add)

            with pool.Fori(0, BATCH) as b:
                pool.wait_ge(s["i_var"], b + 1)
                alone(pool, s["pool_passed"], b + 1)
                rstd(MV1, VE1, R1, EPS, s["i_ve"], b + 1).then_inc(s["i_rstd"], 1)

            pool.wait_ge(s["var1"], at["var1"] + 1)
            alone(pool, s["pool_passed"], 1)
            rstd(MV1, VE1, R1, EPS, s["p1_ve"], at["p1_ve"] + 1).then_inc(s["rstd1"], 1)

            def step(n, b, front, back):
                static = isinstance(n, int)
                if not static or n < ITEMS:
                    pool.wait_ge(s["xTf"], n + 1)
                    pool.tensor_tensor(XTL[:, :], XTF[:, :], XTH[:, :].bitcast(FP32), ALU.subtract).then_inc(s["xTl"], 1)
                if not static or 1 <= n <= ITEMS:
                    if some(n):
                        pool.wait_ge(s["var2"], n)
                        alone(pool, s["pool_passed"], n)
                    rstd(MV2, VE2, R2, EPS, s["p2_ve"], n).then_inc(s["rstd2"], 1)
                if not static or n < ITEMS:
                    pool.wait_ge(s["qmax"], n + 1)
                    pool.tensor_tensor(heads(QB[:, :]), heads(QB[:, :]), QMX[:, :].unsqueeze(2).broadcast_to([P, 32, DH]),
                                       ALU.subtract).then_inc(s["q_sub"], 1)
                if not static or n < ITEMS - 1:
                    pool.wait_ge(s["var1"], at["var1"] + n + 2)
                    alone(pool, s["pool_passed"], n + 2)
                    rstd(MV1, VE1, R1, EPS, s["p1_ve"], at["p1_ve"] + n + 2).then_inc(s["rstd1"], 1)
                if not static or n < ITEMS:
                    pool.wait_ge(s["q_rec"], n + 1)
                    pool.tensor_tensor(heads(QB[:, :]), heads(QB[:, :]), QRC[:, :].unsqueeze(2).broadcast_to([P, 32, DH]),
                                       ALU.mult).then_inc(s["q_nrm"], 1)

            layers(pool, step, lambda l, slot, times: None)

            def spiking(n, live):
                if live(0):
                    pool.wait_ge(s["s_iv"], at["s_iv"] + n + 1)
                    if some(n):
                        pool.wait_ge(s["s_zi"], n)
                        alone(pool, s["pool_passed"], n)
                    rstd(MV1, VE1, R1, EPS, s["si_ve"], at["si_ve"] + n + 1).then_inc(s["si_r"], 1)
                    mean_rstd(MV1, R1, NM1, s["si_r"], n + 1, s["si_mr"], n + 1).then_inc(s["s_ir"], 1)
                if live(1):
                    i = n - 1
                    pool.wait_ge(s["s_xv"], at["s_xv"] + i + 1)
                    if some(i):
                        pool.wait_ge(s["s_xr"], i)
                        alone(pool, s["pool_passed"], i)
                    rstd(MV2, VE2, R2, EPS, s["sx_ve"], at["sx_ve"] + i + 1).then_inc(s["s_xrs"], 1)
                if live(4):
                    i = n - 4
                    pool.wait_ge(s["s_cv"], i + 1)
                    if some(i):
                        pool.wait_ge(s["s_zc"], i)
                        alone(pool, s["pool_passed"], i)
                    rstd(MV3, VE3, R3, EPS * STEPS * STEPS, s["sc_ve"], i + 1).then_inc(s["sc_r"], 1)
                    mean_rstd(MV3, R3, NM3, s["sc_r"], i + 1, s["sc_mr"], i + 1).then_inc(s["s_cr"], 1)

            pipeline(pool, 5, spiking)

            def ssm_in(n, live):
                if live(0):
                    pool.wait_ge(s["c_xv"], at["c_xv"] + n + 1)
                    if some(n):
                        pool.wait_ge(s["c_xr"], n)
                        alone(pool, s["pool_passed"], n)
                    rstd(MV2, VE2, R2, EPS, s["cx_ve"], at["cx_ve"] + n + 1).then_inc(s["c_rs"], 1)

            pipeline(pool, 2, ssm_in)
            with pool.Fori(0, BATCH) as i:
                pool.wait_ge(s["c_ov"], at["c_ov"] + i + 1)
                alone(pool, s["pool_passed"], i + 1)
                rstd(MV3, VE3, R3, EPS, s["co_ve"], at["co_ve"] + i + 1).then_inc(s["co_r"], 1)
                mean_rstd(MV3, R3, NM3, s["co_r"], at["co_r"] + i + 1, s["co_mr"], at["co_mr"] + i + 1).then_inc(s["c_or"], 1)

            def mix(n, live):
                if live(0):
                    pool.wait_ge(s["d_xv"], at["d_xv"] + n + 1)
                    if some(n):
                        pool.wait_ge(s["d_zn"], n)
                        alone(pool, s["pool_passed"], n)
                    rstd(MV1, VE1, R1, EPS, s["dx_ve"], at["dx_ve"] + n + 1).then_inc(s["dx_r"], 1)
                    mean_rstd(MV1, R1, NM1, s["dx_r"], at["dx_r"] + n + 1, s["dx_mr"], at["dx_mr"] + n + 1).then_inc(s["d_xs"], 1)
                if live(3):
                    i = n - 3
                    pool.wait_ge(s["d_ov"], at["d_ov"] + i + 1)
                    if some(i):
                        pool.wait_ge(s["d_zo"], i)
                        alone(pool, s["pool_passed"], i)
                    rstd(MV3, VE3, R3, EPS, s["do_ve"], at["do_ve"] + i + 1).then_inc(s["do_r"], 1)
                    mean_rstd(MV3, R3, NM3, s["do_r"], at["do_r"] + i + 1, s["do_mr"], at["do_mr"] + i + 1).then_inc(s["d_os"], 1)

            pipeline(pool, 3, mix)

        @block.scalar
        def _(act):
            def copy(o, i):
                return nc.scalar.activation(o, i, ACT.Copy)

            def normalise(o, i, r, nm):
                for j in range(TILES):
                    cols = slice(j * P, (j + 1) * P)
                    last = nc.scalar.activation(o[:, cols], i[:, cols] if not callable(i) else i(j), ACT.Identity,
                                                bias=nm[:, j:j + 1], scale=r[:, j:j + 1])
                return last

            def prepare(l, slot, times):
                act.wait_ge(s["wqkv_ps"], l + 1)
                copy(QKH[slot][:, :], pW[:, 0:2 * P]).then_inc(s["wqk_hi"], 1)
                copy(WV[slot][:, :], pW[:, 2 * P:3 * P]).then_inc(s["wqkv_out"], 1)
                act.wait_ge(s["w1_ps"], l + 1)
                copy(W1H[slot][:, :], pW[:, :]).then_inc(s["w1_hi"], 1)
                act.wait_ge(s["bias_ps"], l + 1)
                copy(BIAS[slot][:, :], pW[:, 0:2 + FB]).then_inc(s["bias_out"], 1)
                act.wait_ge(s["bm_ps"], l + 1)
                copy(BM[slot][:, :], pW[:, 0:P]).then_inc(s["bm_out"], 1)

            act.wait_ge(s["ssm_in"], SSM_LOADS)
            nc.scalar.activation(LA[:, :], ALOG[:, :], ACT.Exp, scale=-1.0).then_inc(s["la_exp"], 1)
            prepare(0, 0, 1)
            act.wait_ge(s["e1_arg"], 1)
            nc.scalar.activation(E1[:, :], E1[:, :], ACT.Exp).then_inc(s["e1"], 1)
            for p4 in range(PAIRS // 4):
                act.wait_ge(s["e2_arg"], p4 + 1)
                nc.scalar.activation(E2[:, p4 * 512:(p4 + 1) * 512], E2[:, p4 * 512:(p4 + 1) * 512], ACT.Exp).then_inc(s["e2"], 1)
            act.wait_ge(s["k_ps"], 1)
            for h in range(2):
                last = copy(KTM[:, :].rearrange("p (q h i) -> p h i q", q=TILES, h=2)[:, h],
                            pH[0][:, :].rearrange("p (i h q) -> p h i q", h=2, q=TILES)[:, h])
            last.then_inc(s["k_out"], 1)
            for part, (o, i) in enumerate(((KRE[:, :], pH[1][:, :]), (KIM[:, :], pY[:, :]), (KRE2[:, :], pX2[:, 0:P]))):
                act.wait_ge(s["kf_ps"], part + 1)
                copy(o, i).then_inc(s["kf"], 1)

            def step(n, b, front, back):
                static = isinstance(n, int)
                has_n = not static or n < ITEMS
                m = n - 2
                has_m = not static or 2 <= n
                wa, wf = front, back
                k0 = m * FB

                def ha(f):
                    if not has_m:
                        return
                    act.wait_ge(s["h_ps"], k0 + f + 1)
                    if some(k0 + f - 1):
                        act.wait_ge(s["hl"], k0 + f - 1)
                    nc.scalar.activation(HA[f % 2][:, :], pH[f % 2][:, :], ACT.Identity,
                                         bias=BIAS[wf][:, 2 + f:3 + f]).then_inc(s["ha"], 1)

                if has_m:
                    act.wait_ge(s["x2T_ps"], m + 1)
                    copy(X2H[:, :], pX2[:, :]).then_inc(s["x2h"], 1)
                if has_n:
                    act.wait_ge(s["xT_ps"], n + 1)
                    copy(XTH[:, :], pXT[:, :])
                    copy(XTF[:, :], pXT[:, :]).then_inc(s["xTf"], 1)
                ha(0)
                ha(1)
                ha(2)
                if has_n:
                    act.wait_ge(s["q_ps"], n + 1)
                    nc.scalar.activation(QF[:, :], pQ[:, :], ACT.Identity, bias=BIAS[wa][:, 0:1]).then_inc(s["q_fm"], 1)
                    act.wait_ge(s["kmax"], n + 1)
                    nc.scalar.activation(EK[:, :], pK[:, :], ACT.Exp, bias=NKM[:, 0:1], accum_out=KSM[:, 0:1]).then_inc(s["ek"], 1)
                ha(3)
                if has_n:
                    act.wait_ge(s["ekT_ps"], n + 1)
                    copy(EKT[:, :], pXT[:, :]).then_inc(s["ek_tm"], 1)
                    act.wait_ge(s["q_sub"], n + 1)
                    nc.scalar.activation(QB[:, :], QB[:, :], ACT.Exp).then_inc(s["q_exp"], 1)
                    act.wait_ge(s["g_ps"], n + 1)
                    copy(GT[:, :], pK[:, 0:P]).then_inc(s["gt"], 1)

            layers(act, step, prepare)

            act.wait_ge(s["fc_ps"], 1)
            copy(FCH[:, :], pW[:, :]).then_inc(s["fc_hi"], 1)
            act.wait_ge(s["win_ps"], 1)
            copy(WINC[:, :], pW[:, 0:P]).then_inc(s["win_out"], 1)

            def spiking(n, live):
                if live(2):
                    i = n - 2
                    act.wait_ge(s["s_xT_ps"], at["s_xT_ps"] + i + 1)
                    copy(X2H[:, :], pX2[:, :]).then_inc(s["s_hi"], 1)
                if live(0):
                    act.wait_ge(s["s_ir"], at["s_ir"] + n + 1)
                    if some(n):
                        act.wait_ge(s["s_x1"], n)
                    normalise(XR[:, :], lambda j: tile(XI, n, j), R1, NM1).then_inc(s["s_zi"], 1)
                if live(2):
                    for f in range(FB):
                        k = i * FB + f
                        act.wait_ge(s["s_h_ps"], at["s_h_ps"] + k + 1)
                        nc.scalar.activation(HA[f % 2][:, :], pH[f % 2][:, :], ACT.Relu).then_inc(s["s_relu"], 1)
                        act.wait_ge(s["s_relu"], at["s_relu"] + k + 1)
                        if some(k - 1):
                            act.wait_ge(s["s_y_ps"], at["s_y_ps"] + k - 1)
                        nc.scalar.activation(HL[f % 2][:, :], HA[f % 2][:, :], ACT.Square).then_inc(s["s_sq"], 1)
                if live(4):
                    i = n - 4
                    act.wait_ge(s["s_cr"], i + 1)
                    if some(i):
                        act.wait_ge(s["s_x2"], i)
                    normalise(EK[:, :], pQ[:, :], R3, NM3).then_inc(s["s_zc"], 1)

            pipeline(act, 5, spiking)

            def ssm_in(n, live):
                if live(1):
                    i = n - 1
                    act.wait_ge(s["c_xT_ps"], at["c_xT_ps"] + i + 1)
                    if some(i):
                        act.wait_ge(s["c_u_ps"], at["c_u_ps"] + i)
                    copy(XTF[:, :], pX2[:, :]).then_inc(s["c_xT"], 1)

            pipeline(act, 2, ssm_in)

            def ssm_norm(item):
                act.wait_ge(s["c_or"], at["c_or"] + item + 1)
                if some(item):
                    act.wait_ge(s["c_x"], item)
                normalise(EK[:, :], EKT[:, :], R3, NM3).then_inc(s["c_zo"], 1)

            with act.Fori(0, BATCH // GROUP) as g:
                for i in range(GROUP):
                    item = g * GROUP + i
                    act.wait_ge(s["c_y_ps"], item + 1)
                    if some(item):
                        act.wait_ge(s["c_o_ps"], item)
                    copy(XTF[:, :], PS[2 + i % 2][:, :]).then_inc(s["c_yT"], 1)
                    if i >= 1:
                        ssm_norm(item - 1)
                ssm_norm(g * GROUP + GROUP - 1)

            def mix(n, live):
                if live(0):
                    act.wait_ge(s["d_xs"], at["d_xs"] + n + 1)
                    if some(n):
                        act.wait_ge(s["d_xT_ps"], at["d_xT_ps"] + n)
                    normalise(XR2[:, :], lambda j: tile(X, n, j), R1, NM1).then_inc(s["d_zn"], 1)
                if live(1):
                    i = n - 1
                    act.wait_ge(s["d_xT_ps"], at["d_xT_ps"] + i + 1)
                    if some(i):
                        act.wait_ge(s["d_mix"], i)
                    copy(SH[:, 1:1 + SEQ], pX2[:, :]).then_inc(s["d_xT"], 1)
                if live(2):
                    i = n - 2
                    act.wait_ge(s["d_k_ps"], at["d_k_ps"] + i + 1)
                    nc.scalar.activation(QF[:, :], pK[:, :], ACT.Relu).then_inc(s["d_relu"], 1)
                    act.wait_ge(s["d_relu"], at["d_relu"] + i + 1)
                    if some(i):
                        act.wait_ge(s["d_v_ps"], at["d_v_ps"] + i)
                    nc.scalar.activation(HL[0][:, :], QF[:, :], ACT.Square).then_inc(s["d_sq"], 1)
                    act.wait_ge(s["d_r_ps"], at["d_r_ps"] + i + 1)
                    if some(i):
                        act.wait_ge(s["d_rv"], i)
                    nc.scalar.activation(QB[:, :], pQ[:, :], ACT.Sigmoid).then_inc(s["d_sig"], 1)
                if live(3):
                    i = n - 3
                    act.wait_ge(s["d_os"], at["d_os"] + i + 1)
                    if some(i):
                        act.wait_ge(s["d_out"], i)
                    normalise(EKT[:, :], EK[:, :], R3, NM3).then_inc(s["d_zo"], 1)

            pipeline(act, 3, mix)

        @block.vector
        def _(dve):
            tt, ts, stt = nc.vector.tensor_tensor, nc.vector.tensor_scalar, nc.vector.scalar_tensor_tensor

            def stats(src, st, mv, parted, count):
                for j in range(TILES):
                    last = nc.vector.bn_stats(st[:, j * 6:(j + 1) * 6], src(j))
                last.then_inc(parted, 1)
                dve.wait_ge(parted, count)
                alone(dve, s["dve_passed"], count)
                for j in range(TILES):
                    last = nc.vector.bn_aggr(mv[:, 2 * j:2 * j + 2], st[:, j * 6:(j + 1) * 6])
                return last

            nc.vector.memset(EIGHTH[0:1, :], 1.0 / HEADS).then_inc(s["eighth"], 1)

            def prepare(l, slot, times):
                dve.wait_ge(s["w_in"][slot], times * W_LOADS)
                ts(LNP[0][:, :], CENT[:, :], LNC[slot][:, 0:1], None, ALU.mult)
                ts(LNP[1][:, :], CENT[:, :], LNC[slot][:, 2:3], None, ALU.mult).then_inc(s["lnp"], 1)
                dve.wait_ge(s["wqk_hi"], l + 1)
                dve.wait_ge(s["wqkv_out"], 2 * l + 1)
                tt(QKL[slot][:, :], pW[:, 0:2 * P], QKH[slot][:, :].bitcast(FP32), ALU.subtract).then_inc(s["wqkv_out"], 1)
                dve.wait_ge(s["w1_hi"], l + 1)
                tt(W1L[slot][:, :], pW[:, :], W1H[slot][:, :].bitcast(FP32), ALU.subtract).then_inc(s["w1_out"], 1)
                dve.wait_ge(s["bias_out"], l + 1)
                ts(MBV[:, :], HMASK[:, :], BIAS[slot][:, 1:2], None, ALU.mult).then_inc(s["mbv"], 1)
                dve.wait_ge(s["bm_out"], l + 1)
                dve.sem_inc(s["w_ready"], 1)

            dve.wait_ge(s["c_in"], 3 * 16)
            nc.vector.tensor_copy(IDB[:, :], ID[:, :])
            prepare(0, 0, 1)

            dve.wait_ge(s["ssm_in"], SSM_LOADS)
            dve.wait_ge(s["la_exp"], 1)
            tt(CDB[:, :], BMAT[:, :], DTR[:, :], ALU.mult).then_inc(s["cdb"], 1)
            stt(out=LA[:, :], in0=LA[:, :], scalar=-1.0, in1=DTR[:, :], op0=ALU.mult, op1=ALU.mult).then_inc(s["la"], 1)
            dve.wait_ge(s["cdb"], 1)
            dve.wait_ge(s["la"], 1)
            tt(CDB[:, :], CMAT[:, :], CDB[:, :], ALU.mult).then_inc(s["cdb"], 1)
            for q in range(TILES):
                last = ts(E1[:, :].rearrange("p (i q) -> p i q", q=TILES)[:, :, q], LA[:, :], float(q * P), None, ALU.mult)
            last.then_inc(s["e1_arg"], 1)
            for p4 in range(PAIRS // 4):
                tt(E2[:, p4 * 512:(p4 + 1) * 512].rearrange("p (i r) -> p i r", i=4),
                   LA[:, 4 * p4:4 * p4 + 4].unsqueeze(2).broadcast_to([P, 4, P]),
                   IOTA[:, :].unsqueeze(1).broadcast_to([P, 4, P]), ALU.mult).then_inc(s["e2_arg"], 1)
                if p4 == 0:
                    dve.wait_ge(s["e1"], 1)
                    dve.wait_ge(s["cdb"], 2)
                    dve.wait_ge(s["ce1_zero"], 1)
                    for h in range(2):
                        o = slice(h * STATES, (h + 1) * STATES)
                        last = tt(CE1[o, :].rearrange("p (i h q) -> p h i q", h=2, q=TILES)[:, h],
                                  E1[o, :].rearrange("p (i q) -> p i q", q=TILES),
                                  CDB[o, :].unsqueeze(2).broadcast_to([STATES, PAIRS, TILES]), ALU.mult)
                    last.then_inc(s["ce1"], 1)
            dve.wait_ge(s["k_out"], 1)
            tt(KTM[0:1, 0:P], KTM[0:1, 0:P], DP[0:1, :], ALU.add).then_inc(s["ktm"], 1)

            dve.wait_ge(s["x_in"], 16 * BATCH)
            with dve.Fori(0, BATCH) as b:
                stats(lambda j: tile(X, b, j), ST1, MV1, s["i_st"], b + 1).then_inc(s["i_var"], 1)
                dve.wait_ge(s["i_rstd"], b + 1)
                dve.wait_ge(s["i_var"], b + 1)
                for j in range(TILES):
                    last = ts(tile(XI, b, j), tile(X, b, j), MV1[:, 2 * j:2 * j + 1], R1[:, j:j + 1], ALU.subtract, ALU.mult)
                last.then_inc(s["xi_init"], 1)
            dve.wait_ge(s["xi_init"], BATCH)

            def ln1(n, b):
                stats(lambda j: tile(XI, b, j), ST1, MV1, s["v1_st"], at["v1_st"] + n + 1).then_inc(s["var1"], 1)

            def ln1_scale(n, b):
                dve.wait_ge(s["rstd1"], at["rstd1"] + n + 1)
                if some(n):
                    dve.wait_ge(s["g_ps"], n)
                tt(tiles(XR[:, :]), tiles(seq(XI, b)), per_tile(R1[:, :]), ALU.mult).then_inc(s["xr"], 1)

            ln1(0, 0)
            ln1_scale(0, 0)

            def step(n, b, front, back):
                static = isinstance(n, int)
                has_n = not static or n < ITEMS
                has_o = not static or 1 <= n <= ITEMS
                m = n - 2
                has_m = not static or 2 <= n
                wa = front
                k0 = m * FB

                def hl(f):
                    if not has_m:
                        return
                    dve.wait_ge(s["ha"], k0 + f + 1)
                    if some(k0 + f - 1):
                        dve.wait_ge(s["y_ps"], k0 + f - 1)
                    stt(out=HL[f % 2][:, :], in0=HA[f % 2][:, :], scalar=LEAK, in1=HA[f % 2][:, :],
                        op0=ALU.mult, op1=ALU.max).then_inc(s["hl"], 1)

                if has_m:
                    dve.wait_ge(s["x2h"], m + 1)
                    tt(X2L[:, :], pX2[:, :], X2H[:, :].bitcast(FP32), ALU.subtract).then_inc(s["x2l"], 1)
                if has_o:
                    if some(n):
                        dve.wait_ge(s["out_ps"], n)
                    xo = seq(XI, before(b, 1))
                    tt(xo, pQ[:, :], xo, ALU.add).then_inc(s["resid1"], 1)
                    if some(n):
                        dve.wait_ge(s["resid1"], n)
                        alone(dve, s["dve_passed"], n)
                    stats(lambda j: tile(XI, before(b, 1), j), ST2, MV2, s["v2_st"], n).then_inc(s["var2"], 1)
                hl(0)
                hl(1)
                if has_o:
                    if some(n):
                        dve.wait_ge(s["rstd2"], n)
                    tt(tiles(XR2[:, :]), tiles(seq(XI, before(b, 1))), per_tile(R2[:, :]), ALU.mult).then_inc(s["xr2"], 1)
                if has_n:
                    dve.wait_ge(s["k_ps2"], n + 1)
                    nc.vector.tensor_reduce(NKM[:, 0:1], pK[:, :], AX.X, ALU.max, negate=True).then_inc(s["kmax"], 1)
                hl(2)
                if has_n:
                    dve.wait_ge(s["q_fm"], n + 1)
                    nc.vector.transpose(QB[:, :], QF[:, :]).then_inc(s["q_blk"], 1)
                    dve.wait_ge(s["q_blk"], n + 1)
                    nc.vector.tensor_reduce(QMX[:, :], heads(QB[:, :]), AX.X, ALU.max).then_inc(s["qmax"], 1)
                hl(3)
                more = not static or n < ITEMS - 1
                if more:
                    ln1(n + 1, before(b, -1))
                if has_n:
                    dve.wait_ge(s["q_exp"], n + 1)
                    nc.vector.tensor_reduce(QSM[:, :], heads(QB[:, :]), AX.X, ALU.add).then_inc(s["q_sum"], 1)
                    dve.wait_ge(s["q_sum"], n + 1)
                    nc.vector.reciprocal(QRC[:, :], QSM[:, :]).then_inc(s["q_rec"], 1)
                    nc.vector.reciprocal(KRC[:, :], KSM[:, :]).then_inc(s["k_rec"], 1)
                if more:
                    ln1_scale(n + 1, before(b, -1))
                if has_n:
                    dve.wait_ge(s["c_ps"], n + 1)
                    tt(CT[:, :], pK[:, P:2 * P], HMASK[:, :], ALU.mult).then_inc(s["ct"], 1)
                    dve.wait_ge(s["m_ps"], n + 1)
                    dve.wait_ge(s["k_rec"], n + 1)
                    stt(out=MM[:, :], in0=pK[:, 2 * P:3 * P], scalar=KRC[:, 0:1], in1=BM[wa][:, :],
                        op0=ALU.mult, op1=ALU.add).then_inc(s["m_ready"], 1)
                if has_m:
                    dve.wait_ge(s["y_ps"], k0 + FB)
                    xo = seq(XI, before(b, 2))
                    tt(xo, pY[:, :], xo, ALU.add).then_inc(s["resid2"], 1)
                if has_n:
                    dve.wait_ge(s["q_nrm"], n + 1)
                    nc.vector.transpose(QS[:, :], QB[:, :]).then_inc(s["qs"], 1)

            layers(dve, step, prepare)

            dve.wait_ge(s["resid2"], ITEMS)
            dve.wait_ge(s["late_in"], LATE_LOADS)
            dve.sem_inc(s["x2"], 1)
            dve.wait_ge(s["fc_hi"], 1)
            tt(FCL[:, :], pW[:, :], FCH[:, :].bitcast(FP32), ALU.subtract).then_inc(s["fc_out"], 1)

            def add_to_x(b, z):
                return tt(seq(X, b), seq(X, b), z, ALU.add)

            def spiking(n, live):
                if live(4):
                    i = n - 4
                    dve.wait_ge(s["s_cnt"], at["s_cnt"] + i + 1)
                    if some(i):
                        dve.wait_ge(s["s_cr"], i)
                        alone(dve, s["dve_passed"], i)
                    stats(lambda j: pQ[:, j * P:(j + 1) * P], ST3, MV3, s["scv_st"], i + 1).then_inc(s["s_cv"], 1)
                if live(2):
                    i = n - 2
                    dve.wait_ge(s["s_xrs"], at["s_xrs"] + i + 1)
                    if some(i):
                        dve.wait_ge(s["s_xT_ps"], at["s_xT_ps"] + i)
                    tt(tiles(XR2[:, :]), tiles(seq(X, i)), per_tile(R2[:, :]), ALU.mult).then_inc(s["s_xr"], 1)
                if live(0):
                    if some(n):
                        dve.wait_ge(s["s_ir"], at["s_ir"] + n)
                        alone(dve, s["dve_passed"], n)
                    stats(lambda j: tile(XI, n, j), ST1, MV1, s["siv_st"], at["siv_st"] + n + 1).then_inc(s["s_iv"], 1)
                if live(2):
                    i = n - 2
                    dve.wait_ge(s["s_hi"], at["s_hi"] + i + 1)
                    tt(X2L[:, :], pX2[:, :], X2H[:, :].bitcast(FP32), ALU.subtract).then_inc(s["s_lo"], 1)
                if live(1):
                    i = n - 1
                    dve.wait_ge(s["s_zi"], i + 1)
                    add_to_x(i, XR[:, :]).then_inc(s["s_x1"], 1)
                    dve.wait_ge(s["s_x1"], i + 1)
                    alone(dve, s["dve_passed"], i + 1)
                    stats(lambda j: tile(X, i, j), ST2, MV2, s["sxv_st"], at["sxv_st"] + i + 1).then_inc(s["s_xv"], 1)
                if live(3):
                    i = n - 3
                    dve.wait_ge(s["s_y_ps"], at["s_y_ps"] + (i + 1) * FB)
                    if some(i):
                        dve.wait_ge(s["s_cnt"], at["s_cnt"] + i)
                    nc.vector.tensor_copy(YM[:, :], pY[:, :]).then_inc(s["s_y1"], 1)
                    dve.wait_ge(s["s_y1"], i + 1)
                    mem = YM
                    for t in range(STEPS):
                        ts(SPK[t][:, :], mem[:, :], 1.0, None, ALU.is_gt).then_inc(s["s_spk"], 1)
                        if t == STEPS - 1:
                            break
                        stt(out=ACC[:, :], in0=mem[:, :], scalar=BETA, in1=YM[:, :], op0=ALU.mult,
                            op1=ALU.add).then_inc(s["s_acc"], 1)
                        dve.wait_ge(s["s_spk"], i * STEPS + t + 1)
                        dve.wait_ge(s["s_acc"], i * (STEPS - 1) + t + 1)
                        mem = MEM
                        tt(MEM[:, :], ACC[:, :], SPK[t][:, :], ALU.subtract).then_inc(s["s_mem"], 1)
                        dve.wait_ge(s["s_mem"], i * (STEPS - 1) + t + 1)
                if live(5):
                    i = n - 5
                    dve.wait_ge(s["s_zc"], i + 1)
                    add_to_x(i, EK[:, :]).then_inc(s["s_x2"], 1)

            pipeline(dve, 5, spiking)

            def ssm_in(n, live):
                if live(0):
                    if isinstance(n, int):
                        dve.wait_ge(s["s_x2"], BATCH)
                    if some(n):
                        dve.wait_ge(s["c_rs"], at["c_rs"] + n)
                        alone(dve, s["dve_passed"], n)
                    stats(lambda j: tile(X, n, j), ST2, MV2, s["cxv_st"], at["cxv_st"] + n + 1).then_inc(s["c_xv"], 1)
                    dve.wait_ge(s["c_rs"], at["c_rs"] + n + 1)
                    if some(n):
                        dve.wait_ge(s["c_xT_ps"], at["c_xT_ps"] + n)
                    tt(tiles(XR2[:, :]), tiles(seq(X, n)), per_tile(R2[:, :]), ALU.mult).then_inc(s["c_xr"], 1)
                if live(1):
                    i = n - 1
                    dve.wait_ge(s["c_u_ps"], at["c_u_ps"] + i + 1)
                    tt(tiles(UALL[:, bass.ds(i * SEQ, SEQ)]), tiles(pY[:, :]), BIN[:, :].unsqueeze(1).broadcast_to([P, TILES, P]),
                       ALU.add).then_inc(s["c_u"], 1)

            pipeline(dve, 2, ssm_in)

            def ssm_out(item):
                dve.wait_ge(s["c_o_ps"], item + 1)
                if some(item):
                    dve.wait_ge(s["c_zo"], item)
                tt(tiles(EKT[:, :]), tiles(pXT[:, :]), BOUT[:, :].unsqueeze(1).broadcast_to([P, TILES, P]), ALU.add).then_inc(s["c_z"], 1)
                dve.wait_ge(s["c_z"], item + 1)
                if some(item):
                    dve.wait_ge(s["c_or"], at["c_or"] + item)
                    alone(dve, s["dve_passed"], item)
                stats(lambda j: EKT[:, j * P:(j + 1) * P], ST3, MV3, s["cov_st"], at["cov_st"] + item + 1).then_inc(s["c_ov"], 1)

            def ssm_add(item):
                dve.wait_ge(s["c_zo"], item + 1)
                add_to_x(item, EK[:, :]).then_inc(s["c_x"], 1)

            with dve.Fori(0, BATCH // GROUP) as g:
                for k in range(TILES):
                    dve.wait_ge(s["c_f_ps"], at["c_f_ps"] + g * TILES + k + 1)
                    pr, pi = PS[4 + (k % 2) * 2], PS[5 + (k % 2) * 2]
                    kr = KRE[:, k * P:(k + 1) * P].unsqueeze(1).broadcast_to([P, GROUP, P])
                    ki = KIM[:, k * P:(k + 1) * P].unsqueeze(1).broadcast_to([P, GROUP, P])
                    kr2 = (KRE2[:, :] if k == 0 else KRE[:, k * P:(k + 1) * P]).unsqueeze(1).broadcast_to([P, GROUP, P])
                    yr, yi = YF[:, k * SEQ:(k + 1) * SEQ], YF[:, (TILES + k) * SEQ:(TILES + k + 1) * SEQ]
                    if k:
                        dve.wait_ge(s["c_yf"], g * TILES + k)
                    tt(tiles(HA[0][:, :]), tiles(pi[:, :]), ki, ALU.mult).then_inc(s["c_m"], 1)
                    tt(tiles(HA[1][:, :]), tiles(pi[:, :]), kr2, ALU.mult).then_inc(s["c_m"], 1)
                    tt(tiles(yr), tiles(pr[:, :]), kr, ALU.mult).then_inc(s["c_m"], 1)
                    tt(tiles(yi), tiles(pr[:, :]), ki, ALU.mult).then_inc(s["c_m"], 1)
                    dve.wait_ge(s["c_m"], (g * TILES + k) * 4 + 4)
                    tt(yr, yr, HA[0][:, :], ALU.subtract)
                    tt(yi, yi, HA[1][:, :], ALU.add).then_inc(s["c_yf"], 1)
                for i in range(GROUP):
                    ssm_out(g * GROUP + i)
                    ssm_add(g * GROUP + i)

            dve.wait_ge(s["c_x"], BATCH)
            nc.vector.memset(SH[:, 0:1], 0.0).then_inc(s["sh0"], 1)
            dve.wait_ge(s["sh0"], 1)

            def mix(n, live):
                if live(0):
                    if some(n):
                        dve.wait_ge(s["d_xs"], at["d_xs"] + n)
                        alone(dve, s["dve_passed"], n)
                    stats(lambda j: tile(X, n, j), ST1, MV1, s["dxv_st"], at["dxv_st"] + n + 1).then_inc(s["d_xv"], 1)
                if live(1):
                    i = n - 1
                    dve.wait_ge(s["d_xT"], at["d_xT"] + i + 1)
                    tt(YM[:, :], SH[:, 1:1 + SEQ], SH[:, 0:SEQ], ALU.subtract).then_inc(s["d_diff"], 1)
                    dve.wait_ge(s["d_diff"], i + 1)
                    if some(i):
                        dve.wait_ge(s["d_r_ps"], at["d_r_ps"] + i)
                    stt(out=HA[0][:, :], in0=YM[:, :], scalar=MU[:, 0:1], in1=SH[:, 0:SEQ], op0=ALU.mult, op1=ALU.add)
                    stt(out=HA[1][:, :], in0=YM[:, :], scalar=MU[:, 1:2], in1=SH[:, 0:SEQ], op0=ALU.mult,
                        op1=ALU.add).then_inc(s["d_mix"], 1)
                if live(2):
                    i = n - 2
                    dve.wait_ge(s["d_sig"], i + 1)
                    dve.wait_ge(s["d_v_ps"], at["d_v_ps"] + i + 1)
                    if some(i):
                        dve.wait_ge(s["d_zo"], i)
                    tt(EK[:, :], pY[:, :], QB[:, :], ALU.mult).then_inc(s["d_rv"], 1)
                    dve.wait_ge(s["d_rv"], i + 1)
                    if some(i):
                        dve.wait_ge(s["d_os"], at["d_os"] + i)
                        alone(dve, s["dve_passed"], i)
                    stats(lambda j: EK[:, j * P:(j + 1) * P], ST3, MV3, s["dov_st"], at["dov_st"] + i + 1).then_inc(s["d_ov"], 1)
                if live(3):
                    i = n - 3
                    dve.wait_ge(s["d_zo"], i + 1)
                    add_to_x(i, EKT[:, :]).then_inc(s["d_out"], 1)

            pipeline(dve, 3, mix)


_ARGS = ["x", "qkv", "wo", "w1", "w2", "lnc", "bo", "fcT", "proj", "winT", "woutT", "alog", "bmat", "cmat", "dtr", "dp",
         "bins", "bouts", "wrT", "wkT", "wvT", "mu", "ident", "cent", "hmask", "iota", "fwd", "fwdx", "inv"]


def spectrum_matrices():
    n = 2 * SEQ
    t = np.arange(SEQ)
    phase = (np.outer(t, t) % n) * (2 * np.pi / n)
    sign = 1.0 - 2.0 * (t % 2)
    re, im = np.cos(phase), -np.sin(phase)
    packed = im.copy()
    packed[:, 0] = sign
    fwd = np.concatenate([re, packed], axis=1)
    re2 = re[:, 0:P].copy()
    re2[:, 0] = sign
    fwdx = np.concatenate([im[:, 0:P], re2], axis=1)
    inv = fwd.T * (2.0 / n)
    inv[0] /= 2
    inv[SEQ] /= 2
    return fwd.astype(np.float32), fwdx.astype(np.float32), inv.astype(np.float32)


def kernel(**inputs):
    import concourse.bacc as bacc
    from concourse.bass_utils import run_bass_kernel_spmd

    a = {k: np.asarray(v) for k, v in inputs.items()}

    def state_rows(m):
        return m.T.reshape(STATES, 2, PAIRS).transpose(1, 0, 2).reshape(P, PAIRS)

    fwd, fwdx, inv = spectrum_matrices()
    head = np.arange(P) // DH
    lay = {
        "x": a["L0_attn_x"],
        "qkv": np.concatenate([a["L0_attn_wq"], a["L0_attn_wk"], a["L0_attn_wv"]], axis=2),
        "wo": a["L0_attn_wo"],
        "w1": a["L0_attn_w1"],
        "w2": a["L0_attn_w2"],
        "lnc": np.stack([a["L0_attn_ln1_w"], a["L0_attn_ln1_b"], a["L0_attn_ln2_w"], a["L0_attn_ln2_b"]], axis=2),
        "bo": a["L0_attn_bo"],
        "fcT": a["L0_ffn_W_fc"].T,
        "proj": a["L0_ffn_W_proj"].T,
        "winT": a["L1_attn_Win"].T,
        "woutT": a["L1_attn_Wout"].T,
        "alog": state_rows(a["L1_attn_A_log"]),
        "bmat": state_rows(a["L1_attn_B"]),
        "cmat": state_rows(a["L1_attn_C"]),
        "dtr": np.repeat(a["L1_attn_dt"].reshape(2, PAIRS), STATES, axis=0),
        "dp": a["L1_attn_Dp"].reshape(1, P),
        "bins": a["L1_attn_bin_"].reshape(1, P),
        "bouts": a["L1_attn_bout"].reshape(1, P),
        "wrT": a["L1_ffn_W_r"].T,
        "wkT": a["L1_ffn_W_k"].T,
        "wvT": a["L1_ffn_W_v"].T,
        "mu": np.stack([a["L1_ffn_mu_r"], a["L1_ffn_mu_k"]], axis=1),
        "ident": np.eye(P, dtype=np.float32),
        "cent": np.eye(P, dtype=np.float32) - np.float32(1.0 / P),
        "hmask": (head[:, None] == head[None, :]).astype(np.float32),
        "iota": np.ascontiguousarray(np.broadcast_to(np.arange(P, dtype=np.float32), (P, P))),
        "fwd": fwd, "fwdx": fwdx, "inv": inv,
    }
    nc = bacc.Bacc("TRN2", target_bir_lowering=False, num_devices=1)
    arrays, args = {}, []
    for name in _ARGS:
        v = np.ascontiguousarray(lay[name])
        arrays[f"in_{name}"] = v
        args.append(nc.dram_tensor(f"in_{name}", v.shape, mybir.dt.from_np(v.dtype), kind="ExternalInput").ap())
    args.append(nc.dram_tensor("out_0", (BATCH, SEQ, P), FP32, kind="ExternalOutput").ap())
    build(nc, *args)
    r = run_bass_kernel_spmd(nc, [arrays], core_ids=[0])
    return r.results[0]["out_0"]
```

```python
import numpy as np
import concourse.bass as bass
from concourse import mybir
from contextlib import ExitStack

FP32 = mybir.dt.float32
F32R = mybir.dt.float32r
BF16 = mybir.dt.bfloat16
ALU = mybir.AluOpType
ACT = mybir.ActivationFunctionType
AX = mybir.AxisListType

P = 128
BATCH = 8
SEQ = 512
TILES = SEQ // P
LAYERS = 6
HEADS = 8
DH = P // HEADS
FB = 4
STATES = 64
BINS = 2 * SEQ // P
GROUP = 4
PAIRS = P // 2
EPS = 1e-5
LEAK = 0.01
BETA = 0.9
STEPS = 5
ITEMS = LAYERS * BATCH


def some(value):
    return not isinstance(value, int) or value > 0


def alone(eng, passed, value):
    if not isinstance(value, int):
        eng.sem_inc(passed, 1)


SHARED = [
    [("siv_st", 8), ("dxv_st", 8)],
    [("sxv_st", 8), ("cov_st", 8)],
    [("cxv_st", 8), ("dov_st", 8)],
    [("i_var", 8), ("s_iv", 8), ("d_xv", 8)],
    [("s_xv", 8), ("c_ov", 8)],
    [("c_xv", 8), ("d_ov", 8)],
    [("i_ve", 8), ("si_ve", 8), ("dx_ve", 8)],
    [("sx_ve", 8), ("co_ve", 8)],
    [("cx_ve", 8), ("do_ve", 8)],
    [("i_rstd", 8), ("s_ir", 8), ("d_xs", 8)],
    [("s_xrs", 8), ("c_or", 8)],
    [("c_rs", 8), ("d_os", 8)],
    [("si_r", 8), ("dx_r", 8)],
    [("si_mr", 8), ("dx_mr", 8)],
    [("sc_r", 8), ("co_r", 8)],
    [("sc_mr", 8), ("co_mr", 8)],
    [("x2T_ps", 48), ("s_xT_ps", 8), ("d_xT_ps", 8)],
    [("xT_ps", 48), ("c_xT_ps", 8)],
    [("k_ps2", 48), ("c_f_ps", 8)],
    [("g_ps", 48), ("d_k_ps", 8)],
    [("q_ps", 48), ("s_cnt", 8), ("d_r_ps", 8)],
    [("out_ps", 48), ("d_v_ps", 8)],
    [("m_ps", 48), ("c_u_ps", 8)],
    [("y_ps", 192), ("s_y_ps", 32)],
    [("h_ps", 192), ("s_h_ps", 32)],
    [("ha", 192), ("s_relu", 32), ("d_relu", 8)],
    [("q_fm", 48), ("s_sq", 32), ("d_sq", 8)],
    [("x2h", 48), ("s_hi", 8), ("d_xT", 8)],
    [("xTf", 48), ("c_xT", 8)],
    [("q_exp", 48), ("c_xr", 8)],
]


def seq(t, b):
    return t[:, bass.ds(b * SEQ, SEQ)]


def tile(t, b, j):
    return t[:, bass.ds(b * SEQ + j * P, P)]


def per_tile(col):
    return col.unsqueeze(2).broadcast_to([P, TILES, P])


def tiles(ap):
    return ap.rearrange("p (j c) -> p j c", c=P)


def heads(ap):
    return ap.rearrange("p (a d) -> p a d", d=DH)


def pipeline(eng, lag, step):
    for n in range(lag):
        step(n, lambda k, n=n: n - k >= 0)
    with eng.Fori(lag, BATCH) as n:
        step(n, lambda k: True)
    for n in range(BATCH, BATCH + lag):
        step(n, lambda k, n=n: n - k < BATCH)


def layers(eng, step):

    def layer(first, slot, following):
        step(first, 0, (slot, 1 - slot, 1 - slot), None)
        step(first + 1, 1, (slot, slot, 1 - slot), None)
        start = 2
        if isinstance(first, int) and first == 0:
            step(2, 2, (slot, slot, slot), None)
            start = 3
        with eng.Fori(start, BATCH - 1) as b:
            step(first + b, b, (slot, slot, slot), None)
        step(first + BATCH - 1, BATCH - 1, (slot, slot, slot), following)

    layer(0, 0, (1, 1, 1))
    with eng.Fori(0, (LAYERS - 2) // 2) as r:
        layer(r * (2 * BATCH) + BATCH, 1, (r * 2 + 2, 0, r + 2))
        layer(r * (2 * BATCH) + 2 * BATCH, 0, (r * 2 + 3, 1, r + 2))
    last = (LAYERS - 1) % 2
    layer((LAYERS - 1) * BATCH, last, None)
    for extra in range(2):
        step(ITEMS + extra, extra, (last, last, last), None)


def live(n):
    if not isinstance(n, int):
        return True, True, True
    return n < ITEMS, 1 <= n <= ITEMS, 2 <= n <= ITEMS + 1


def interleaved(forward, inverse, project, mix):
    def mixed(n):
        mix(n, lambda k: 0 <= n - k < BATCH)

    for k in range(TILES):
        forward(0, k)
    for i in range(GROUP):
        inverse(0, i)
        if i:
            project(i - 1)
    for k in range(TILES):
        forward(1, k)
        if k == 0:
            project(GROUP - 1)
        mixed(k)
    for i in range(GROUP):
        inverse(1, i)
        if i:
            project(GROUP + i - 1)
            mixed(GROUP + i - 1)
    project(BATCH - 1)
    for n in range(BATCH - 1, BATCH + 3):
        mixed(n)


def before(b, k):
    return (b - k) % BATCH if isinstance(b, int) else b - k


def build(nc, x, qkv, wo, w1, w2, lnc, bo, fcT, proj, winT, woutT, alog, bmat, cmat, dtr, dp, bins_,
          bouts, wrT, wkT, wvT, mu, ident, cent, hmask, iota, fwd, fwdx, inv, out):
    ctx = ExitStack()
    with ctx:
        def sb(name, shape, dt=FP32):
            return ctx.enter_context(nc.sbuf_tensor(name, [P, *shape] if len(shape) == 1 else shape, dt))

        def sem(name):
            return ctx.enter_context(nc.semaphore(name))

        X = sb("X", [BATCH * SEQ])
        XI = sb("XI", [BATCH * SEQ])
        ID = sb("ID", [P])
        CENT = sb("CENT", [P])
        HMASK = sb("HMASK", [P])
        IOTA = sb("IOTA", [P])
        EIGHTH = sb("EIGHTH", [1, P])
        MHALF = sb("MHALF", [2 * TILES])
        IDB = sb("IDB", [P], BF16)
        QKV = [sb(f"QKV{s}", [3 * P]) for s in range(2)]
        WO = [sb(f"WO{s}", [P]) for s in range(2)]
        W1 = [sb(f"W1{s}", [FB * P]) for s in range(2)]
        W2 = [sb(f"W2{s}", [FB * P]) for s in range(2)]
        LNC = [sb(f"LNC{s}", [4]) for s in range(2)]
        BO = [sb(f"BO{s}", [1, P]) for s in range(2)]
        QKH = [sb(f"QKH{s}", [2 * P], F32R) for s in range(2)]
        QKL = [sb(f"QKL{s}", [2 * P], F32R) for s in range(2)]
        WV = [sb(f"WV{s}", [P]) for s in range(2)]
        W1H = [sb(f"W1H{s}", [FB * P], F32R) for s in range(2)]
        W1L = [sb(f"W1L{s}", [FB * P], F32R) for s in range(2)]
        BIAS = [sb(f"BIAS{s}", [2 + FB]) for s in range(2)]
        BM = [sb(f"BM{s}", [P]) for s in range(2)]
        LNP = [sb(f"LNP{i}", [P]) for i in range(2)]
        MBV = sb("MBV", [P])
        STATS, JOIN, RSTD = sb("STATS", [P, 2 * TILES, 6]), sb("JOIN", [P, 6, 2 * TILES]), sb("RSTD", [2 * TILES])
        ST1, MV1, VE1, R1 = sb("ST1", [24]), sb("MV1", [8]), sb("VE1", [4]), sb("R1", [4])
        ST2, MV2, VE2, R2 = sb("ST2", [24]), sb("MV2", [8]), sb("VE2", [4]), sb("R2", [4])
        XR = sb("XR", [SEQ])
        XTF = sb("XTF", [SEQ])
        XTH, XTL = sb("XTH", [SEQ], F32R), sb("XTL", [SEQ], F32R)
        QF, QB = sb("QF", [SEQ]), sb("QB", [SEQ])
        QMX, QSM, QRC = sb("QMX", [32]), sb("QSM", [32]), sb("QRC", [32])
        QS = sb("QS", [SEQ])
        NKM, KSM, KRC = sb("NKM", [1]), sb("KSM", [1]), sb("KRC", [1])
        EK, EKT = sb("EK", [SEQ]), sb("EKT", [SEQ])
        GT, CT, MM = sb("GT", [P]), sb("CT", [P]), sb("MM", [P])
        NM1, ST3, MV3, VE3, R3, NM3 = sb("NM1", [4]), sb("ST3", [24]), sb("MV3", [8]), sb("VE3", [4]), sb("R3", [4]), sb("NM3", [4])
        ST4, MV4, VE4, R4, NM2 = sb("ST4", [24]), sb("MV4", [8]), sb("VE4", [4]), sb("R4", [4]), sb("NM2", [4])
        STX, MVX = sb("STX", [BATCH * TILES * 6]), sb("MVX", [BATCH * TILES * 2])
        VEX, RX = sb("VEX", [BATCH * TILES]), sb("RX", [BATCH * TILES])
        XR2 = sb("XR2", [SEQ])
        X2H, X2L = sb("X2H", [SEQ], F32R), sb("X2L", [SEQ], F32R)
        HA = [sb(f"HA{i}", [SEQ]) for i in range(2)]
        HL = [sb(f"HL{i}", [SEQ]) for i in range(2)]
        FCT = sb("FCT", [FB * P])
        FCH, FCL = sb("FCH", [FB * P], F32R), sb("FCL", [FB * P], F32R)
        PROJ = sb("PROJ", [FB * P])
        SPK = [sb(f"SPK{i}", [SEQ], BF16) for i in range(STEPS)]
        YM, ACC, MEM = sb("YM", [SEQ]), sb("ACC", [SEQ]), sb("MEM", [SEQ])
        SH = sb("SH", [1 + SEQ])
        FWD = sb("FWD", [TILES * BINS * P])
        FWDX = sb("FWDX", [TILES * 2 * P])
        INV = sb("INV", [BINS * SEQ])
        BIG = sb("BIG", [PAIRS * P])
        E2 = BIG
        UALL = BIG[:, 0:BATCH * SEQ]
        YF = BIG[:, BATCH * SEQ:BATCH * SEQ + BINS * SEQ]
        ALOG, BMAT, CMAT, DTR = (sb(n, [PAIRS]) for n in ("ALOG", "BMAT", "CMAT", "DTR"))
        LA, CDB = sb("LA", [PAIRS]), sb("CDB", [PAIRS])
        E1 = sb("E1", [PAIRS * TILES])
        CE1 = sb("CE1", [PAIRS * 2 * TILES])
        DP = sb("DP", [1, P])
        KTM = sb("KTM", [TILES * P])
        KRE, KIM, KRE2 = sb("KRE", [TILES * P]), sb("KIM", [TILES * P]), sb("KRE2", [P])
        WINT, WOUTT, BIN, BOUT = (sb(n, [P]) for n in ("WINT", "WOUTT", "BIN", "BOUT"))
        WINC = sb("WINC", [P])
        WRT, WKT, WVT, MU = sb("WRT", [P]), sb("WKT", [P]), sb("WVT", [P]), sb("MU", [2])

        PS = [ctx.enter_context(nc.psum_tensor(f"PS{i}", [P, SEQ], FP32)) for i in range(8)]
        pXT, pQ, pK, pX2, pH, pY, pW = PS[0], PS[1], PS[2], PS[3], PS[4:6], PS[6], PS[7]

        signals = {name: sem(name) for name in (
            "bias_out bias_ps bm_out bm_ps c_in c_m c_o_ps c_ps c_u c_x c_yT c_y_ps c_yf c_z c_zo cdb ce1 "
            "ce1_zero ct d_diff d_mix d_out d_rv d_sig d_zn d_zo do_mr do_r dve_passed e1 e1_arg e2 e2_arg "
            "eighth ek ekT_ps ek_tm fc_hi fc_out fc_ps gt hl i_st k_out k_ps k_rec kf kf_ps kmax ktm la "
            "la_exp late_in ln1_rstd ln2_rstd ln_part lnp m_ready mbv p_const pool_passed q_blk q_nrm q_rec "
            "q_sub q_sum qmax qs resid1 resid2 s_acc s_cr s_cv s_lo s_mem s_spk s_x1 s_x2 s_xr s_y1 s_zc "
            "s_zi sc_ve scv_st sh0 sp_passed ssm_in stats_ready stored w1_hi w1_out w1_ps w_ready win_out "
            "win_ps wqk_hi wqkv_out wqkv_ps x2 x2l xTl x_in xi_init xr xr2 ").split()}
        starts = {}
        for row in SHARED:
            first, total = sem(row[0][0]), 0
            for name, counts in row:
                signals[name], starts[name] = first, total
                total += counts
        s = {"w_in": [sem("w_in0"), sem("w_in1")], **signals}
        at = starts

        block = ctx.enter_context(nc.Block())

        @block.sync
        def _(sp):
            def load(l, slot):
                sp.dma_start(QKV[slot][:, :], qkv[bass.ds(l, 1)].rearrange("a p n -> (a p) n")).then_inc(s["w_in"][slot], 16)
                sp.dma_start(LNC[slot][:, :], lnc[bass.ds(l, 1)].rearrange("a p n -> (a p) n")).then_inc(s["w_in"][slot], 16)
                sp.dma_start(W1[slot][:, :], w1[bass.ds(l, 1)].rearrange("a p n -> (a p) n")).then_inc(s["w_in"][slot], 16)
                sp.dma_start(WO[slot][:, :], wo[bass.ds(l, 1)].rearrange("a p n -> (a p) n")).then_inc(s["w_in"][slot], 16)
                sp.dma_start(tiles(W2[slot][:, :]),
                             w2[bass.ds(l, 1)].rearrange("a (f p) n -> (a p) f n", p=P)).then_inc(s["w_in"][slot], 16)
                sp.dma_start(BO[slot][:, :], bo[bass.ds(l, 1)]).then_inc(s["w_in"][slot], 16)

            for t, d in ((ALOG, alog), (DTR, dtr), (IOTA, iota), (BMAT, bmat), (CMAT, cmat), (DP, dp)):
                sp.dma_start(t[:, :], d).then_inc(s["ssm_in"], 16)
            sp.dma_start(CENT[:, :], cent).then_inc(s["c_in"], 16)
            sp.dma_start(ID[:, :], ident).then_inc(s["c_in"], 16)
            sp.dma_start(HMASK[:, :], hmask).then_inc(s["c_in"], 16)
            load(0, 0)
            for b in range(BATCH):
                sp.dma_start(tiles(X[:, b * SEQ:(b + 1) * SEQ]),
                             x[b].rearrange("(j p) c -> p j c", p=P)).then_inc(s["x_in"], 16)
            load(1, 1)
            sp.dma_start(FWD[:, :].rearrange("p (j f) -> p j f", j=TILES), fwd.rearrange("(j p) f -> p j f", p=P)).then_inc(s["late_in"], 16)
            sp.dma_start(FWDX[:, :].rearrange("p (j f) -> p j f", j=TILES), fwdx.rearrange("(j p) f -> p j f", p=P)).then_inc(s["late_in"], 16)
            sp.dma_start(INV[:, :].rearrange("p (k t) -> p k t", k=BINS), inv.rearrange("(k p) t -> p k t", p=P)).then_inc(s["late_in"], 16)
            sp.dma_start(FCT[:, :], fcT).then_inc(s["late_in"], 16)
            sp.dma_start(tiles(PROJ[:, :]), proj.rearrange("(f p) n -> p f n", p=P)).then_inc(s["late_in"], 16)
            for t, d in ((WINT, winT), (WOUTT, woutT), (WRT, wrT), (WKT, wkT), (WVT, wvT), (MU, mu)):
                sp.dma_start(t[:, :], d).then_inc(s["late_in"], 16)
            sp.dma_start(BIN[:, :], bins_.broadcast_to([P, P])).then_inc(s["late_in"], 16)
            sp.dma_start(BOUT[:, :], bouts.broadcast_to([P, P])).then_inc(s["late_in"], 16)

            with sp.Fori(0, (LAYERS - 2) // 2) as r:
                sp.wait_ge(s["resid2"], r * (2 * BATCH) + BATCH)
                alone(sp, s["sp_passed"], r * (2 * BATCH) + BATCH)
                sp.wait_ge(s["w_ready"], r * 2 + 2)
                alone(sp, s["sp_passed"], r * 2 + 2)
                load(r * 2 + 2, 0)
                sp.wait_ge(s["resid2"], r * (2 * BATCH) + 2 * BATCH)
                alone(sp, s["sp_passed"], r * (2 * BATCH) + 2 * BATCH)
                sp.wait_ge(s["w_ready"], r * 2 + 3)
                alone(sp, s["sp_passed"], r * 2 + 3)
                load(r * 2 + 3, 1)

            with sp.Fori(0, BATCH) as b:
                sp.wait_ge(s["d_out"], b + 1)
                alone(sp, s["sp_passed"], b + 1)
                sp.dma_start(out[bass.ds(b, 1)].rearrange("a (j p) c -> (a p) j c", p=P), tiles(seq(X, b))).then_inc(s["stored"], 16)
            sp.wait_ge(s["stored"], 16 * BATCH)

        W_LOADS = 6 * 16
        SSM_LOADS = 6 * 16
        LATE_LOADS = 13 * 16

        @block.tensor
        def _(pe):
            def mm(o, l, r, start=True, stop=True):
                return nc.tensor.matmul(o, l, r, start=start, stop=stop, skip_group_check=True)

            def split3(o, lh, ll, rh, rl):
                mm(o, ll, rh, True, False)
                mm(o, lh, rl, False, False)
                return mm(o, lh, rh, False, True)

            def transposes(o, i):
                for j in range(TILES):
                    last = nc.tensor.transpose(o[:, j * P:(j + 1) * P], i[:, j * P:(j + 1) * P], ID[:, :])
                return last

            def prepare(l, slot, times, part):
                if part == 0:
                    pe.wait_ge(s["w_in"][slot], times * W_LOADS)
                    pe.wait_ge(s["lnp"], l + 1)
                    if some(l):
                        pe.wait_ge(s["bm_out"], l)
                    mm(pW[:, 0:3 * P], LNP[0][:, :], QKV[slot][:, :]).then_inc(s["wqkv_ps"], 1)
                if part == 1:
                    pe.wait_ge(s["wqkv_out"], 2 * (l + 1))
                    mm(pW[:, :], LNP[1][:, :], W1[slot][:, :]).then_inc(s["w1_ps"], 1)
                if part == 2:
                    pe.wait_ge(s["w1_out"], l + 1)
                    mm(pW[:, 0:1], QKV[slot][:, 0:P], LNC[slot][:, 1:2])
                    mm(pW[:, 1:2], QKV[slot][:, 2 * P:3 * P], LNC[slot][:, 1:2])
                    for f in range(FB):
                        last = mm(pW[:, 2 + f:3 + f], W1[slot][:, f * P:(f + 1) * P], LNC[slot][:, 3:4])
                    last.then_inc(s["bias_ps"], 1)
                if part == 3:
                    pe.wait_ge(s["mbv"], l + 1)
                    mm(pW[:, 0:P], MBV[:, :], WO[slot][:, :], True, False)
                    mm(pW[:, 0:P], EIGHTH[0:1, :], BO[slot][0:1, :], False, True).then_inc(s["bm_ps"], 1)

            pe.wait_ge(s["c_in"], 3 * 16)
            pe.wait_ge(s["eighth"], 1)
            for part in range(4):
                prepare(0, 0, 1, part)
                if part == 0:
                    pe.wait_ge(s["ce1"], 1)
                pe.wait_ge(s["e2"], (part + 1) * PAIRS // 16)
                for i in range(part * PAIRS // 4, (part + 1) * PAIRS // 4):
                    last = mm(pH[0][:, i * 8:i * 8 + 8], E2[:, i * P:(i + 1) * P], CE1[:, i * 8:i * 8 + 8])
            last.then_inc(s["k_ps"], 1)
            pe.wait_ge(s["k_out"], 1)

            def step(n, b, slots, following):
                has_n, has_p, has_m = live(n)
                wa, wp, wf = slots
                m = n - 2

                def h(item, f, w, there):
                    if not there:
                        return
                    if f == 0:
                        pe.wait_ge(s["x2l"], item + 1)
                    k = item * FB + f
                    if some(k - 1):
                        pe.wait_ge(s["ha"], k - 1)
                    o = slice(f * P, (f + 1) * P)
                    split3(pH[f % 2][:, :], W1H[w][:, o], W1L[w][:, o], X2H[:, :], X2L[:, :]).then_inc(s["h_ps"], 1)

                def y(item, f):
                    if not has_m:
                        return
                    pe.wait_ge(s["hl"], item * FB + f + 1)
                    if f == 0:
                        if some(item):
                            pe.wait_ge(s["resid2"], item)
                    for j in range(TILES):
                        last = mm(pY[:, j * P:(j + 1) * P], HL[f % 2][:, j * P:(j + 1) * P],
                                  W2[wf][:, f * P:(f + 1) * P], f == 0 and j == 0, f == FB - 1)
                    last.then_inc(s["y_ps"], 1)

                def part(i):
                    if following is not None:
                        prepare(*following, i)

                if has_n:
                    pe.wait_ge(s["xr"], n + 1)
                    if some(n):
                        pe.wait_ge(s["ek_tm"], n)
                    transposes(pXT, XR).then_inc(s["xT_ps"], 1)
                part(0)
                y(m, 0)
                if has_p:
                    pe.wait_ge(s["m_ready"], n)
                    pe.wait_ge(s["qs"], n)
                    pe.wait_ge(s["q_fm"], n)
                    for j in range(TILES):
                        last = mm(pQ[:, j * P:(j + 1) * P], QS[:, j * P:(j + 1) * P], MM[:, :])
                    last.then_inc(s["out_ps"], 1)
                h(m, 2, wf, has_m)
                part(1)
                if has_n:
                    pe.wait_ge(s["xTl"], n + 1)
                    split3(pK[:, :], QKH[wa][:, P:2 * P], QKL[wa][:, P:2 * P], XTH[:, :], XTL[:, :]).then_inc(s["k_ps2"], 1)
                    if some(n):
                        pe.wait_ge(s["resid1"], n)
                    split3(pQ[:, :], QKH[wa][:, 0:P], QKL[wa][:, 0:P], XTH[:, :], XTL[:, :]).then_inc(s["q_ps"], 1)
                y(m, 1)
                h(m, 3, wf, has_m)
                part(2)
                if has_n:
                    pe.wait_ge(s["ek"], n + 1)
                    transposes(pXT, EK).then_inc(s["ekT_ps"], 1)
                y(m, 2)
                if has_n:
                    pe.wait_ge(s["ek_tm"], n + 1)
                    for j in range(TILES):
                        last = mm(pK[:, 0:P], XR[:, j * P:(j + 1) * P], EKT[:, j * P:(j + 1) * P], j == 0, j == TILES - 1)
                    last.then_inc(s["g_ps"], 1)
                if has_p:
                    pe.wait_ge(s["xr2"], n)
                    transposes(pX2, XR2).then_inc(s["x2T_ps"], 1)
                y(m, 3)
                part(3)
                if has_n:
                    pe.wait_ge(s["gt"], n + 1)
                    mm(pK[:, P:2 * P], WV[wa][:, :], GT[:, :]).then_inc(s["c_ps"], 1)
                h(m + 1, 0, wp, has_p)
                if has_n:
                    pe.wait_ge(s["ct"], n + 1)
                    mm(pK[:, 2 * P:3 * P], CT[:, :], WO[wa][:, :]).then_inc(s["m_ps"], 1)
                h(m + 1, 1, wp, has_p)

            layers(pe, step)

            pe.wait_ge(s["late_in"], LATE_LOADS)
            pe.wait_ge(s["bm_out"], LAYERS)
            mm(pW[:, :], CENT[:, :], FCT[:, :]).then_inc(s["fc_ps"], 1)
            pe.wait_ge(s["fc_out"], 1)
            mm(pW[:, 0:P], CENT[:, :], WINT[:, :]).then_inc(s["win_ps"], 1)
            pe.wait_ge(s["win_out"], 1)

            def spectrum(unit):
                part, k = divmod(unit, TILES)
                if unit == 0:
                    pe.wait_ge(s["ktm"], 1)
                elif k == 0:
                    pe.wait_ge(s["kf"], part)
                for j in range(TILES):
                    lhs = FWD[:, j * BINS * P + (part % 2) * SEQ + k * P:][:, 0:P]
                    if part == 1 and k == 0:
                        lhs = FWDX[:, j * 2 * P:j * 2 * P + P]
                    if part == 2:
                        lhs = FWDX[:, j * 2 * P + P:(j + 1) * 2 * P]
                    last = mm(pW[:, k * P:(k + 1) * P], lhs, KTM[:, j * P:(j + 1) * P], j == 0, j == TILES - 1)
                if k == TILES - 1 or part == 2:
                    last.then_inc(s["kf_ps"], 1)

            def spiking(n, live):
                m = n - 2

                def hidden(f):
                    if not live(2):
                        return
                    if f == 0:
                        pe.wait_ge(s["s_lo"], m + 1)
                    k = m * FB + f
                    if some(k - 1):
                        pe.wait_ge(s["s_relu"], at["s_relu"] + k - 1)
                    o = slice(f * P, (f + 1) * P)
                    split3(pH[f % 2][:, :], FCH[:, o], FCL[:, o], X2H[:, :], X2L[:, :]).then_inc(s["s_h_ps"], 1)

                def projected(f):
                    if live(2):
                        proj_block(m, f)

                hidden(0)
                hidden(1)
                projected(0)
                hidden(2)
                projected(1)
                hidden(3)
                if live(6):
                    i = n - 6
                    pe.wait_ge(s["c_xr"], at["c_xr"] + i + 1)
                    if some(i):
                        pe.wait_ge(s["c_xT"], at["c_xT"] + i)
                    transposes(pXT, QS).then_inc(s["c_xT_ps"], 1)
                projected(2)
                if live(1):
                    pe.wait_ge(s["s_xr"], n)
                    transposes(pX2, XR2).then_inc(s["s_xT_ps"], 1)
                if isinstance(n, int) and n <= 5:
                    spectrum(n)
                if isinstance(n, int) and 8 <= n <= 10:
                    spectrum(n - 2)
                projected(3)
                if live(6):
                    pe.wait_ge(s["c_xT"], at["c_xT"] + i + 1)
                    if some(i):
                        pe.wait_ge(s["c_u"], i)
                    for j in range(TILES):
                        last = mm(pK[:, j * P:(j + 1) * P], XTF[:, j * P:(j + 1) * P], WINC[:, :])
                    last.then_inc(s["c_u_ps"], 1)
                if live(3):
                    i = n - 3
                    if some(i):
                        pe.wait_ge(s["s_zc"], i)
                    for t in range(STEPS):
                        pe.wait_ge(s["s_spk"], i * STEPS + t + 1)
                        last = mm(pQ[:, :], IDB[:, :], SPK[t][:, :], t == 0, t == STEPS - 1)
                    last.then_inc(s["s_cnt"], 1)

            def proj_block(i, f):
                pe.wait_ge(s["s_sq"], at["s_sq"] + i * FB + f + 1)
                if f == 0:
                    if some(i):
                        pe.wait_ge(s["s_y1"], i)
                for j in range(TILES):
                    last = mm(pY[:, j * P:(j + 1) * P], HL[f % 2][:, j * P:(j + 1) * P],
                              PROJ[:, f * P:(f + 1) * P], f == 0 and j == 0, f == FB - 1)
                last.then_inc(s["s_y_ps"], 1)

            pipeline(pe, 6, spiking)

            def out_proj(item):
                pe.wait_ge(s["c_yT"], item + 1)
                if some(item):
                    pe.wait_ge(s["c_z"], item)
                for j in range(TILES):
                    last = mm(pY[:, j * P:(j + 1) * P], XTF[:, j * P:(j + 1) * P], WOUTT[:, :])
                last.then_inc(s["c_o_ps"], 1)

            pe.wait_ge(s["kf"], 3)
            pe.wait_ge(s["s_y1"], BATCH)
            pe.wait_ge(s["s_relu"], at["s_relu"] + BATCH * FB)

            def forward(g, k):
                if k == 0:
                    pe.wait_ge(s["c_u"], (g + 1) * GROUP)
                if g and k == 0:
                    pe.wait_ge(s["c_yT"], g * GROUP)
                if g and k == 1:
                    pe.wait_ge(s["c_z"], g * GROUP)
                if k >= 2:
                    pe.wait_ge(s["c_yf"], g * TILES + k - 1)
                u4 = UALL[:, g * GROUP * SEQ:(g + 1) * GROUP * SEQ].rearrange("p (b j d) -> p j b d", b=GROUP, j=TILES)
                for half in range(2):
                    bank = PS[4 + (k % 2) * 2 + half]
                    for j in range(TILES):
                        lhs = FWD[:, j * BINS * P + half * SEQ + k * P:][:, 0:P]
                        last = mm(bank[:, :].rearrange("p (b d) -> p b d", b=GROUP), lhs, u4[:, j], j == 0, j == TILES - 1)
                last.then_inc(s["c_f_ps"], 1)

            def inverse(g, i):
                item = g * GROUP + i
                if i == 0:
                    pe.wait_ge(s["c_yf"], (g + 1) * TILES)
                if i >= 2:
                    pe.wait_ge(s["c_yT"], item - 1)
                bank = PS[4 + i % 2]
                for k in range(BINS):
                    last = mm(bank[:, :], YF[:, k * SEQ + i * P:k * SEQ + (i + 1) * P],
                              INV[:, k * SEQ:(k + 1) * SEQ], k == 0, k == BINS - 1)
                last.then_inc(s["c_y_ps"], 1)

            def mix(n, live):
                if live(1):
                    i = n - 1
                    pe.wait_ge(s["d_zn"], i + 1)
                    if some(i):
                        pe.wait_ge(s["d_xT"], at["d_xT"] + i)
                    transposes(pX2, XR2).then_inc(s["d_xT_ps"], 1)
                if live(2):
                    i = n - 2
                    pe.wait_ge(s["d_mix"], i + 1)
                    if some(i):
                        pe.wait_ge(s["d_relu"], at["d_relu"] + i)
                    mm(pK[:, :], WKT[:, :], QS[:, :]).then_inc(s["d_k_ps"], 1)
                    if some(i):
                        pe.wait_ge(s["d_sig"], i)
                    for j in range(TILES):
                        last = mm(pQ[:, j * P:(j + 1) * P], XR[:, j * P:(j + 1) * P], WRT[:, :])
                    last.then_inc(s["d_r_ps"], 1)
                    pe.wait_ge(s["d_sq"], at["d_sq"] + i + 1)
                    if some(i):
                        pe.wait_ge(s["d_rv"], i)
                    for j in range(TILES):
                        last = mm(pXT[:, j * P:(j + 1) * P], HL[0][:, j * P:(j + 1) * P], WVT[:, :])
                    last.then_inc(s["d_v_ps"], 1)

            interleaved(forward, inverse, out_proj, mix)

        @block.gpsimd
        def _(pool):
            pool.memset(MHALF[:, :], -0.5).then_inc(s["p_const"], 1)
            pool.memset(CE1[:, :], 0.0).then_inc(s["ce1_zero"], 1)
            pool.wait_ge(s["p_const"], 1)
            own = [0]

            def rstd(mv, ve, r, eps, summed, count):
                pool.tensor_scalar(ve[:, :], mv[:, :].rearrange("p (j t) -> p j t", t=2)[:, :, 1], eps, 1.0,
                                   ALU.add, ALU.mult).then_inc(summed, 1)
                pool.wait_ge(summed, count)
                return pool.tensor_tensor(r[:, :], ve[:, :], MHALF[:, 0:TILES], ALU.pow)

            def mean_rstd(mv, r, nm, powered, r_count, scaled, count):
                pool.wait_ge(powered, r_count)
                pool.tensor_tensor(nm[:, :], mv[:, :].rearrange("p (j t) -> p j t", t=2)[:, :, 0], r[:, :],
                                   ALU.mult).then_inc(scaled, 1)
                pool.wait_ge(scaled, count)
                alone(pool, s["pool_passed"], count)
                return pool.tensor_scalar(nm[:, :], nm[:, :], -1.0, 0.0, ALU.mult, ALU.add)

            for b in range(BATCH):
                cols = slice(b * TILES, (b + 1) * TILES)
                pool.wait_ge(s["i_var"], b + 1)
                pool.tensor_scalar(VEX[:, cols], MVX[:, b * 2 * TILES:(b + 1) * 2 * TILES].rearrange("p (j t) -> p j t", t=2)[:, :, 1],
                                   EPS, 1.0, ALU.add, ALU.mult).then_inc(s["i_ve"], 1)
                pool.wait_ge(s["i_ve"], b + 1)
                pool.tensor_tensor(RX[:, cols], VEX[:, cols], MHALF[:, 0:TILES], ALU.pow).then_inc(s["i_rstd"], 1)

            def join(first, end, turn):
                def part(i):
                    return STATS[:, first:end, i]

                d, g, e, h, f, v = (JOIN[:, i, first:end] for i in range(6))
                pool.wait_ge(s["stats_ready"], turn + 1)
                pool.tensor_tensor(d, part(1), part(4), ALU.subtract)
                pool.tensor_tensor(g, part(2), part(5), ALU.add).then_inc(s["ln_part"], 1)
                pool.wait_ge(s["ln_part"], turn * 4 + 1)
                alone(pool, s["pool_passed"], turn)
                pool.tensor_scalar(e, d, 0.25, 0.0, ALU.mult, ALU.add)
                pool.tensor_scalar(h, g, 1.0 / P, EPS, ALU.mult, ALU.add).then_inc(s["ln_part"], 1)
                pool.wait_ge(s["ln_part"], turn * 4 + 2)
                pool.tensor_tensor(f, e, d, ALU.mult).then_inc(s["ln_part"], 1)
                pool.wait_ge(s["ln_part"], turn * 4 + 3)
                pool.tensor_tensor(v, f, h, ALU.add).then_inc(s["ln_part"], 1)
                pool.wait_ge(s["ln_part"], turn * 4 + 4)
                if first + TILES <= end and end == 2 * TILES:
                    if some(turn - 2):
                        pool.wait_ge(s["xr2"], turn - 2)
                    pool.tensor_tensor(RSTD[:, TILES:end], JOIN[:, 5, TILES:end], MHALF[:, TILES:end],
                                       ALU.pow).then_inc(s["ln2_rstd"], 1)

            def ln1_power(turn):
                if some(turn):
                    pool.wait_ge(s["xr"], turn)
                pool.tensor_tensor(RSTD[:, 0:TILES], JOIN[:, 5, 0:TILES], MHALF[:, 0:TILES],
                                   ALU.pow).then_inc(s["ln1_rstd"], 1)

            join(0, TILES, 0)
            ln1_power(0)

            def step(n, b, slots, following):
                has_n, has_p, _ = live(n)
                if has_n:
                    pool.wait_ge(s["xTf"], n + 1)
                    pool.tensor_tensor(XTL[:, :], XTF[:, :], XTH[:, :].bitcast(FP32), ALU.subtract).then_inc(s["xTl"], 1)
                has_next = not isinstance(n, int) or n < ITEMS - 1
                if has_p or has_next:
                    join(0 if has_next else TILES, 2 * TILES if has_p else TILES, n + 1)
                if has_n:
                    pool.wait_ge(s["qmax"], n + 1)
                    pool.tensor_tensor(heads(QB[:, :]), heads(QB[:, :]), QMX[:, :].unsqueeze(2).broadcast_to([P, 32, DH]),
                                       ALU.subtract).then_inc(s["q_sub"], 1)
                if has_next:
                    ln1_power(n + 1)
                if has_n:
                    pool.wait_ge(s["q_rec"], n + 1)
                    pool.tensor_tensor(heads(QB[:, :]), heads(QB[:, :]), QRC[:, :].unsqueeze(2).broadcast_to([P, 32, DH]),
                                       ALU.mult).then_inc(s["q_nrm"], 1)

            layers(pool, step)

            def add_to_x(b, z):
                return pool.tensor_tensor(seq(X, b), seq(X, b), z, ALU.add)

            def spiking(n, live):
                if live(1):
                    i = n - 1
                    pool.wait_ge(s["s_zi"], i + 1)
                    add_to_x(i, XR[:, :]).then_inc(s["s_x1"], 1)
                if live(5):
                    i = n - 5
                    pool.wait_ge(s["s_zc"], i + 1)
                    add_to_x(i, EK[:, :]).then_inc(s["s_x2"], 1)
                if live(1):
                    i = n - 1
                    pool.wait_ge(s["s_xv"], at["s_xv"] + i + 1)
                    if some(i):
                        pool.wait_ge(s["s_xr"], i)
                        alone(pool, s["pool_passed"], i)
                    rstd(MV2, VE2, R2, EPS, s["sx_ve"], at["sx_ve"] + i + 1).then_inc(s["s_xrs"], 1)
                if live(0):
                    pool.wait_ge(s["s_iv"], at["s_iv"] + n + 1)
                    if some(n):
                        pool.wait_ge(s["s_zi"], n)
                        alone(pool, s["pool_passed"], n)
                    rstd(MV1, VE1, R1, EPS, s["si_ve"], at["si_ve"] + n + 1).then_inc(s["si_r"], 1)
                    mean_rstd(MV1, R1, NM1, s["si_r"], n + 1, s["si_mr"], n + 1).then_inc(s["s_ir"], 1)
                if live(4):
                    i = n - 4
                    pool.wait_ge(s["s_cv"], i + 1)
                    if some(i):
                        pool.wait_ge(s["s_zc"], i)
                        alone(pool, s["pool_passed"], i)
                    rstd(MV3, VE3, R3, EPS * STEPS * STEPS, s["sc_ve"], i + 1).then_inc(s["sc_r"], 1)
                    mean_rstd(MV3, R3, NM3, s["sc_r"], i + 1, s["sc_mr"], i + 1).then_inc(s["s_cr"], 1)
                if live(5):
                    i = n - 5
                    pool.wait_ge(s["c_xv"], at["c_xv"] + i + 1)
                    if some(i):
                        pool.wait_ge(s["c_xr"], at["c_xr"] + i)
                        alone(pool, s["pool_passed"], i)
                    rstd(MV4, VE4, R4, EPS, s["cx_ve"], at["cx_ve"] + i + 1).then_inc(s["c_rs"], 1)

            pipeline(pool, 6, spiking)

            def project(item):
                pool.wait_ge(s["c_ov"], at["c_ov"] + item + 1)
                if some(item):
                    pool.wait_ge(s["c_zo"], item)
                rstd(MV3, VE3, R3, EPS, s["co_ve"], at["co_ve"] + item + 1).then_inc(s["co_r"], 1)
                mean_rstd(MV3, R3, NM3, s["co_r"], at["co_r"] + item + 1, s["co_mr"], at["co_mr"] + item + 1).then_inc(s["c_or"], 1)
                pool.wait_ge(s["c_zo"], item + 1)
                add_to_x(item, EK[:, :]).then_inc(s["c_x"], 1)

            def mix(n, live):
                if live(3):
                    i = n - 3
                    pool.wait_ge(s["d_ov"], at["d_ov"] + i + 1)
                    if some(i):
                        pool.wait_ge(s["d_zo"], i)
                    rstd(MV2, VE2, R2, EPS, s["do_ve"], at["do_ve"] + i + 1).then_inc(s["do_r"], 1)
                    mean_rstd(MV2, R2, NM2, s["do_r"], i + 1, s["do_mr"], i + 1).then_inc(s["d_os"], 1)
                    pool.wait_ge(s["d_zo"], i + 1)
                    add_to_x(i, MEM[:, :]).then_inc(s["d_out"], 1)
                if live(0):
                    pool.wait_ge(s["d_xv"], at["d_xv"] + n + 1)
                    if some(n):
                        pool.wait_ge(s["d_zn"], n)
                    rstd(MV1, VE1, R1, EPS, s["dx_ve"], at["dx_ve"] + n + 1).then_inc(s["dx_r"], 1)
                    mean_rstd(MV1, R1, NM1, s["dx_r"], at["dx_r"] + n + 1, s["dx_mr"], at["dx_mr"] + n + 1).then_inc(s["d_xs"], 1)

            interleaved(lambda g, k: None, lambda g, i: None, project, mix)

        @block.scalar
        def _(act):
            def copy(o, i):
                return nc.scalar.activation(o, i, ACT.Copy)

            def normalise(o, i, r, nm):
                for j in range(TILES):
                    cols = slice(j * P, (j + 1) * P)
                    last = nc.scalar.activation(o[:, cols], i[:, cols] if not callable(i) else i(j), ACT.Identity,
                                                bias=nm[:, j:j + 1], scale=r[:, j:j + 1])
                return last

            def prepare(l, slot, times, part):
                if part == 0:
                    act.wait_ge(s["wqkv_ps"], l + 1)
                    copy(QKH[slot][:, :], pW[:, 0:2 * P]).then_inc(s["wqk_hi"], 1)
                    copy(WV[slot][:, :], pW[:, 2 * P:3 * P]).then_inc(s["wqkv_out"], 1)
                if part == 1:
                    act.wait_ge(s["w1_ps"], l + 1)
                    copy(W1H[slot][:, :], pW[:, :]).then_inc(s["w1_hi"], 1)
                if part == 2:
                    act.wait_ge(s["bias_ps"], l + 1)
                    copy(BIAS[slot][:, :], pW[:, 0:2 + FB]).then_inc(s["bias_out"], 1)
                if part == 3:
                    act.wait_ge(s["bm_ps"], l + 1)
                    copy(BM[slot][:, :], pW[:, 0:P]).then_inc(s["bm_out"], 1)

            act.wait_ge(s["ssm_in"], SSM_LOADS)
            nc.scalar.activation(LA[:, :], ALOG[:, :], ACT.Exp, scale=-1.0).then_inc(s["la_exp"], 1)
            act.wait_ge(s["e1_arg"], 1)
            nc.scalar.activation(E1[:, :], E1[:, :], ACT.Exp).then_inc(s["e1"], 1)
            for p4 in range(PAIRS // 4):
                act.wait_ge(s["e2_arg"], p4 + 1)
                nc.scalar.activation(E2[:, p4 * 512:(p4 + 1) * 512], E2[:, p4 * 512:(p4 + 1) * 512], ACT.Exp).then_inc(s["e2"], 1)
            for part in range(4):
                prepare(0, 0, 1, part)

            act.wait_ge(s["k_ps"], 1)
            for h in range(2):
                last = copy(KTM[:, :].rearrange("p (q h i) -> p h i q", q=TILES, h=2)[:, h],
                            pH[0][:, :].rearrange("p (i h q) -> p h i q", h=2, q=TILES)[:, h])
            last.then_inc(s["k_out"], 1)

            def scaled(o, b, first, src=XI, r=RSTD):
                for j in range(TILES):
                    last = nc.scalar.activation(o[:, j * P:(j + 1) * P], tile(src, b, j), ACT.Copy,
                                                scale=r[:, first + j:first + j + 1])
                return last

            def step(n, b, slots, following):
                has_n, has_p, has_m = live(n)
                has_next = not isinstance(n, int) or n < ITEMS - 1
                wa, wp, wf = slots
                m = n - 2
                k0 = m * FB

                def ha(f):
                    if not has_m:
                        return
                    act.wait_ge(s["h_ps"], k0 + f + 1)
                    if some(k0 + f - 1):
                        act.wait_ge(s["hl"], k0 + f - 1)
                    nc.scalar.activation(HA[f % 2][:, :], pH[f % 2][:, :], ACT.Identity,
                                         bias=BIAS[wf][:, 2 + f:3 + f]).then_inc(s["ha"], 1)

                def part(i):
                    if following is not None:
                        prepare(*following, i)

                ha(0)
                ha(1)
                if has_n:
                    act.wait_ge(s["xT_ps"], n + 1)
                    copy(XTH[:, :], pXT[:, :])
                    copy(XTF[:, :], pXT[:, :]).then_inc(s["xTf"], 1)
                part(0)
                ha(2)
                part(1)
                if has_n:
                    act.wait_ge(s["q_ps"], n + 1)
                    nc.scalar.activation(QF[:, :], pQ[:, :], ACT.Identity, bias=BIAS[wa][:, 0:1]).then_inc(s["q_fm"], 1)
                    act.wait_ge(s["kmax"], n + 1)
                    nc.scalar.activation(EK[:, :], pK[:, :], ACT.Exp, bias=NKM[:, 0:1], accum_out=KSM[:, 0:1]).then_inc(s["ek"], 1)
                ha(3)
                if has_n:
                    act.wait_ge(s["ekT_ps"], n + 1)
                    copy(EKT[:, :], pXT[:, :]).then_inc(s["ek_tm"], 1)
                part(2)
                if has_p:
                    act.wait_ge(s["ln2_rstd"], n)
                    scaled(XR2, before(b, 1), TILES).then_inc(s["xr2"], 1)
                if has_n:
                    act.wait_ge(s["g_ps"], n + 1)
                    copy(GT[:, :], pK[:, 0:P]).then_inc(s["gt"], 1)
                if has_p:
                    act.wait_ge(s["x2T_ps"], n)
                    copy(X2H[:, :], pX2[:, :]).then_inc(s["x2h"], 1)
                if has_n:
                    act.wait_ge(s["q_sub"], n + 1)
                    nc.scalar.activation(QB[:, :], QB[:, :], ACT.Exp).then_inc(s["q_exp"], 1)
                if has_next:
                    act.wait_ge(s["ln1_rstd"], n + 2)
                    scaled(XR, before(b, -1), 0).then_inc(s["xr"], 1)
                part(3)

            act.wait_ge(s["ln1_rstd"], 1)
            scaled(XR, 0, 0).then_inc(s["xr"], 1)
            layers(act, step)

            act.wait_ge(s["fc_ps"], 1)
            copy(FCH[:, :], pW[:, :]).then_inc(s["fc_hi"], 1)
            act.wait_ge(s["win_ps"], 1)
            copy(WINC[:, :], pW[:, 0:P]).then_inc(s["win_out"], 1)

            def spiking(n, live):
                m = n - 2

                def squared(f):
                    if not live(2):
                        return
                    k = m * FB + f
                    act.wait_ge(s["s_h_ps"], at["s_h_ps"] + k + 1)
                    nc.scalar.activation(HA[f % 2][:, :], pH[f % 2][:, :], ACT.Relu).then_inc(s["s_relu"], 1)
                    act.wait_ge(s["s_relu"], at["s_relu"] + k + 1)
                    if some(k - 1):
                        act.wait_ge(s["s_y_ps"], at["s_y_ps"] + k - 1)
                    nc.scalar.activation(HL[f % 2][:, :], HA[f % 2][:, :], ACT.Square).then_inc(s["s_sq"], 1)

                squared(0)
                squared(1)
                if live(6):
                    i = n - 6
                    act.wait_ge(s["c_rs"], at["c_rs"] + i + 1)
                    if some(i):
                        act.wait_ge(s["c_xT_ps"], at["c_xT_ps"] + i)
                    scaled(QS, i, 0, X, R4).then_inc(s["c_xr"], 1)
                squared(2)
                if live(1):
                    i = n - 1
                    act.wait_ge(s["s_xrs"], at["s_xrs"] + i + 1)
                    if some(i):
                        act.wait_ge(s["s_xT_ps"], at["s_xT_ps"] + i)
                    scaled(XR2, i, 0, X, R2).then_inc(s["s_xr"], 1)
                squared(3)
                if live(1):
                    act.wait_ge(s["s_xT_ps"], at["s_xT_ps"] + n)
                    copy(X2H[:, :], pX2[:, :]).then_inc(s["s_hi"], 1)
                if live(6):
                    i = n - 6
                    act.wait_ge(s["c_xT_ps"], at["c_xT_ps"] + i + 1)
                    if some(i):
                        act.wait_ge(s["c_u_ps"], at["c_u_ps"] + i)
                    copy(XTF[:, :], pXT[:, :]).then_inc(s["c_xT"], 1)
                if live(0):
                    act.wait_ge(s["s_ir"], at["s_ir"] + n + 1)
                    if some(n):
                        act.wait_ge(s["s_x1"], n)
                    normalise(XR[:, :], lambda j: tile(XI, n, j), R1, NM1).then_inc(s["s_zi"], 1)
                if live(2):
                    act.wait_ge(s["s_y_ps"], at["s_y_ps"] + (m + 1) * FB)
                    if some(m):
                        act.wait_ge(s["s_acc"], m * (STEPS - 1))
                    copy(YM[:, :], pY[:, :]).then_inc(s["s_y1"], 1)
                if live(4):
                    i = n - 4
                    act.wait_ge(s["s_cr"], i + 1)
                    if some(i):
                        act.wait_ge(s["s_x2"], i)
                    normalise(EK[:, :], pQ[:, :], R3, NM3).then_inc(s["s_zc"], 1)
                for part, (when, o, width) in enumerate(((3, KRE, SEQ), (9, KIM, SEQ), (10, KRE2, P))):
                    if isinstance(n, int) and n == when:
                        act.wait_ge(s["kf_ps"], part + 1)
                        copy(o[:, :], pW[:, 0:width]).then_inc(s["kf"], 1)

            pipeline(act, 6, spiking)

            def inverse(g, i):
                item = g * GROUP + i
                act.wait_ge(s["c_y_ps"], item + 1)
                if some(item):
                    act.wait_ge(s["c_o_ps"], item)
                copy(XTF[:, :], PS[4 + i % 2][:, :]).then_inc(s["c_yT"], 1)

            def project(item):
                act.wait_ge(s["c_or"], at["c_or"] + item + 1)
                if some(item):
                    act.wait_ge(s["c_x"], item)
                normalise(EK[:, :], EKT[:, :], R3, NM3).then_inc(s["c_zo"], 1)

            def mix(n, live):
                if live(1):
                    i = n - 1
                    act.wait_ge(s["d_xT_ps"], at["d_xT_ps"] + i + 1)
                    if some(i):
                        act.wait_ge(s["d_mix"], i)
                    copy(SH[:, 1:1 + SEQ], pX2[:, :]).then_inc(s["d_xT"], 1)
                if live(2):
                    i = n - 2
                    act.wait_ge(s["d_k_ps"], at["d_k_ps"] + i + 1)
                    nc.scalar.activation(QF[:, :], pK[:, :], ACT.Relu).then_inc(s["d_relu"], 1)
                    act.wait_ge(s["d_relu"], at["d_relu"] + i + 1)
                    if some(i):
                        act.wait_ge(s["d_v_ps"], at["d_v_ps"] + i)
                    nc.scalar.activation(HL[0][:, :], QF[:, :], ACT.Square).then_inc(s["d_sq"], 1)
                    act.wait_ge(s["d_r_ps"], at["d_r_ps"] + i + 1)
                    if some(i):
                        act.wait_ge(s["d_rv"], i)
                    nc.scalar.activation(QB[:, :], pQ[:, :], ACT.Sigmoid).then_inc(s["d_sig"], 1)
                if live(3):
                    i = n - 3
                    act.wait_ge(s["d_os"], at["d_os"] + i + 1)
                    if some(i):
                        act.wait_ge(s["d_out"], i)
                    normalise(MEM[:, :], ACC[:, :], R2, NM2).then_inc(s["d_zo"], 1)
                if live(0):
                    act.wait_ge(s["d_xs"], at["d_xs"] + n + 1)
                    if some(n):
                        act.wait_ge(s["d_xT_ps"], at["d_xT_ps"] + n)
                    normalise(XR2[:, :], lambda j: tile(X, n, j), R1, NM1).then_inc(s["d_zn"], 1)

            interleaved(lambda g, k: None, inverse, project, mix)

        @block.vector
        def _(dve):
            tt, ts, stt = nc.vector.tensor_tensor, nc.vector.tensor_scalar, nc.vector.scalar_tensor_tensor

            def stats(src, st, mv, parted, count):
                for j in range(TILES):
                    last = nc.vector.bn_stats(st[:, j * 6:(j + 1) * 6], src(j))
                last.then_inc(parted, 1)
                dve.wait_ge(parted, count)
                alone(dve, s["dve_passed"], count)
                for j in range(TILES):
                    last = nc.vector.bn_aggr(mv[:, 2 * j:2 * j + 2], st[:, j * 6:(j + 1) * 6])
                return last

            nc.vector.memset(EIGHTH[0:1, :], 1.0 / HEADS).then_inc(s["eighth"], 1)

            def prepare(l, slot, times, part):
                if part == 0:
                    dve.wait_ge(s["w_in"][slot], times * W_LOADS)
                    ts(LNP[0][:, :], CENT[:, :], LNC[slot][:, 0:1], None, ALU.mult)
                    ts(LNP[1][:, :], CENT[:, :], LNC[slot][:, 2:3], None, ALU.mult).then_inc(s["lnp"], 1)
                if part == 1:
                    dve.wait_ge(s["wqk_hi"], l + 1)
                    dve.wait_ge(s["wqkv_out"], 2 * l + 1)
                    tt(QKL[slot][:, :], pW[:, 0:2 * P], QKH[slot][:, :].bitcast(FP32), ALU.subtract).then_inc(s["wqkv_out"], 1)
                if part == 2:
                    dve.wait_ge(s["w1_hi"], l + 1)
                    tt(W1L[slot][:, :], pW[:, :], W1H[slot][:, :].bitcast(FP32), ALU.subtract).then_inc(s["w1_out"], 1)
                if part == 3:
                    dve.wait_ge(s["bias_out"], l + 1)
                    ts(MBV[:, :], HMASK[:, :], BIAS[slot][:, 1:2], None, ALU.mult).then_inc(s["mbv"], 1)
                if part == 4:
                    dve.wait_ge(s["bm_out"], l + 1)
                    dve.sem_inc(s["w_ready"], 1)


            dve.wait_ge(s["ssm_in"], SSM_LOADS)
            dve.wait_ge(s["la_exp"], 1)
            tt(CDB[:, :], BMAT[:, :], DTR[:, :], ALU.mult).then_inc(s["cdb"], 1)
            stt(out=LA[:, :], in0=LA[:, :], scalar=-1.0, in1=DTR[:, :], op0=ALU.mult, op1=ALU.mult).then_inc(s["la"], 1)
            dve.wait_ge(s["cdb"], 1)
            dve.wait_ge(s["la"], 1)
            tt(CDB[:, :], CMAT[:, :], CDB[:, :], ALU.mult).then_inc(s["cdb"], 1)
            for q in range(TILES):
                last = ts(E1[:, :].rearrange("p (i q) -> p i q", q=TILES)[:, :, q], LA[:, :], float(q * P), None, ALU.mult)
            last.then_inc(s["e1_arg"], 1)
            for p4 in range(PAIRS // 4):
                tt(E2[:, p4 * 512:(p4 + 1) * 512].rearrange("p (i r) -> p i r", i=4),
                   LA[:, 4 * p4:4 * p4 + 4].unsqueeze(2).broadcast_to([P, 4, P]),
                   IOTA[:, :].unsqueeze(1).broadcast_to([P, 4, P]), ALU.mult).then_inc(s["e2_arg"], 1)
                if p4 == 0:
                    dve.wait_ge(s["e1"], 1)
                    dve.wait_ge(s["cdb"], 2)
                    dve.wait_ge(s["ce1_zero"], 1)
                    for h in range(2):
                        o = slice(h * STATES, (h + 1) * STATES)
                        last = tt(CE1[o, :].rearrange("p (i h q) -> p h i q", h=2, q=TILES)[:, h],
                                  E1[o, :].rearrange("p (i q) -> p i q", q=TILES),
                                  CDB[o, :].unsqueeze(2).broadcast_to([STATES, PAIRS, TILES]), ALU.mult)
                    last.then_inc(s["ce1"], 1)
            dve.wait_ge(s["c_in"], 3 * 16)
            nc.vector.tensor_copy(IDB[:, :], ID[:, :])
            nc.vector.memset(SH[:, 0:1], 0.0).then_inc(s["sh0"], 1)
            prepare(0, 0, 1, 0)

            dve.wait_ge(s["x_in"], 16 * BATCH)
            for b in range(BATCH + 1):
                if b < BATCH:
                    for j in range(b * TILES, (b + 1) * TILES):
                        last = nc.vector.bn_stats(STX[:, 6 * j:6 * j + 6], X[:, j * P:(j + 1) * P])
                    last.then_inc(s["i_st"], 1)
                if b:
                    dve.wait_ge(s["i_st"], b)
                    for j in range((b - 1) * TILES, b * TILES):
                        last = nc.vector.bn_aggr(MVX[:, 2 * j:2 * j + 2], STX[:, 6 * j:6 * j + 6])
                    last.then_inc(s["i_var"], 1)
            for b in range(BATCH):
                if b % 2 == 0:
                    prepare(0, 0, 1, b // 2 + 1)
                dve.wait_ge(s["i_var"], b + 1)
                dve.wait_ge(s["i_rstd"], b + 1)
                for j in range(b * TILES, (b + 1) * TILES):
                    last = ts(XI[:, j * P:(j + 1) * P], X[:, j * P:(j + 1) * P], MVX[:, 2 * j:2 * j + 1], RX[:, j:j + 1],
                              ALU.subtract, ALU.mult)
                last.then_inc(s["xi_init"], 1)
            dve.wait_ge(s["xi_init"], BATCH)

            def ln_stats(b, first):
                for j in range(TILES):
                    last = nc.vector.bn_stats(STATS[:, first + j, :], tile(XI, b, j))
                return last

            ln_stats(0, 0).then_inc(s["stats_ready"], 1)
            dve.wait_ge(s["k_out"], 1)
            tt(KTM[0:1, 0:P], KTM[0:1, 0:P], DP[0:1, :], ALU.add).then_inc(s["ktm"], 1)

            def step(n, b, slots, following):
                has_n, has_p, has_m = live(n)
                wa, wp, wf = slots
                has_next = not isinstance(n, int) or n < ITEMS - 1
                m = n - 2
                k0 = m * FB

                def hl(f):
                    if not has_m:
                        return
                    dve.wait_ge(s["ha"], k0 + f + 1)
                    if some(k0 + f - 1):
                        dve.wait_ge(s["y_ps"], k0 + f - 1)
                    stt(out=HL[f % 2][:, :], in0=HA[f % 2][:, :], scalar=LEAK, in1=HA[f % 2][:, :],
                        op0=ALU.mult, op1=ALU.max).then_inc(s["hl"], 1)

                def part(i):
                    if following is not None:
                        prepare(*following, i)

                part(0)
                hl(0)
                if has_p:
                    dve.wait_ge(s["q_nrm"], n)
                    nc.vector.transpose(QS[:, :], QB[:, :]).then_inc(s["qs"], 1)
                hl(1)
                if has_next:
                    dve.wait_ge(s["ln1_rstd"], n + 1)
                    alone(dve, s["dve_passed"], n)
                    last = ln_stats(before(b, -1), 0)
                    if not has_p:
                        last.then_inc(s["stats_ready"], 1)
                elif has_p:
                    dve.wait_ge(s["ln1_rstd"], ITEMS)
                    dve.wait_ge(s["ln2_rstd"], n - 1)
                part(1)
                if has_p:
                    dve.wait_ge(s["out_ps"], n)
                    xo = seq(XI, before(b, 1))
                    tt(xo, pQ[:, :], xo, ALU.add).then_inc(s["resid1"], 1)
                    dve.wait_ge(s["resid1"], n)
                    alone(dve, s["dve_passed"], n)
                    ln_stats(before(b, 1), TILES).then_inc(s["stats_ready"], 1)
                if has_n:
                    dve.wait_ge(s["k_ps2"], n + 1)
                    nc.vector.tensor_reduce(NKM[:, 0:1], pK[:, :], AX.X, ALU.max, negate=True).then_inc(s["kmax"], 1)
                hl(2)
                part(2)
                if has_n:
                    dve.wait_ge(s["q_fm"], n + 1)
                    nc.vector.transpose(QB[:, :], QF[:, :]).then_inc(s["q_blk"], 1)
                    dve.wait_ge(s["q_blk"], n + 1)
                    nc.vector.tensor_reduce(QMX[:, :], heads(QB[:, :]), AX.X, ALU.max).then_inc(s["qmax"], 1)
                hl(3)
                if has_n:
                    dve.wait_ge(s["ek"], n + 1)
                    nc.vector.reciprocal(KRC[:, :], KSM[:, :]).then_inc(s["k_rec"], 1)
                part(3)
                if has_p:
                    dve.wait_ge(s["x2h"], n)
                    tt(X2L[:, :], pX2[:, :], X2H[:, :].bitcast(FP32), ALU.subtract).then_inc(s["x2l"], 1)
                if has_n:
                    dve.wait_ge(s["c_ps"], n + 1)
                    tt(CT[:, :], pK[:, P:2 * P], HMASK[:, :], ALU.mult).then_inc(s["ct"], 1)
                    dve.wait_ge(s["q_exp"], n + 1)
                    nc.vector.tensor_reduce(QSM[:, :], heads(QB[:, :]), AX.X, ALU.add).then_inc(s["q_sum"], 1)
                    dve.wait_ge(s["q_sum"], n + 1)
                    nc.vector.reciprocal(QRC[:, :], QSM[:, :]).then_inc(s["q_rec"], 1)
                if has_m:
                    dve.wait_ge(s["y_ps"], k0 + FB)
                    xo = seq(XI, before(b, 2))
                    tt(xo, pY[:, :], xo, ALU.add).then_inc(s["resid2"], 1)
                if has_n:
                    dve.wait_ge(s["m_ps"], n + 1)
                    dve.wait_ge(s["k_rec"], n + 1)
                    stt(out=MM[:, :], in0=pK[:, 2 * P:3 * P], scalar=KRC[:, 0:1], in1=BM[wa][:, :],
                        op0=ALU.mult, op1=ALU.add).then_inc(s["m_ready"], 1)
                part(4)

            layers(dve, step)

            dve.wait_ge(s["resid2"], ITEMS)
            dve.wait_ge(s["fc_hi"], 1)
            tt(FCL[:, :], pW[:, :], FCH[:, :].bitcast(FP32), ALU.subtract).then_inc(s["fc_out"], 1)

            def bn_parts(src, st, half, parted):
                for j in range(2 * half, 2 * half + 2):
                    last = nc.vector.bn_stats(st[:, j * 6:(j + 1) * 6], src(j))
                if half:
                    last.then_inc(parted, 1)

            def bn_join(st, mv):
                for j in range(TILES):
                    last = nc.vector.bn_aggr(mv[:, 2 * j:2 * j + 2], st[:, j * 6:(j + 1) * 6])
                return last

            def spiking(n, live):
                if live(1):
                    i = n - 1
                    dve.wait_ge(s["s_x1"], i + 1)
                    if some(i):
                        dve.wait_ge(s["s_xrs"], at["s_xrs"] + i)
                    alone(dve, s["dve_passed"], i + 1)
                    stats(lambda j: tile(X, i, j), ST2, MV2, s["sxv_st"], at["sxv_st"] + i + 1).then_inc(s["s_xv"], 1)

                def parts(t, half):
                    if t == 0 and live(0):
                        if half == 0 and some(n):
                            dve.wait_ge(s["s_ir"], at["s_ir"] + n)
                            alone(dve, s["dve_passed"], n)
                        return bn_parts(lambda j: tile(XI, n, j), ST1, half, s["siv_st"])
                    if t == 1 and live(4):
                        if half == 0:
                            dve.wait_ge(s["s_cnt"], at["s_cnt"] + n - 3)
                            if some(n - 4):
                                dve.wait_ge(s["s_cr"], n - 4)
                            alone(dve, s["dve_passed"], n - 3)
                        return bn_parts(lambda j: pQ[:, j * P:(j + 1) * P], ST3, half, s["scv_st"])
                    if t == 2 and live(5):
                        if half == 0:
                            dve.wait_ge(s["s_x2"], n - 4)
                            if some(n - 5):
                                dve.wait_ge(s["c_rs"], at["c_rs"] + n - 5)
                            alone(dve, s["dve_passed"], n - 4)
                        return bn_parts(lambda j: tile(X, n - 5, j), ST4, half, s["cxv_st"])

                def joined(t):
                    if t == 1 and live(0):
                        dve.wait_ge(s["siv_st"], at["siv_st"] + n + 1)
                        alone(dve, s["dve_passed"], n + 1)
                        bn_join(ST1, MV1).then_inc(s["s_iv"], 1)
                    if t == 2 and live(4):
                        dve.wait_ge(s["scv_st"], n - 3)
                        alone(dve, s["dve_passed"], n - 3)
                        bn_join(ST3, MV3).then_inc(s["s_cv"], 1)
                    if t == 3 and live(5):
                        dve.wait_ge(s["cxv_st"], at["cxv_st"] + n - 4)
                        alone(dve, s["dve_passed"], n - 4)
                        bn_join(ST4, MV4).then_inc(s["c_xv"], 1)

                i = n - 3
                if live(3):
                    dve.wait_ge(s["s_y1"], i + 1)
                    if some(i):
                        dve.wait_ge(s["s_cnt"], at["s_cnt"] + i)
                mem = YM
                for t in range(STEPS):
                    if live(3):
                        if t:
                            dve.wait_ge(s["s_mem"], i * (STEPS - 1) + t)
                        ts(SPK[t][:, :], mem[:, :], 1.0, None, ALU.is_gt).then_inc(s["s_spk"], 1)
                        if t < STEPS - 1:
                            stt(out=ACC[:, :], in0=mem[:, :], scalar=BETA, in1=YM[:, :], op0=ALU.mult,
                                op1=ALU.add).then_inc(s["s_acc"], 1)
                    joined(t)
                    parts(t, 0)
                    if live(3) and t < STEPS - 1:
                        dve.wait_ge(s["s_spk"], i * STEPS + t + 1)
                        dve.wait_ge(s["s_acc"], i * (STEPS - 1) + t + 1)
                        mem = MEM
                        tt(MEM[:, :], ACC[:, :], SPK[t][:, :], ALU.subtract).then_inc(s["s_mem"], 1)
                    parts(t, 1)
                    if t == 3 and live(1):
                        dve.wait_ge(s["s_hi"], at["s_hi"] + n)
                        tt(X2L[:, :], pX2[:, :], X2H[:, :].bitcast(FP32), ALU.subtract).then_inc(s["s_lo"], 1)
                if live(6):
                    i = n - 6
                    dve.wait_ge(s["c_u_ps"], at["c_u_ps"] + i + 1)
                    tt(tiles(UALL[:, bass.ds(i * SEQ, SEQ)]), tiles(pK[:, :]), BIN[:, :].unsqueeze(1).broadcast_to([P, TILES, P]),
                       ALU.add).then_inc(s["c_u"], 1)

            pipeline(dve, 6, spiking)

            def forward(g, k):
                dve.wait_ge(s["c_f_ps"], at["c_f_ps"] + g * TILES + k + 1)
                if g and k == 0:
                    dve.wait_ge(s["c_y_ps"], g * GROUP)
                if some(g * TILES + k):
                    dve.wait_ge(s["c_yf"], g * TILES + k)
                pr, pi = PS[4 + (k % 2) * 2], PS[5 + (k % 2) * 2]
                kr = KRE[:, k * P:(k + 1) * P].unsqueeze(1).broadcast_to([P, GROUP, P])
                ki = KIM[:, k * P:(k + 1) * P].unsqueeze(1).broadcast_to([P, GROUP, P])
                kr2 = (KRE2[:, :] if k == 0 else KRE[:, k * P:(k + 1) * P]).unsqueeze(1).broadcast_to([P, GROUP, P])
                yr, yi = YF[:, k * SEQ:(k + 1) * SEQ], YF[:, (TILES + k) * SEQ:(TILES + k + 1) * SEQ]
                tt(tiles(HA[0][:, :]), tiles(pi[:, :]), ki, ALU.mult).then_inc(s["c_m"], 1)
                tt(tiles(HA[1][:, :]), tiles(pi[:, :]), kr2, ALU.mult).then_inc(s["c_m"], 1)
                tt(tiles(yr), tiles(pr[:, :]), kr, ALU.mult).then_inc(s["c_m"], 1)
                tt(tiles(yi), tiles(pr[:, :]), ki, ALU.mult).then_inc(s["c_m"], 1)
                dve.wait_ge(s["c_m"], (g * TILES + k) * 4 + 4)
                tt(yr, yr, HA[0][:, :], ALU.subtract)
                tt(yi, yi, HA[1][:, :], ALU.add).then_inc(s["c_yf"], 1)

            def project(item):
                dve.wait_ge(s["c_o_ps"], item + 1)
                if some(item):
                    dve.wait_ge(s["c_zo"], item)
                tt(tiles(EKT[:, :]), tiles(pY[:, :]), BOUT[:, :].unsqueeze(1).broadcast_to([P, TILES, P]), ALU.add).then_inc(s["c_z"], 1)
                dve.wait_ge(s["c_z"], item + 1)
                stats(lambda j: EKT[:, j * P:(j + 1) * P], ST3, MV3, s["cov_st"], at["cov_st"] + item + 1).then_inc(s["c_ov"], 1)

            dve.wait_ge(s["sh0"], 1)

            def mix(n, live):
                if live(1):
                    i = n - 1
                    dve.wait_ge(s["d_xT"], at["d_xT"] + i + 1)
                    tt(YM[:, :], SH[:, 1:1 + SEQ], SH[:, 0:SEQ], ALU.subtract).then_inc(s["d_diff"], 1)
                    dve.wait_ge(s["d_diff"], i + 1)
                    if some(i):
                        dve.wait_ge(s["d_r_ps"], at["d_r_ps"] + i)
                    stt(out=XR[:, :], in0=YM[:, :], scalar=MU[:, 0:1], in1=SH[:, 0:SEQ], op0=ALU.mult, op1=ALU.add)
                    stt(out=QS[:, :], in0=YM[:, :], scalar=MU[:, 1:2], in1=SH[:, 0:SEQ], op0=ALU.mult,
                        op1=ALU.add).then_inc(s["d_mix"], 1)
                if live(2):
                    i = n - 2
                    dve.wait_ge(s["d_sig"], i + 1)
                    dve.wait_ge(s["d_v_ps"], at["d_v_ps"] + i + 1)
                    if some(i):
                        dve.wait_ge(s["d_zo"], i)
                    tt(ACC[:, :], pXT[:, :], QB[:, :], ALU.mult).then_inc(s["d_rv"], 1)
                    dve.wait_ge(s["d_rv"], i + 1)
                    stats(lambda j: ACC[:, j * P:(j + 1) * P], ST2, MV2, s["dov_st"], at["dov_st"] + i + 1).then_inc(s["d_ov"], 1)
                if live(0):
                    dve.wait_ge(s["c_x"], n + 1)
                    if some(n):
                        dve.wait_ge(s["d_xs"], at["d_xs"] + n)
                    stats(lambda j: tile(X, n, j), ST1, MV1, s["dxv_st"], at["dxv_st"] + n + 1).then_inc(s["d_xv"], 1)

            interleaved(forward, lambda g, i: None, project, mix)


_ARGS = ["x", "qkv", "wo", "w1", "w2", "lnc", "bo", "fcT", "proj", "winT", "woutT", "alog", "bmat", "cmat", "dtr", "dp",
         "bins", "bouts", "wrT", "wkT", "wvT", "mu", "ident", "cent", "hmask", "iota", "fwd", "fwdx", "inv"]


def spectrum_matrices():
    n = 2 * SEQ
    t = np.arange(SEQ)
    phase = (np.outer(t, t) % n) * (2 * np.pi / n)
    sign = 1.0 - 2.0 * (t % 2)
    re, im = np.cos(phase), -np.sin(phase)
    packed = im.copy()
    packed[:, 0] = sign
    fwd = np.concatenate([re, packed], axis=1)
    re2 = re[:, 0:P].copy()
    re2[:, 0] = sign
    fwdx = np.concatenate([im[:, 0:P], re2], axis=1)
    inv = fwd.T * (2.0 / n)
    inv[0] /= 2
    inv[SEQ] /= 2
    return fwd.astype(np.float32), fwdx.astype(np.float32), inv.astype(np.float32)


def kernel(**inputs):
    import concourse.bacc as bacc
    from concourse.bass_utils import run_bass_kernel_spmd

    a = {k: np.asarray(v) for k, v in inputs.items()}

    def state_rows(m):
        return m.T.reshape(STATES, 2, PAIRS).transpose(1, 0, 2).reshape(P, PAIRS)

    fwd, fwdx, inv = spectrum_matrices()
    head = np.arange(P) // DH
    lay = {
        "x": a["L0_attn_x"],
        "qkv": np.concatenate([a["L0_attn_wq"], a["L0_attn_wk"], a["L0_attn_wv"]], axis=2),
        "wo": a["L0_attn_wo"],
        "w1": a["L0_attn_w1"],
        "w2": a["L0_attn_w2"],
        "lnc": np.stack([a["L0_attn_ln1_w"], a["L0_attn_ln1_b"], a["L0_attn_ln2_w"], a["L0_attn_ln2_b"]], axis=2),
        "bo": a["L0_attn_bo"],
        "fcT": a["L0_ffn_W_fc"].T,
        "proj": a["L0_ffn_W_proj"].T,
        "winT": a["L1_attn_Win"].T,
        "woutT": a["L1_attn_Wout"].T,
        "alog": state_rows(a["L1_attn_A_log"]),
        "bmat": state_rows(a["L1_attn_B"]),
        "cmat": state_rows(a["L1_attn_C"]),
        "dtr": np.repeat(a["L1_attn_dt"].reshape(2, PAIRS), STATES, axis=0),
        "dp": a["L1_attn_Dp"].reshape(1, P),
        "bins": a["L1_attn_bin_"].reshape(1, P),
        "bouts": a["L1_attn_bout"].reshape(1, P),
        "wrT": a["L1_ffn_W_r"].T,
        "wkT": a["L1_ffn_W_k"].T,
        "wvT": a["L1_ffn_W_v"].T,
        "mu": np.stack([a["L1_ffn_mu_r"], a["L1_ffn_mu_k"]], axis=1),
        "ident": np.eye(P, dtype=np.float32),
        "cent": np.eye(P, dtype=np.float32) - np.float32(1.0 / P),
        "hmask": (head[:, None] == head[None, :]).astype(np.float32),
        "iota": np.ascontiguousarray(np.broadcast_to(np.arange(P, dtype=np.float32), (P, P))),
        "fwd": fwd, "fwdx": fwdx, "inv": inv,
    }
    nc = bacc.Bacc("TRN2", target_bir_lowering=False, num_devices=1)
    arrays, args = {}, []
    for name in _ARGS:
        v = np.ascontiguousarray(lay[name])
        arrays[f"in_{name}"] = v
        args.append(nc.dram_tensor(f"in_{name}", v.shape, mybir.dt.from_np(v.dtype), kind="ExternalInput").ap())
    args.append(nc.dram_tensor("out_0", (BATCH, SEQ, P), FP32, kind="ExternalOutput").ap())
    build(nc, *args)
    r = run_bass_kernel_spmd(nc, [arrays], core_ids=[0])
    return r.results[0]["out_0"]
```

```python
import numpy as np
import concourse.bass as bass
from concourse import mybir
from contextlib import ExitStack

FP32 = mybir.dt.float32
F32R = mybir.dt.float32r
BF16 = mybir.dt.bfloat16
ALU = mybir.AluOpType
ACT = mybir.ActivationFunctionType
AX = mybir.AxisListType

P = 128
BATCH = 8
SEQ = 512
TILES = SEQ // P
LAYERS = 6
HEADS = 8
DH = P // HEADS
FB = 4
STATES = 64
BINS = 2 * SEQ // P
GROUP = 4
PAIRS = P // 2
EPS = 1e-5
LEAK = 0.01
BETA = 0.9
STEPS = 5
ITEMS = LAYERS * BATCH


def some(value):
    return not isinstance(value, int) or value > 0


def alone(eng, passed, value):
    if not isinstance(value, int):
        eng.sem_inc(passed, 1)


SHARED = [
    [("siv_st", 8), ("dxv_st", 8)],
    [("sxv_st", 8), ("cov_st", 8)],
    [("cxv_st", 8), ("dov_st", 8)],
    [("i_var", 8), ("s_iv", 8), ("d_xv", 8)],
    [("s_xv", 8), ("c_ov", 8)],
    [("c_xv", 8), ("d_ov", 8)],
    [("i_ve", 8), ("si_ve", 8), ("dx_ve", 8)],
    [("sx_ve", 8), ("co_ve", 8)],
    [("cx_ve", 8), ("do_ve", 8)],
    [("i_rstd", 8), ("s_ir", 8), ("d_xs", 8)],
    [("s_xrs", 8), ("c_or", 8)],
    [("c_rs", 8), ("d_os", 8)],
    [("si_r", 8), ("dx_r", 8)],
    [("si_mr", 8), ("dx_mr", 8)],
    [("sc_r", 8), ("co_r", 8)],
    [("sc_mr", 8), ("co_mr", 8)],
    [("x2T_ps", 48), ("s_xT_ps", 8), ("d_xT_ps", 8)],
    [("xT_ps", 48), ("c_xT_ps", 8)],
    [("k_ps2", 48), ("c_f_ps", 8)],
    [("g_ps", 48), ("d_k_ps", 8)],
    [("q_ps", 48), ("s_cnt", 8), ("d_r_ps", 8)],
    [("out_ps", 48), ("d_v_ps", 8)],
    [("m_ps", 48), ("c_u_ps", 8)],
    [("y_ps", 192), ("s_y_ps", 32)],
    [("h_ps", 192), ("s_h_ps", 32)],
    [("ha", 192), ("s_relu", 32), ("d_relu", 8)],
    [("q_fm", 48), ("s_sq", 32), ("d_sq", 8)],
    [("x2h", 48), ("s_hi", 8), ("d_xT", 8)],
    [("xTf", 48), ("c_xT", 8)],
    [("q_exp", 48), ("c_xr", 8)],
]


def seq(t, b):
    return t[:, bass.ds(b * SEQ, SEQ)]


def tile(t, b, j):
    return t[:, bass.ds(b * SEQ + j * P, P)]


def per_tile(col):
    return col.unsqueeze(2).broadcast_to([P, TILES, P])


def tiles(ap):
    return ap.rearrange("p (j c) -> p j c", c=P)


def heads(ap):
    return ap.rearrange("p (a d) -> p a d", d=DH)


def pipeline(eng, lag, step):
    for n in range(lag):
        step(n, lambda k, n=n: n - k >= 0)
    with eng.Fori(lag, BATCH) as n:
        step(n, lambda k: True)
    for n in range(BATCH, BATCH + lag):
        step(n, lambda k, n=n: n - k < BATCH)


def layers(eng, step):

    def layer(first, slot, following):
        step(first, 0, (slot, 1 - slot, 1 - slot), None)
        step(first + 1, 1, (slot, slot, 1 - slot), None)
        start = 2
        if isinstance(first, int) and first == 0:
            step(2, 2, (slot, slot, slot), None)
            start = 3
        with eng.Fori(start, BATCH - 2) as b:
            step(first + b, b, (slot, slot, slot), None)
        step(first + BATCH - 2, BATCH - 2, (slot, slot, slot), None)
        step(first + BATCH - 1, BATCH - 1, (slot, slot, slot), following)

    layer(0, 0, (1, 1, 1))
    with eng.Fori(0, (LAYERS - 2) // 2) as r:
        layer(r * (2 * BATCH) + BATCH, 1, (r * 2 + 2, 0, r + 2))
        layer(r * (2 * BATCH) + 2 * BATCH, 0, (r * 2 + 3, 1, r + 2))
    last = (LAYERS - 1) % 2
    layer((LAYERS - 1) * BATCH, last, None)
    for extra in range(2):
        step(ITEMS + extra, extra, (last, last, last), None)


def live(n):
    if not isinstance(n, int):
        return True, True, True
    return n < ITEMS, 1 <= n <= ITEMS, 2 <= n <= ITEMS + 1


INVERSE, PROJECT, NORM, LN, TURN, MIX, GATE, FINISH = range(8)
STARTS = [0, 1, 2, 3, None, None, 4, 5, 6, 7]


def slots(slot):
    for t in range(len(STARTS) + FINISH):
        item = [STARTS[t - k] if 0 <= t - k < len(STARTS) else None for k in range(FINISH + 1)]
        slot(item, *{GROUP: ((0,), (1,)), GROUP + 1: ((2, 3), ())}.get(t, ((), ())))


def before(b, k):
    return (b - k) % BATCH if isinstance(b, int) else b - k


def build(nc, x, qkv, wo, w1, w2, lnc, bo, fcT, proj, winT, woutT, alog, bmat, cmat, dtr, dp, bins_,
          bouts, wrT, wkT, wvT, mu, ident, cent, hmask, iota, fwd, fwdx, inv, out):
    ctx = ExitStack()
    with ctx:
        def sb(name, shape, dt=FP32):
            return ctx.enter_context(nc.sbuf_tensor(name, [P, *shape] if len(shape) == 1 else shape, dt))

        def sem(name):
            return ctx.enter_context(nc.semaphore(name))

        X = sb("X", [BATCH * SEQ])
        XI = sb("XI", [BATCH * SEQ])
        ID = sb("ID", [P])
        CENT = sb("CENT", [P])
        HMASK = sb("HMASK", [P])
        IOTA = sb("IOTA", [P])
        EIGHTH = sb("EIGHTH", [1, P])
        MHALF = sb("MHALF", [2 * TILES])
        IDB = sb("IDB", [P], BF16)
        QKV = [sb(f"QKV{s}", [3 * P]) for s in range(2)]
        WO = [sb(f"WO{s}", [P]) for s in range(2)]
        W1 = [sb(f"W1{s}", [FB * P]) for s in range(2)]
        W2 = [sb(f"W2{s}", [FB * P]) for s in range(2)]
        LNC = [sb(f"LNC{s}", [4]) for s in range(2)]
        BO = [sb(f"BO{s}", [1, P]) for s in range(2)]
        QKH = [sb(f"QKH{s}", [2 * P], F32R) for s in range(2)]
        QKL = [sb(f"QKL{s}", [2 * P], F32R) for s in range(2)]
        WV = [sb(f"WV{s}", [P]) for s in range(2)]
        W1H = [sb(f"W1H{s}", [FB * P], F32R) for s in range(2)]
        W1L = [sb(f"W1L{s}", [FB * P], F32R) for s in range(2)]
        BIAS = [sb(f"BIAS{s}", [2 + FB]) for s in range(2)]
        BM = [sb(f"BM{s}", [P]) for s in range(2)]
        LNP = [sb(f"LNP{i}", [P]) for i in range(2)]
        MBV = sb("MBV", [P])
        STATS, JOIN, RSTD = sb("STATS", [P, 2 * TILES, 6]), sb("JOIN", [P, 5, 2 * TILES]), sb("RSTD", [2 * TILES])
        ST1, MV1, VE1, R1 = sb("ST1", [24]), sb("MV1", [8]), sb("VE1", [4]), sb("R1", [4])
        ST2, MV2, VE2, R2 = sb("ST2", [24]), sb("MV2", [8]), sb("VE2", [4]), sb("R2", [4])
        XR = sb("XR", [SEQ])
        XTF = sb("XTF", [SEQ])
        XTH, XTL = sb("XTH", [SEQ], F32R), sb("XTL", [SEQ], F32R)
        QF, QB = sb("QF", [SEQ]), sb("QB", [SEQ])
        QMX, QSM, QRC = sb("QMX", [32]), sb("QSM", [32]), sb("QRC", [32])
        QS = sb("QS", [SEQ])
        NKM, KSM, KRC = sb("NKM", [1]), sb("KSM", [1]), sb("KRC", [1])
        EK, EKT = sb("EK", [SEQ]), sb("EKT", [SEQ])
        GT, CT, MM = sb("GT", [P]), sb("CT", [P]), sb("MM", [P])
        NM1, ST3, MV3, VE3, R3, NM3 = sb("NM1", [4]), sb("ST3", [24]), sb("MV3", [8]), sb("VE3", [4]), sb("R3", [4]), sb("NM3", [4])
        ST4, MV4, VE4, R4, NM2 = sb("ST4", [24]), sb("MV4", [8]), sb("VE4", [4]), sb("R4", [4]), sb("NM2", [4])
        STX, MVX = sb("STX", [BATCH * TILES * 6]), sb("MVX", [BATCH * TILES * 2])
        VEX, RX = sb("VEX", [BATCH * TILES]), sb("RX", [BATCH * TILES])
        XR2 = sb("XR2", [SEQ])
        X2H, X2L = sb("X2H", [SEQ], F32R), sb("X2L", [SEQ], F32R)
        HA = [sb(f"HA{i}", [SEQ]) for i in range(2)]
        HL = [sb(f"HL{i}", [SEQ]) for i in range(2)]
        FCT = sb("FCT", [FB * P])
        FCH, FCL = sb("FCH", [FB * P], F32R), sb("FCL", [FB * P], F32R)
        PROJ = sb("PROJ", [FB * P])
        SPK = [sb(f"SPK{i}", [SEQ], BF16) for i in range(STEPS)]
        YM, ACC, MEM = sb("YM", [SEQ]), sb("ACC", [SEQ]), sb("MEM", [SEQ])
        SH = sb("SH", [1 + SEQ])
        FWD = sb("FWD", [2 * BINS * P])
        FWDX = sb("FWDX", [2 * 2 * P])
        INV = sb("INV", [BINS * 2 * P])
        BIG = sb("BIG", [PAIRS * P])
        E2 = BIG
        V = BIG
        YF = XI
        YAC, YBD, YE, YG = (sb(n, [2 * P]) for n in ("YAC", "YBD", "YE", "YG"))
        YBC, YR, YS = sb("YBC", [2 * P]), sb("YR", [2 * P]), sb("YS", [2 * P])
        U, FLY, KV = sb("U", [SEQ]), sb("FLY", [6 * P]), sb("KV", [BINS * P])
        ALOG, BMAT, CMAT, DTR = (sb(n, [PAIRS]) for n in ("ALOG", "BMAT", "CMAT", "DTR"))
        LA, CDB = sb("LA", [PAIRS]), sb("CDB", [PAIRS])
        E1 = sb("E1", [PAIRS * TILES])
        CE1 = sb("CE1", [PAIRS * 2 * TILES])
        DP = sb("DP", [1, P])
        KTM = sb("KTM", [TILES * P])
        KRE, KIM, KRE2 = sb("KRE", [TILES * P]), sb("KIM", [TILES * P]), sb("KRE2", [P])
        WINT, WOUTT, BIN, BOUT = (sb(n, [P]) for n in ("WINT", "WOUTT", "BIN", "BOUT"))
        WINC = sb("WINC", [P])
        WRT, WKT, WVT, MU = sb("WRT", [P]), sb("WKT", [P]), sb("WVT", [P]), sb("MU", [2])

        PS = [ctx.enter_context(nc.psum_tensor(f"PS{i}", [P, SEQ], FP32)) for i in range(8)]
        pXT, pQ, pK, pX2, pH, pY, pW = PS[0], PS[1], PS[2], PS[3], PS[4:6], PS[6], PS[7]

        signals = {name: sem(name) for name in (
            "bias_out bias_ps bm_out c_second c_rot c_halves fly_pair fly_root k_skip c_ub bm_ps c_in c_m c_o_ps c_ps c_u c_x c_yT c_y_ps c_yf c_z c_zo cdb ce1 "
            "ce1_zero ct d_diff d_mix d_out d_rv d_sig d_zn d_zo do_mr do_r dve_passed e1 e1_arg e2 e2_arg "
            "eighth ek ekT_ps ek_tm fc_hi fc_out fc_ps gt hl i_st k_out k_ps k_rec kf kf_ps kmax ktm la "
            "la_exp late_in ln1_rstd ln2_rstd ln_part lnp m_ready mbv p_const pool_passed q_blk q_nrm q_rec "
            "q_sub q_sum qmax qs resid1 resid2 s_acc s_cr s_cv s_lo s_mem s_spk s_x1 s_x2 s_xr s_y1 s_zc "
            "s_zi sc_ve scv_st sh0 sp_passed ssm_in stats_ready stored w1_hi w1_out w1_ps w_ready win_out "
            "win_ps wqk_hi wqkv_out wqkv_ps x2 x2l xTl x_in xi_init xr xr2 ").split()}
        starts = {}
        for row in SHARED:
            first, total = sem(row[0][0]), 0
            for name, counts in row:
                signals[name], starts[name] = first, total
                total += counts
        s = {"w_in": [sem("w_in0"), sem("w_in1")], **signals}
        at = starts

        block = ctx.enter_context(nc.Block())

        @block.sync
        def _(sp):
            def load(l, slot):
                sp.dma_start(QKV[slot][:, :], qkv[bass.ds(l, 1)].rearrange("a p n -> (a p) n")).then_inc(s["w_in"][slot], 16)
                sp.dma_start(LNC[slot][:, :], lnc[bass.ds(l, 1)].rearrange("a p n -> (a p) n")).then_inc(s["w_in"][slot], 16)
                sp.dma_start(W1[slot][:, :], w1[bass.ds(l, 1)].rearrange("a p n -> (a p) n")).then_inc(s["w_in"][slot], 16)
                sp.dma_start(WO[slot][:, :], wo[bass.ds(l, 1)].rearrange("a p n -> (a p) n")).then_inc(s["w_in"][slot], 16)
                sp.dma_start(tiles(W2[slot][:, :]),
                             w2[bass.ds(l, 1)].rearrange("a (f p) n -> (a p) f n", p=P)).then_inc(s["w_in"][slot], 16)
                sp.dma_start(BO[slot][:, :], bo[bass.ds(l, 1)]).then_inc(s["w_in"][slot], 16)

            for t, d in ((ALOG, alog), (DTR, dtr), (IOTA, iota), (BMAT, bmat), (CMAT, cmat), (DP, dp)):
                sp.dma_start(t[:, :], d).then_inc(s["ssm_in"], 16)
            sp.dma_start(CENT[:, :], cent).then_inc(s["c_in"], 16)
            sp.dma_start(ID[:, :], ident).then_inc(s["c_in"], 16)
            sp.dma_start(HMASK[:, :], hmask).then_inc(s["c_in"], 16)
            load(0, 0)
            for b in range(BATCH):
                sp.dma_start(tiles(X[:, b * SEQ:(b + 1) * SEQ]),
                             x[b].rearrange("(j p) c -> p j c", p=P)).then_inc(s["x_in"], 16)
            load(1, 1)
            sp.dma_start(FWD[:, :].rearrange("p (j f) -> p j f", j=2), fwd.rearrange("j p f -> p j f")).then_inc(s["late_in"], 16)
            sp.dma_start(FWDX[:, :].rearrange("p (j f) -> p j f", j=2), fwdx.rearrange("j p f -> p j f")).then_inc(s["late_in"], 16)
            sp.dma_start(INV[:, :].rearrange("p (k t) -> p k t", k=BINS), inv.rearrange("(k p) t -> p k t", p=P)).then_inc(s["late_in"], 16)
            sp.dma_start(FCT[:, :], fcT).then_inc(s["late_in"], 16)
            sp.dma_start(tiles(PROJ[:, :]), proj.rearrange("(f p) n -> p f n", p=P)).then_inc(s["late_in"], 16)
            for t, d in ((WINT, winT), (WOUTT, woutT), (WRT, wrT), (WKT, wkT), (WVT, wvT), (MU, mu)):
                sp.dma_start(t[:, :], d).then_inc(s["late_in"], 16)
            sp.dma_start(BIN[:, :], bins_.broadcast_to([P, P])).then_inc(s["late_in"], 16)
            sp.dma_start(BOUT[:, :], bouts.broadcast_to([P, P])).then_inc(s["late_in"], 16)

            with sp.Fori(0, (LAYERS - 2) // 2) as r:
                sp.wait_ge(s["resid2"], r * (2 * BATCH) + BATCH)
                alone(sp, s["sp_passed"], r * (2 * BATCH) + BATCH)
                sp.wait_ge(s["w_ready"], r * 2 + 2)
                alone(sp, s["sp_passed"], r * 2 + 2)
                load(r * 2 + 2, 0)
                sp.wait_ge(s["resid2"], r * (2 * BATCH) + 2 * BATCH)
                alone(sp, s["sp_passed"], r * (2 * BATCH) + 2 * BATCH)
                sp.wait_ge(s["w_ready"], r * 2 + 3)
                alone(sp, s["sp_passed"], r * 2 + 3)
                load(r * 2 + 3, 1)

            with sp.Fori(0, BATCH) as b:
                sp.wait_ge(s["d_out"], b + 1)
                alone(sp, s["sp_passed"], b + 1)
                sp.dma_start(out[bass.ds(b, 1)].rearrange("a (j p) c -> (a p) j c", p=P), tiles(seq(X, b))).then_inc(s["stored"], 16)
            sp.wait_ge(s["stored"], 16 * BATCH)

        W_LOADS = 6 * 16
        SSM_LOADS = 6 * 16
        LATE_LOADS = 13 * 16

        @block.tensor
        def _(pe):
            def mm(o, l, r, start=True, stop=True):
                return nc.tensor.matmul(o, l, r, start=start, stop=stop, skip_group_check=True)

            def split3(o, lh, ll, rh, rl):
                mm(o, ll, rh, True, False)
                mm(o, lh, rl, False, False)
                return mm(o, lh, rh, False, True)

            def transposes(o, i, first=0, end=TILES):
                for j in range(first, end):
                    last = nc.tensor.transpose(o[:, j * P:(j + 1) * P], i[:, j * P:(j + 1) * P], ID[:, :])
                return last

            def prepare(l, slot, times, part):
                if part == 0:
                    pe.wait_ge(s["w_in"][slot], times * W_LOADS)
                    pe.wait_ge(s["lnp"], l + 1)
                    if some(l):
                        pe.wait_ge(s["bm_out"], l)
                    mm(pW[:, 0:3 * P], LNP[0][:, :], QKV[slot][:, :]).then_inc(s["wqkv_ps"], 1)
                if part == 1:
                    pe.wait_ge(s["wqkv_out"], 2 * (l + 1))
                    mm(pW[:, :], LNP[1][:, :], W1[slot][:, :]).then_inc(s["w1_ps"], 1)
                if part == 2:
                    pe.wait_ge(s["w1_out"], l + 1)
                    mm(pW[:, 0:1], QKV[slot][:, 0:P], LNC[slot][:, 1:2])
                    mm(pW[:, 1:2], QKV[slot][:, 2 * P:3 * P], LNC[slot][:, 1:2])
                    for f in range(FB):
                        last = mm(pW[:, 2 + f:3 + f], W1[slot][:, f * P:(f + 1) * P], LNC[slot][:, 3:4])
                    last.then_inc(s["bias_ps"], 1)
                if part == 3:
                    pe.wait_ge(s["mbv"], l + 1)
                    mm(pW[:, 0:P], MBV[:, :], WO[slot][:, :], True, False)
                    mm(pW[:, 0:P], EIGHTH[0:1, :], BO[slot][0:1, :], False, True).then_inc(s["bm_ps"], 1)

            pe.wait_ge(s["c_in"], 3 * 16)
            pe.wait_ge(s["eighth"], 1)
            def kernel_part(first, end):
                for i in range(first, end):
                    last = mm(pW[:, i * 8:i * 8 + 8], E2[:, i * P:(i + 1) * P], CE1[:, i * 8:i * 8 + 8])
                if end == PAIRS:
                    last.then_inc(s["k_ps"], 1)

            for part in range(4):
                prepare(0, 0, 1, part)
            pe.wait_ge(s["bm_out"], 1)
            pe.wait_ge(s["ce1"], 1)
            pe.wait_ge(s["e2"], PAIRS // 4)

            def step(n, b, slots, following):
                has_n, has_p, has_m = live(n)
                wa, wp, wf = slots
                m = n - 2

                def h(item, f, w, there):
                    if not there:
                        return
                    if f == 0:
                        pe.wait_ge(s["x2l"], item + 1)
                    k = item * FB + f
                    if some(k - 1):
                        pe.wait_ge(s["ha"], k - 1)
                    o = slice(f * P, (f + 1) * P)
                    split3(pH[f % 2][:, :], W1H[w][:, o], W1L[w][:, o], X2H[:, :], X2L[:, :]).then_inc(s["h_ps"], 1)

                def y(item, f):
                    if not has_m:
                        return
                    pe.wait_ge(s["hl"], item * FB + f + 1)
                    if f == 0:
                        if some(item):
                            pe.wait_ge(s["resid2"], item)
                    for j in range(TILES):
                        last = mm(pY[:, j * P:(j + 1) * P], HL[f % 2][:, j * P:(j + 1) * P],
                                  W2[wf][:, f * P:(f + 1) * P], f == 0 and j == 0, f == FB - 1)
                    last.then_inc(s["y_ps"], 1)

                def part(i):
                    if following is not None:
                        prepare(*following, i)

                if has_n:
                    pe.wait_ge(s["xr"], n + 1)
                    if some(n):
                        pe.wait_ge(s["ek_tm"], n)
                    transposes(pXT, XR).then_inc(s["xT_ps"], 1)
                part(0)
                if isinstance(n, int) and n == 0:
                    kernel_part(0, 8)
                if isinstance(n, int) and n == 1:
                    kernel_part(40, 48)
                h(m, 2, wf, has_m)
                y(m, 0)
                if has_p:
                    pe.wait_ge(s["m_ready"], n)
                    pe.wait_ge(s["qs"], n)
                    pe.wait_ge(s["q_fm"], n)
                    for j in range(TILES):
                        last = mm(pQ[:, j * P:(j + 1) * P], QS[:, j * P:(j + 1) * P], MM[:, :])
                    last.then_inc(s["out_ps"], 1)
                part(1)
                if has_n:
                    pe.wait_ge(s["xTl"], n + 1)
                    split3(pK[:, :], QKH[wa][:, P:2 * P], QKL[wa][:, P:2 * P], XTH[:, :], XTL[:, :]).then_inc(s["k_ps2"], 1)
                    if some(n):
                        pe.wait_ge(s["resid1"], n)
                    split3(pQ[:, :], QKH[wa][:, 0:P], QKL[wa][:, 0:P], XTH[:, :], XTL[:, :]).then_inc(s["q_ps"], 1)
                if isinstance(n, int) and n == 0:
                    kernel_part(8, 16)
                if isinstance(n, int) and n == 1:
                    kernel_part(48, 56)
                y(m, 1)
                h(m, 3, wf, has_m)
                part(2)
                if has_n:
                    pe.wait_ge(s["ek"], n + 1)
                    transposes(pXT, EK).then_inc(s["ekT_ps"], 1)
                if isinstance(n, int) and n == 0:
                    kernel_part(16, 24)
                if isinstance(n, int) and n == 1:
                    kernel_part(56, 64)
                y(m, 2)
                if has_n:
                    pe.wait_ge(s["ek_tm"], n + 1)
                    for j in range(TILES):
                        last = mm(pK[:, 0:P], XR[:, j * P:(j + 1) * P], EKT[:, j * P:(j + 1) * P], j == 0, j == TILES - 1)
                    last.then_inc(s["g_ps"], 1)
                if has_p:
                    pe.wait_ge(s["xr2"], 2 * n - 1)
                    transposes(pX2, XR2, 0, 2)
                    pe.wait_ge(s["xr2"], 2 * n)
                    transposes(pX2, XR2, 2, 4).then_inc(s["x2T_ps"], 1)
                y(m, 3)
                part(3)
                if has_n:
                    pe.wait_ge(s["gt"], n + 1)
                    mm(pK[:, P:2 * P], WV[wa][:, :], GT[:, :]).then_inc(s["c_ps"], 1)
                h(m + 1, 0, wp, has_p)
                if has_n:
                    pe.wait_ge(s["ct"], n + 1)
                    mm(pK[:, 2 * P:3 * P], CT[:, :], WO[wa][:, :]).then_inc(s["m_ps"], 1)
                h(m + 1, 1, wp, has_p)
                if isinstance(n, int) and n == 0:
                    kernel_part(24, 40)

            layers(pe, step)

            pe.wait_ge(s["late_in"], LATE_LOADS)
            pe.wait_ge(s["bm_out"], LAYERS)
            mm(pW[:, :], CENT[:, :], FCT[:, :]).then_inc(s["fc_ps"], 1)
            pe.wait_ge(s["fc_out"], 1)
            mm(pW[:, 0:P], CENT[:, :], WINT[:, :]).then_inc(s["win_ps"], 1)
            pe.wait_ge(s["win_out"], 1)

            def spectrum(unit):
                part, k = divmod(unit, TILES)
                if unit == 0:
                    pe.wait_ge(s["ktm"], 1)
                elif k == 0:
                    pe.wait_ge(s["kf"], part)
                for j in range(2):
                    lhs = FWD[:, j * BINS * P + (part % 2) * SEQ + k * P:][:, 0:P]
                    if part == 1 and k == 0:
                        lhs = FWDX[:, j * 2 * P:j * 2 * P + P]
                    if part == 2:
                        lhs = FWDX[:, j * 2 * P + P:(j + 1) * 2 * P]
                    last = mm(pW[:, k * P:(k + 1) * P], lhs, KV[:, (2 * k + j) * P:(2 * k + j + 1) * P], j == 0, j == 1)
                if k == TILES - 1 or part == 2:
                    last.then_inc(s["kf_ps"], 1)

            def spiking(n, live):
                m = n - 2

                def hidden(f):
                    if not live(2):
                        return
                    if f == 0:
                        pe.wait_ge(s["s_lo"], m + 1)
                    k = m * FB + f
                    if some(k - 1):
                        pe.wait_ge(s["s_relu"], at["s_relu"] + k - 1)
                    o = slice(f * P, (f + 1) * P)
                    split3(pH[f % 2][:, :], FCH[:, o], FCL[:, o], X2H[:, :], X2L[:, :]).then_inc(s["s_h_ps"], 1)

                def projected(f):
                    if live(2):
                        proj_block(m, f)

                hidden(0)
                hidden(1)
                projected(0)
                hidden(2)
                projected(1)
                hidden(3)
                if live(6):
                    i = n - 6
                    pe.wait_ge(s["c_xr"], at["c_xr"] + i + 1)
                    if some(i):
                        pe.wait_ge(s["c_xT"], at["c_xT"] + i)
                    transposes(pXT, QS).then_inc(s["c_xT_ps"], 1)
                projected(2)
                if live(1):
                    pe.wait_ge(s["s_xr"], n)
                    transposes(pX2, XR2).then_inc(s["s_xT_ps"], 1)
                if isinstance(n, int) and n <= 5:
                    spectrum(n)
                if isinstance(n, int) and 8 <= n <= 10:
                    spectrum(n - 2)
                projected(3)
                if live(6):
                    pe.wait_ge(s["c_xT"], at["c_xT"] + i + 1)
                    if some(i):
                        pe.wait_ge(s["c_u"], i)
                    for j in range(TILES):
                        last = mm(pK[:, j * P:(j + 1) * P], XTF[:, j * P:(j + 1) * P], WINC[:, :])
                    last.then_inc(s["c_u_ps"], 1)
                if live(3):
                    i = n - 3
                    if some(i):
                        pe.wait_ge(s["s_zc"], i)
                    for t in range(STEPS):
                        pe.wait_ge(s["s_spk"], i * STEPS + t + 1)
                        last = mm(pQ[:, :], IDB[:, :], SPK[t][:, :], t == 0, t == STEPS - 1)
                    last.then_inc(s["s_cnt"], 1)

            def proj_block(i, f):
                pe.wait_ge(s["s_sq"], at["s_sq"] + i * FB + f + 1)
                if f == 0:
                    if some(i):
                        pe.wait_ge(s["s_y1"], i)
                for j in range(TILES):
                    last = mm(pY[:, j * P:(j + 1) * P], HL[f % 2][:, j * P:(j + 1) * P],
                              PROJ[:, f * P:(f + 1) * P], f == 0 and j == 0, f == FB - 1)
                last.then_inc(s["s_y_ps"], 1)

            pipeline(pe, 6, spiking)

            def out_proj(item):
                pe.wait_ge(s["c_yT"], item + 1)
                if some(item):
                    pe.wait_ge(s["c_z"], item)
                for j in range(TILES):
                    last = mm(pY[:, j * P:(j + 1) * P], XTF[:, j * P:(j + 1) * P], WOUTT[:, :])
                last.then_inc(s["c_o_ps"], 1)

            pe.wait_ge(s["kf"], 3)
            pe.wait_ge(s["s_y1"], BATCH)
            pe.wait_ge(s["s_relu"], at["s_relu"] + BATCH * FB)

            def forward(g, k):
                if k == 0:
                    pe.wait_ge(s["c_u"], (g + 1) * GROUP)
                if g and k == 0:
                    pe.wait_ge(s["c_yT"], g * GROUP)
                if g and k == 1:
                    pe.wait_ge(s["c_z"], g * GROUP)
                if k >= 2:
                    pe.wait_ge(s["c_yf"], g * TILES + k - 1)
                for half in range(2):
                    bank = PS[4 + (k % 2) * 2 + half]
                    for j in range(2):
                        lhs = FWD[:, j * BINS * P + half * SEQ + k * P:][:, 0:P]
                        first = (2 * k + j) * BATCH * P + g * GROUP * P
                        last = mm(bank[:, :], lhs, V[:, first:first + GROUP * P], j == 0, j == 1)
                last.then_inc(s["c_f_ps"], 1)

            def inverse(item):
                g, i = divmod(item, GROUP)
                if i == 0:
                    pe.wait_ge(s["c_yf"], (g + 1) * TILES)
                if item >= 2:
                    pe.wait_ge(s["c_yT"], item - 1)
                for block in (0, 2, 1, 3):
                    if block == 1 and item:
                        pe.wait_ge(s["c_rot"], item)
                    bank = PS[(4, 7)[i % 2]] if block % 2 == 0 else PS[5]
                    o = bank[:, (block // 2) * 2 * P:(block // 2 + 1) * 2 * P]
                    for part in range(2):
                        k = part * TILES + block
                        last = mm(o, YF[:, k * SEQ + i * P:k * SEQ + (i + 1) * P],
                                  INV[:, k * 2 * P:(k + 1) * 2 * P], part == 0, part == 1)
                last.then_inc(s["c_y_ps"], 1)

            for k in range(TILES):
                forward(0, k)

            def slot(item, early, late):
                if item[INVERSE] is not None:
                    inverse(item[INVERSE])
                if item[PROJECT] is not None:
                    out_proj(item[PROJECT])
                for k in early:
                    forward(1, k)
                if item[TURN] is not None:
                    i = item[TURN]
                    pe.wait_ge(s["d_zn"], i + 1)
                    if some(i):
                        pe.wait_ge(s["d_xT"], at["d_xT"] + i)
                    transposes(pX2, XR2).then_inc(s["d_xT_ps"], 1)
                if item[MIX] is not None:
                    i = item[MIX]
                    pe.wait_ge(s["d_mix"], i + 1)
                    if some(i):
                        pe.wait_ge(s["d_relu"], at["d_relu"] + i)
                    mm(pK[:, :], WKT[:, :], QS[:, :]).then_inc(s["d_k_ps"], 1)
                    if some(i):
                        pe.wait_ge(s["d_sig"], i)
                    for j in range(TILES):
                        last = mm(pQ[:, j * P:(j + 1) * P], XR[:, j * P:(j + 1) * P], WRT[:, :])
                    last.then_inc(s["d_r_ps"], 1)
                    pe.wait_ge(s["d_sq"], at["d_sq"] + i + 1)
                    if some(i):
                        pe.wait_ge(s["d_rv"], i)
                    for j in range(TILES):
                        last = mm(pXT[:, j * P:(j + 1) * P], HL[0][:, j * P:(j + 1) * P], WVT[:, :])
                    last.then_inc(s["d_v_ps"], 1)
                for k in late:
                    forward(1, k)

            slots(slot)

        @block.gpsimd
        def _(pool):
            pool.memset(MHALF[:, :], -0.5).then_inc(s["p_const"], 1)
            pool.memset(CE1[:, :], 0.0).then_inc(s["ce1_zero"], 1)
            pool.wait_ge(s["p_const"], 1)
            own = [0]

            def rstd(mv, ve, r, eps, summed, count):
                pool.tensor_scalar(ve[:, :], mv[:, :].rearrange("p (j t) -> p j t", t=2)[:, :, 1], eps, 1.0,
                                   ALU.add, ALU.mult).then_inc(summed, 1)
                pool.wait_ge(summed, count)
                return pool.tensor_tensor(r[:, :], ve[:, :], MHALF[:, 0:TILES], ALU.pow)

            def mean_rstd(mv, r, nm, powered, r_count, scaled, count):
                pool.wait_ge(powered, r_count)
                pool.tensor_tensor(nm[:, :], mv[:, :].rearrange("p (j t) -> p j t", t=2)[:, :, 0], r[:, :],
                                   ALU.mult).then_inc(scaled, 1)
                pool.wait_ge(scaled, count)
                alone(pool, s["pool_passed"], count)
                return pool.tensor_scalar(nm[:, :], nm[:, :], -1.0, 0.0, ALU.mult, ALU.add)

            for b in range(BATCH):
                cols = slice(b * TILES, (b + 1) * TILES)
                pool.wait_ge(s["i_var"], b + 1)
                pool.tensor_scalar(VEX[:, cols], MVX[:, b * 2 * TILES:(b + 1) * 2 * TILES].rearrange("p (j t) -> p j t", t=2)[:, :, 1],
                                   EPS, 1.0, ALU.add, ALU.mult).then_inc(s["i_ve"], 1)
                pool.wait_ge(s["i_ve"], b + 1)
                pool.tensor_tensor(RX[:, cols], VEX[:, cols], MHALF[:, 0:TILES], ALU.pow).then_inc(s["i_rstd"], 1)

            def join(first, end, turn):
                def part(i):
                    return STATS[:, first:end, i]

                d, g, h, f, v = (JOIN[:, i, first:end] for i in range(5))
                pool.wait_ge(s["stats_ready"], turn + 1)
                pool.tensor_tensor(d, part(1), part(4), ALU.subtract)
                pool.tensor_tensor(g, part(2), part(5), ALU.add).then_inc(s["ln_part"], 1)
                pool.wait_ge(s["ln_part"], turn * 3 + 1)
                pool.tensor_tensor(f, d, d, ALU.mult)
                pool.tensor_scalar(h, g, 4.0 / P, 4 * EPS, ALU.mult, ALU.add).then_inc(s["ln_part"], 1)
                pool.wait_ge(s["ln_part"], turn * 3 + 2)
                pool.tensor_tensor(v, f, h, ALU.add).then_inc(s["ln_part"], 1)
                pool.wait_ge(s["ln_part"], turn * 3 + 3)
                if first + TILES <= end and end == 2 * TILES:
                    if some(turn - 2):
                        pool.wait_ge(s["xr2"], 2 * (turn - 2))
                    pool.tensor_tensor(RSTD[:, TILES:end], JOIN[:, 4, TILES:end], MHALF[:, TILES:end],
                                       ALU.pow).then_inc(s["ln2_rstd"], 1)

            def ln1_power(turn):
                if some(turn):
                    pool.wait_ge(s["xr"], turn)
                pool.tensor_tensor(RSTD[:, 0:TILES], JOIN[:, 4, 0:TILES], MHALF[:, 0:TILES],
                                   ALU.pow).then_inc(s["ln1_rstd"], 1)

            join(0, TILES, 0)
            ln1_power(0)

            def step(n, b, slots, following):
                has_n, has_p, _ = live(n)
                if has_n:
                    pool.wait_ge(s["xTf"], n + 1)
                    pool.tensor_tensor(XTL[:, :], XTF[:, :], XTH[:, :].bitcast(FP32), ALU.subtract).then_inc(s["xTl"], 1)
                has_next = not isinstance(n, int) or n < ITEMS - 1
                if has_p or has_next:
                    join(0 if has_next else TILES, 2 * TILES if has_p else TILES, n + 1)
                if has_n:
                    pool.wait_ge(s["qmax"], n + 1)
                    pool.tensor_tensor(heads(QB[:, :]), heads(QB[:, :]), QMX[:, :].unsqueeze(2).broadcast_to([P, 32, DH]),
                                       ALU.subtract).then_inc(s["q_sub"], 1)
                if has_next:
                    ln1_power(n + 1)
                if has_n:
                    pool.wait_ge(s["q_rec"], n + 1)
                    pool.tensor_tensor(heads(QB[:, :]), heads(QB[:, :]), QRC[:, :].unsqueeze(2).broadcast_to([P, 32, DH]),
                                       ALU.mult).then_inc(s["q_nrm"], 1)

            layers(pool, step)

            def add_to_x(b, z):
                return pool.tensor_tensor(seq(X, b), seq(X, b), z, ALU.add)

            def spiking(n, live):
                if live(1):
                    i = n - 1
                    pool.wait_ge(s["s_zi"], i + 1)
                    add_to_x(i, XR[:, :]).then_inc(s["s_x1"], 1)
                if live(5):
                    i = n - 5
                    pool.wait_ge(s["s_zc"], i + 1)
                    add_to_x(i, EK[:, :]).then_inc(s["s_x2"], 1)
                if live(1):
                    i = n - 1
                    pool.wait_ge(s["s_xv"], at["s_xv"] + i + 1)
                    if some(i):
                        pool.wait_ge(s["s_xr"], i)
                        alone(pool, s["pool_passed"], i)
                    rstd(MV2, VE2, R2, EPS, s["sx_ve"], at["sx_ve"] + i + 1).then_inc(s["s_xrs"], 1)
                if live(0):
                    pool.wait_ge(s["s_iv"], at["s_iv"] + n + 1)
                    if some(n):
                        pool.wait_ge(s["s_zi"], n)
                        alone(pool, s["pool_passed"], n)
                    rstd(MV1, VE1, R1, EPS, s["si_ve"], at["si_ve"] + n + 1).then_inc(s["si_r"], 1)
                    mean_rstd(MV1, R1, NM1, s["si_r"], n + 1, s["si_mr"], n + 1).then_inc(s["s_ir"], 1)
                if live(4):
                    i = n - 4
                    pool.wait_ge(s["s_cv"], i + 1)
                    if some(i):
                        pool.wait_ge(s["s_zc"], i)
                        alone(pool, s["pool_passed"], i)
                    rstd(MV3, VE3, R3, EPS * STEPS * STEPS, s["sc_ve"], i + 1).then_inc(s["sc_r"], 1)
                    mean_rstd(MV3, R3, NM3, s["sc_r"], i + 1, s["sc_mr"], i + 1).then_inc(s["s_cr"], 1)
                if live(5):
                    i = n - 5
                    pool.wait_ge(s["c_xv"], at["c_xv"] + i + 1)
                    if some(i):
                        pool.wait_ge(s["c_xr"], at["c_xr"] + i)
                        alone(pool, s["pool_passed"], i)
                    rstd(MV4, VE4, R4, EPS, s["cx_ve"], at["cx_ve"] + i + 1).then_inc(s["c_rs"], 1)

            pipeline(pool, 6, spiking)

            def slot(item, early, late):
                if item[LN] is not None:
                    i = item[LN]
                    pool.wait_ge(s["d_xv"], at["d_xv"] + i + 1)
                    if some(i):
                        pool.wait_ge(s["d_zn"], i)
                    rstd(MV1, VE1, R1, EPS, s["dx_ve"], at["dx_ve"] + i + 1).then_inc(s["dx_r"], 1)
                    mean_rstd(MV1, R1, NM1, s["dx_r"], at["dx_r"] + i + 1, s["dx_mr"], at["dx_mr"] + i + 1).then_inc(s["d_xs"], 1)
                if item[FINISH] is not None:
                    i = item[FINISH]
                    pool.wait_ge(s["d_zo"], i + 1)
                    add_to_x(i, MEM[:, :]).then_inc(s["d_out"], 1)
                if item[NORM] is not None:
                    i = item[NORM]
                    pool.wait_ge(s["c_zo"], i + 1)
                    add_to_x(i, EK[:, :]).then_inc(s["c_x"], 1)
                if item[GATE] is not None:
                    i = item[GATE]
                    pool.wait_ge(s["d_ov"], at["d_ov"] + i + 1)
                    if some(i):
                        pool.wait_ge(s["d_zo"], i)
                    rstd(MV2, VE2, R2, EPS, s["do_ve"], at["do_ve"] + i + 1).then_inc(s["do_r"], 1)
                    mean_rstd(MV2, R2, NM2, s["do_r"], i + 1, s["do_mr"], i + 1).then_inc(s["d_os"], 1)
                if item[PROJECT] is not None:
                    i = item[PROJECT]
                    pool.wait_ge(s["c_ov"], at["c_ov"] + i + 1)
                    if some(i):
                        pool.wait_ge(s["c_zo"], i)
                    rstd(MV3, VE3, R3, EPS, s["co_ve"], at["co_ve"] + i + 1).then_inc(s["co_r"], 1)
                    mean_rstd(MV3, R3, NM3, s["co_r"], at["co_r"] + i + 1, s["co_mr"], at["co_mr"] + i + 1).then_inc(s["c_or"], 1)

            slots(slot)

        @block.scalar
        def _(act):
            def copy(o, i):
                return nc.scalar.activation(o, i, ACT.Copy)

            def normalise(o, i, r, nm):
                for j in range(TILES):
                    cols = slice(j * P, (j + 1) * P)
                    last = nc.scalar.activation(o[:, cols], i[:, cols] if not callable(i) else i(j), ACT.Identity,
                                                bias=nm[:, j:j + 1], scale=r[:, j:j + 1])
                return last

            def prepare(l, slot, times, part):
                if part == 0:
                    act.wait_ge(s["wqkv_ps"], l + 1)
                    copy(QKH[slot][:, :], pW[:, 0:2 * P]).then_inc(s["wqk_hi"], 1)
                    copy(WV[slot][:, :], pW[:, 2 * P:3 * P]).then_inc(s["wqkv_out"], 1)
                if part == 1:
                    act.wait_ge(s["w1_ps"], l + 1)
                    copy(W1H[slot][:, :], pW[:, :]).then_inc(s["w1_hi"], 1)
                if part == 2:
                    act.wait_ge(s["bias_ps"], l + 1)
                    copy(BIAS[slot][:, :], pW[:, 0:2 + FB]).then_inc(s["bias_out"], 1)
                if part == 3:
                    act.wait_ge(s["bm_ps"], l + 1)
                    copy(BM[slot][:, :], pW[:, 0:P]).then_inc(s["bm_out"], 1)

            act.wait_ge(s["ssm_in"], SSM_LOADS)
            nc.scalar.activation(LA[:, :], ALOG[:, :], ACT.Exp, scale=-1.0).then_inc(s["la_exp"], 1)
            act.wait_ge(s["e1_arg"], 1)
            nc.scalar.activation(E1[:, :], E1[:, :], ACT.Exp).then_inc(s["e1"], 1)
            for p4 in range(PAIRS // 4):
                act.wait_ge(s["e2_arg"], p4 + 1)
                nc.scalar.activation(E2[:, p4 * 512:(p4 + 1) * 512], E2[:, p4 * 512:(p4 + 1) * 512], ACT.Exp).then_inc(s["e2"], 1)
            for part in range(4):
                prepare(0, 0, 1, part)

            def scaled(o, b, first, src=XI, r=RSTD, begin=0, end=TILES):
                for j in range(begin, end):
                    last = nc.scalar.activation(o[:, j * P:(j + 1) * P], tile(src, b, j), ACT.Copy,
                                                scale=r[:, first + j:first + j + 1])
                return last

            def step(n, b, slots, following):
                has_n, has_p, has_m = live(n)
                has_next = not isinstance(n, int) or n < ITEMS - 1
                wa, wp, wf = slots
                m = n - 2
                k0 = m * FB

                def ha(f):
                    if not has_m:
                        return
                    act.wait_ge(s["h_ps"], k0 + f + 1)
                    if some(k0 + f - 1):
                        act.wait_ge(s["hl"], k0 + f - 1)
                    nc.scalar.activation(HA[f % 2][:, :], pH[f % 2][:, :], ACT.Identity,
                                         bias=BIAS[wf][:, 2 + f:3 + f]).then_inc(s["ha"], 1)

                def part(i):
                    if following is not None:
                        prepare(*following, i)

                if isinstance(n, int) and n == 2:
                    act.wait_ge(s["k_ps"], 1)
                    for h in range(2):
                        last = copy(KTM[:, :].rearrange("p (q h i) -> p h i q", q=TILES, h=2)[:, h],
                                    pW[:, :].rearrange("p (i h q) -> p h i q", h=2, q=TILES)[:, h])
                    last.then_inc(s["k_out"], 1)
                ha(0)
                ha(1)
                if has_n:
                    act.wait_ge(s["xT_ps"], n + 1)
                    copy(XTH[:, :], pXT[:, :])
                    copy(XTF[:, :], pXT[:, :]).then_inc(s["xTf"], 1)
                part(0)
                ha(2)
                part(1)
                if has_n:
                    act.wait_ge(s["q_ps"], n + 1)
                    nc.scalar.activation(QF[:, :], pQ[:, :], ACT.Identity, bias=BIAS[wa][:, 0:1]).then_inc(s["q_fm"], 1)
                    act.wait_ge(s["kmax"], n + 1)
                    nc.scalar.activation(EK[:, :], pK[:, :], ACT.Exp, bias=NKM[:, 0:1], accum_out=KSM[:, 0:1]).then_inc(s["ek"], 1)
                ha(3)
                if has_n:
                    act.wait_ge(s["ekT_ps"], n + 1)
                    copy(EKT[:, :], pXT[:, :]).then_inc(s["ek_tm"], 1)
                part(2)
                if has_p:
                    act.wait_ge(s["ln2_rstd"], n)
                    scaled(XR2, before(b, 1), TILES, end=2).then_inc(s["xr2"], 1)
                    scaled(XR2, before(b, 1), TILES, begin=2).then_inc(s["xr2"], 1)
                if has_n:
                    act.wait_ge(s["g_ps"], n + 1)
                    copy(GT[:, :], pK[:, 0:P]).then_inc(s["gt"], 1)
                if has_p:
                    act.wait_ge(s["x2T_ps"], n)
                    copy(X2H[:, :], pX2[:, :]).then_inc(s["x2h"], 1)
                if has_n:
                    act.wait_ge(s["q_sub"], n + 1)
                    nc.scalar.activation(QB[:, :], QB[:, :], ACT.Exp).then_inc(s["q_exp"], 1)
                if has_next:
                    act.wait_ge(s["ln1_rstd"], n + 2)
                    scaled(XR, before(b, -1), 0).then_inc(s["xr"], 1)
                part(3)

            act.wait_ge(s["ln1_rstd"], 1)
            scaled(XR, 0, 0).then_inc(s["xr"], 1)
            layers(act, step)

            act.wait_ge(s["fc_ps"], 1)
            copy(FCH[:, :], pW[:, :]).then_inc(s["fc_hi"], 1)
            act.wait_ge(s["win_ps"], 1)
            copy(WINC[:, :], pW[:, 0:P]).then_inc(s["win_out"], 1)

            def spiking(n, live):
                m = n - 2

                def squared(f):
                    if not live(2):
                        return
                    k = m * FB + f
                    act.wait_ge(s["s_h_ps"], at["s_h_ps"] + k + 1)
                    nc.scalar.activation(HA[f % 2][:, :], pH[f % 2][:, :], ACT.Relu).then_inc(s["s_relu"], 1)
                    act.wait_ge(s["s_relu"], at["s_relu"] + k + 1)
                    if some(k - 1):
                        act.wait_ge(s["s_y_ps"], at["s_y_ps"] + k - 1)
                    nc.scalar.activation(HL[f % 2][:, :], HA[f % 2][:, :], ACT.Square).then_inc(s["s_sq"], 1)

                squared(0)
                squared(1)
                if live(6):
                    i = n - 6
                    act.wait_ge(s["c_rs"], at["c_rs"] + i + 1)
                    if some(i):
                        act.wait_ge(s["c_xT_ps"], at["c_xT_ps"] + i)
                    scaled(QS, i, 0, X, R4).then_inc(s["c_xr"], 1)
                squared(2)
                if live(1):
                    i = n - 1
                    act.wait_ge(s["s_xrs"], at["s_xrs"] + i + 1)
                    if some(i):
                        act.wait_ge(s["s_xT_ps"], at["s_xT_ps"] + i)
                    scaled(XR2, i, 0, X, R2).then_inc(s["s_xr"], 1)
                squared(3)
                if live(1):
                    act.wait_ge(s["s_xT_ps"], at["s_xT_ps"] + n)
                    copy(X2H[:, :], pX2[:, :]).then_inc(s["s_hi"], 1)
                if live(6):
                    i = n - 6
                    act.wait_ge(s["c_xT_ps"], at["c_xT_ps"] + i + 1)
                    if some(i):
                        act.wait_ge(s["c_u_ps"], at["c_u_ps"] + i)
                    copy(XTF[:, :], pXT[:, :]).then_inc(s["c_xT"], 1)
                if live(0):
                    act.wait_ge(s["s_ir"], at["s_ir"] + n + 1)
                    if some(n):
                        act.wait_ge(s["s_x1"], n)
                    normalise(XR[:, :], lambda j: tile(XI, n, j), R1, NM1).then_inc(s["s_zi"], 1)
                if live(2):
                    act.wait_ge(s["s_y_ps"], at["s_y_ps"] + (m + 1) * FB)
                    if some(m):
                        act.wait_ge(s["s_acc"], m * (STEPS - 1))
                    copy(YM[:, :], pY[:, :]).then_inc(s["s_y1"], 1)
                if live(4):
                    i = n - 4
                    act.wait_ge(s["s_cr"], i + 1)
                    if some(i):
                        act.wait_ge(s["s_x2"], i)
                    normalise(EK[:, :], pQ[:, :], R3, NM3).then_inc(s["s_zc"], 1)
                for part, (when, o, width) in enumerate(((3, KRE, SEQ), (9, KIM, SEQ), (10, KRE2, P))):
                    if isinstance(n, int) and n == when:
                        act.wait_ge(s["kf_ps"], part + 1)
                        copy(o[:, :], pW[:, 0:width]).then_inc(s["kf"], 1)

            pipeline(act, 6, spiking)

            def slot(item, early, late):
                if item[FINISH] is not None:
                    i = item[FINISH]
                    act.wait_ge(s["d_os"], at["d_os"] + i + 1)
                    if some(i):
                        act.wait_ge(s["d_out"], i)
                    normalise(MEM[:, :], ACC[:, :], R2, NM2).then_inc(s["d_zo"], 1)
                if item[NORM] is not None:
                    i = item[NORM]
                    act.wait_ge(s["c_or"], at["c_or"] + i + 1)
                    if some(i):
                        act.wait_ge(s["c_x"], i)
                    normalise(EK[:, :], EKT[:, :], R3, NM3).then_inc(s["c_zo"], 1)
                if item[TURN] is not None:
                    i = item[TURN]
                    act.wait_ge(s["d_xs"], at["d_xs"] + i + 1)
                    if some(i):
                        act.wait_ge(s["d_xT_ps"], at["d_xT_ps"] + i)
                    normalise(XR2[:, :], lambda j: tile(X, i, j), R1, NM1).then_inc(s["d_zn"], 1)
                if item[INVERSE] is not None:
                    i = item[INVERSE]
                    act.wait_ge(s["c_y_ps"], i + 1)
                    if some(i):
                        act.wait_ge(s["c_yT"], i)
                    copy(YR[:, :], PS[5][:, 2 * P:4 * P])
                    copy(YS[:, :], PS[(4, 7)[i % 2]][:, 2 * P:4 * P]).then_inc(s["c_second"], 1)
                if item[TURN] is not None:
                    i = item[TURN]
                    act.wait_ge(s["d_xT_ps"], at["d_xT_ps"] + i + 1)
                    if some(i):
                        act.wait_ge(s["d_mix"], i)
                    copy(SH[:, 1:1 + SEQ], pX2[:, :]).then_inc(s["d_xT"], 1)
                if item[MIX] is not None:
                    i = item[MIX]
                    act.wait_ge(s["d_k_ps"], at["d_k_ps"] + i + 1)
                    nc.scalar.activation(QF[:, :], pK[:, :], ACT.Relu).then_inc(s["d_relu"], 1)
                    act.wait_ge(s["d_relu"], at["d_relu"] + i + 1)
                    if some(i):
                        act.wait_ge(s["d_v_ps"], at["d_v_ps"] + i)
                    nc.scalar.activation(HL[0][:, :], QF[:, :], ACT.Square).then_inc(s["d_sq"], 1)
                    act.wait_ge(s["d_r_ps"], at["d_r_ps"] + i + 1)
                    if some(i):
                        act.wait_ge(s["d_rv"], i)
                    nc.scalar.activation(QB[:, :], pQ[:, :], ACT.Sigmoid).then_inc(s["d_sig"], 1)

            slots(slot)

        @block.vector
        def _(dve):
            tt, ts, stt = nc.vector.tensor_tensor, nc.vector.tensor_scalar, nc.vector.scalar_tensor_tensor

            def stats(src, st, mv, parted, count):
                for j in range(TILES):
                    last = nc.vector.bn_stats(st[:, j * 6:(j + 1) * 6], src(j))
                last.then_inc(parted, 1)
                dve.wait_ge(parted, count)
                alone(dve, s["dve_passed"], count)
                for j in range(TILES):
                    last = nc.vector.bn_aggr(mv[:, 2 * j:2 * j + 2], st[:, j * 6:(j + 1) * 6])
                return last

            nc.vector.memset(EIGHTH[0:1, :], 1.0 / HEADS).then_inc(s["eighth"], 1)

            def prepare(l, slot, times, part):
                if part == 0:
                    dve.wait_ge(s["w_in"][slot], times * W_LOADS)
                    ts(LNP[0][:, :], CENT[:, :], LNC[slot][:, 0:1], 2.0, ALU.mult, ALU.mult)
                    ts(LNP[1][:, :], CENT[:, :], LNC[slot][:, 2:3], 2.0, ALU.mult, ALU.mult).then_inc(s["lnp"], 1)
                if part == 1:
                    dve.wait_ge(s["wqk_hi"], l + 1)
                    dve.wait_ge(s["wqkv_out"], 2 * l + 1)
                    tt(QKL[slot][:, :], pW[:, 0:2 * P], QKH[slot][:, :].bitcast(FP32), ALU.subtract).then_inc(s["wqkv_out"], 1)
                if part == 2:
                    dve.wait_ge(s["w1_hi"], l + 1)
                    tt(W1L[slot][:, :], pW[:, :], W1H[slot][:, :].bitcast(FP32), ALU.subtract).then_inc(s["w1_out"], 1)
                if part == 3:
                    dve.wait_ge(s["bias_out"], l + 1)
                    ts(MBV[:, :], HMASK[:, :], BIAS[slot][:, 1:2], None, ALU.mult).then_inc(s["mbv"], 1)
                if part == 4:
                    dve.wait_ge(s["bm_out"], l + 1)
                    dve.sem_inc(s["w_ready"], 1)


            dve.wait_ge(s["ssm_in"], SSM_LOADS)
            dve.wait_ge(s["la_exp"], 1)
            tt(CDB[:, :], BMAT[:, :], DTR[:, :], ALU.mult).then_inc(s["cdb"], 1)
            stt(out=LA[:, :], in0=LA[:, :], scalar=-1.0, in1=DTR[:, :], op0=ALU.mult, op1=ALU.mult).then_inc(s["la"], 1)
            dve.wait_ge(s["cdb"], 1)
            dve.wait_ge(s["la"], 1)
            tt(CDB[:, :], CMAT[:, :], CDB[:, :], ALU.mult).then_inc(s["cdb"], 1)
            for q in range(TILES):
                last = ts(E1[:, :].rearrange("p (i q) -> p i q", q=TILES)[:, :, q], LA[:, :], float(q * P), None, ALU.mult)
            last.then_inc(s["e1_arg"], 1)
            for p4 in range(PAIRS // 4):
                tt(E2[:, p4 * 512:(p4 + 1) * 512].rearrange("p (i r) -> p i r", i=4),
                   LA[:, 4 * p4:4 * p4 + 4].unsqueeze(2).broadcast_to([P, 4, P]),
                   IOTA[:, :].unsqueeze(1).broadcast_to([P, 4, P]), ALU.mult).then_inc(s["e2_arg"], 1)
                if p4 == 0:
                    dve.wait_ge(s["e1"], 1)
                    dve.wait_ge(s["cdb"], 2)
                    dve.wait_ge(s["ce1_zero"], 1)
                    for h in range(2):
                        o = slice(h * STATES, (h + 1) * STATES)
                        last = tt(CE1[o, :].rearrange("p (i h q) -> p h i q", h=2, q=TILES)[:, h],
                                  E1[o, :].rearrange("p (i q) -> p i q", q=TILES),
                                  CDB[o, :].unsqueeze(2).broadcast_to([STATES, PAIRS, TILES]), ALU.mult)
                    last.then_inc(s["ce1"], 1)
            dve.wait_ge(s["c_in"], 3 * 16)
            nc.vector.tensor_copy(IDB[:, :], ID[:, :])
            nc.vector.memset(SH[:, 0:1], 0.0).then_inc(s["sh0"], 1)
            prepare(0, 0, 1, 0)

            dve.wait_ge(s["x_in"], 16 * BATCH)
            for b in range(BATCH + 1):
                if b < BATCH:
                    for j in range(b * TILES, (b + 1) * TILES):
                        last = nc.vector.bn_stats(STX[:, 6 * j:6 * j + 6], X[:, j * P:(j + 1) * P])
                    last.then_inc(s["i_st"], 1)
                if b:
                    dve.wait_ge(s["i_st"], b)
                    for j in range((b - 1) * TILES, b * TILES):
                        last = nc.vector.bn_aggr(MVX[:, 2 * j:2 * j + 2], STX[:, 6 * j:6 * j + 6])
                    last.then_inc(s["i_var"], 1)
                if b == 2:
                    prepare(0, 0, 1, 1)
                if b == 5:
                    prepare(0, 0, 1, 2)
            prepare(0, 0, 1, 3)

            def ln_stats(b, first):
                for j in range(TILES):
                    last = nc.vector.bn_stats(STATS[:, first + j, :], tile(XI, b, j))
                return last

            dve.wait_ge(s["i_var"], BATCH)
            for b in range(BATCH):
                dve.wait_ge(s["i_rstd"], b + 1)
                for j in range(b * TILES, (b + 1) * TILES):
                    last = ts(XI[:, j * P:(j + 1) * P], X[:, j * P:(j + 1) * P], MVX[:, 2 * j:2 * j + 1], RX[:, j:j + 1],
                              ALU.subtract, ALU.mult)
                last.then_inc(s["xi_init"], 1)
                if b == 0:
                    dve.wait_ge(s["xi_init"], 1)
                    ln_stats(0, 0).then_inc(s["stats_ready"], 1)
            dve.wait_ge(s["xi_init"], BATCH)
            prepare(0, 0, 1, 4)
            dve.wait_ge(s["ln_part"], 1)
            ln_stats(1, 0).then_inc(s["stats_ready"], 1)

            def butterfly(u, o, count):
                pair = FLY[:, 0:4 * P]
                tt(pair[:, 0:2 * P], u[:, 0:2 * P], u[:, 2 * P:4 * P], ALU.add)
                tt(pair[:, 2 * P:4 * P], u[:, 0:2 * P], u[:, 2 * P:4 * P], ALU.subtract).then_inc(s["fly_pair"], 1)
                dve.wait_ge(s["fly_pair"], count)
                tt(o(0), pair[:, 0:P], pair[:, P:2 * P], ALU.add)
                tt(o(1), pair[:, 0:P], pair[:, P:2 * P], ALU.subtract)
                ts(FLY[:, 4 * P:6 * P].rearrange("p (i c) -> p i c", c=P),
                   pair.rearrange("p (i h c) -> p i h c", i=2, h=2)[:, :, 1], 0.5 ** 0.5, None, ALU.mult).then_inc(s["fly_root"], 1)
                nc.vector.tensor_copy(o(4), pair[:, 2 * P:3 * P])
                nc.vector.tensor_copy(o(5), pair[:, 3 * P:4 * P])
                dve.wait_ge(s["fly_root"], count)
                tt(o(2), u[:, 0:P], FLY[:, 5 * P:6 * P], ALU.add)
                tt(o(3), FLY[:, 4 * P:5 * P], u[:, 2 * P:3 * P], ALU.add)
                tt(o(6), u[:, 0:P], FLY[:, 5 * P:6 * P], ALU.subtract)
                return tt(o(7), FLY[:, 4 * P:5 * P], u[:, 2 * P:3 * P], ALU.subtract)

            def step(n, b, slots, following):
                has_n, has_p, has_m = live(n)
                wa, wp, wf = slots
                has_next = not isinstance(n, int) or n < ITEMS - 1
                m = n - 2
                k0 = m * FB

                def hl(f):
                    if not has_m:
                        return
                    dve.wait_ge(s["ha"], k0 + f + 1)
                    if some(k0 + f - 1):
                        dve.wait_ge(s["y_ps"], k0 + f - 1)
                    stt(out=HL[f % 2][:, :], in0=HA[f % 2][:, :], scalar=LEAK, in1=HA[f % 2][:, :],
                        op0=ALU.mult, op1=ALU.max).then_inc(s["hl"], 1)

                def part(i):
                    if following is not None:
                        prepare(*following, i)

                part(0)
                if isinstance(n, int) and n == 2:
                    dve.wait_ge(s["k_out"], 1)
                    tt(KTM[0:1, 0:P], KTM[0:1, 0:P], DP[0:1, :], ALU.add).then_inc(s["k_skip"], 1)
                    dve.wait_ge(s["k_skip"], 1)
                    butterfly(KTM, lambda q: KV[:, q * P:(q + 1) * P], 1).then_inc(s["ktm"], 1)
                hl(0)
                if has_p:
                    dve.wait_ge(s["m_ps"], n)
                    dve.wait_ge(s["k_rec"], n)
                    stt(out=MM[:, :], in0=pK[:, 2 * P:3 * P], scalar=KRC[:, 0:1], in1=BM[wp][:, :],
                        op0=ALU.mult, op1=ALU.add).then_inc(s["m_ready"], 1)
                    dve.wait_ge(s["q_nrm"], n)
                    nc.vector.transpose(QS[:, :], QB[:, :]).then_inc(s["qs"], 1)
                hl(1)
                part(1)
                if has_p:
                    dve.wait_ge(s["out_ps"], n)
                    xo = seq(XI, before(b, 1))
                    tt(xo, pQ[:, :], xo, ALU.add).then_inc(s["resid1"], 1)
                    dve.wait_ge(s["resid1"], n)
                    if some(n - 1):
                        dve.wait_ge(s["ln2_rstd"], n - 1)
                    alone(dve, s["dve_passed"], n)
                    ln_stats(before(b, 1), TILES).then_inc(s["stats_ready"], 1)
                if has_n:
                    dve.wait_ge(s["k_ps2"], n + 1)
                    nc.vector.tensor_reduce(NKM[:, 0:1], pK[:, :], AX.X, ALU.max, negate=True).then_inc(s["kmax"], 1)
                hl(2)
                part(2)
                if has_n:
                    dve.wait_ge(s["q_fm"], n + 1)
                    nc.vector.transpose(QB[:, :], QF[:, :]).then_inc(s["q_blk"], 1)
                    dve.wait_ge(s["q_blk"], n + 1)
                    nc.vector.tensor_reduce(QMX[:, :], heads(QB[:, :]), AX.X, ALU.max).then_inc(s["qmax"], 1)
                hl(3)
                if has_n:
                    dve.wait_ge(s["ek"], n + 1)
                    nc.vector.reciprocal(KRC[:, :], KSM[:, :]).then_inc(s["k_rec"], 1)
                if not isinstance(n, int) or n < ITEMS - 2:
                    dve.wait_ge(s["ln_part"], (n + 1) * 3 + 1)
                    alone(dve, s["dve_passed"], n + 1)
                    ln_stats(before(b, -2), 0)
                part(3)
                if has_p:
                    dve.wait_ge(s["x2h"], n)
                    tt(X2L[:, :], pX2[:, :], X2H[:, :].bitcast(FP32), ALU.subtract).then_inc(s["x2l"], 1)
                if has_n:
                    dve.wait_ge(s["c_ps"], n + 1)
                    tt(CT[:, :], pK[:, P:2 * P], HMASK[:, :], ALU.mult).then_inc(s["ct"], 1)
                    dve.wait_ge(s["q_exp"], n + 1)
                    nc.vector.tensor_reduce(QSM[:, :], heads(QB[:, :]), AX.X, ALU.add).then_inc(s["q_sum"], 1)
                    dve.wait_ge(s["q_sum"], n + 1)
                    nc.vector.reciprocal(QRC[:, :], QSM[:, :]).then_inc(s["q_rec"], 1)
                if has_m:
                    dve.wait_ge(s["y_ps"], k0 + FB)
                    xo = seq(XI, before(b, 2))
                    tt(xo, pY[:, :], xo, ALU.add).then_inc(s["resid2"], 1)
                part(4)

            layers(dve, step)

            dve.wait_ge(s["resid2"], ITEMS)
            dve.wait_ge(s["fc_hi"], 1)
            tt(FCL[:, :], pW[:, :], FCH[:, :].bitcast(FP32), ALU.subtract).then_inc(s["fc_out"], 1)

            def bn_parts(src, st, half, parted):
                for j in range(2 * half, 2 * half + 2):
                    last = nc.vector.bn_stats(st[:, j * 6:(j + 1) * 6], src(j))
                if half:
                    last.then_inc(parted, 1)

            def bn_join(st, mv):
                for j in range(TILES):
                    last = nc.vector.bn_aggr(mv[:, 2 * j:2 * j + 2], st[:, j * 6:(j + 1) * 6])
                return last

            def spiking(n, live):
                if live(1):
                    i = n - 1
                    dve.wait_ge(s["s_x1"], i + 1)
                    if some(i):
                        dve.wait_ge(s["s_xrs"], at["s_xrs"] + i)
                    alone(dve, s["dve_passed"], i + 1)
                    stats(lambda j: tile(X, i, j), ST2, MV2, s["sxv_st"], at["sxv_st"] + i + 1).then_inc(s["s_xv"], 1)

                def parts(t, half):
                    if t == 0 and live(0):
                        if half == 0 and some(n):
                            dve.wait_ge(s["s_ir"], at["s_ir"] + n)
                            alone(dve, s["dve_passed"], n)
                        return bn_parts(lambda j: tile(XI, n, j), ST1, half, s["siv_st"])
                    if t == 1 and live(4):
                        if half == 0:
                            dve.wait_ge(s["s_cnt"], at["s_cnt"] + n - 3)
                            if some(n - 4):
                                dve.wait_ge(s["s_cr"], n - 4)
                            alone(dve, s["dve_passed"], n - 3)
                        return bn_parts(lambda j: pQ[:, j * P:(j + 1) * P], ST3, half, s["scv_st"])
                    if t == 2 and live(5):
                        if half == 0:
                            dve.wait_ge(s["s_x2"], n - 4)
                            if some(n - 5):
                                dve.wait_ge(s["c_rs"], at["c_rs"] + n - 5)
                            alone(dve, s["dve_passed"], n - 4)
                        return bn_parts(lambda j: tile(X, n - 5, j), ST4, half, s["cxv_st"])

                def joined(t):
                    if t == 1 and live(0):
                        dve.wait_ge(s["siv_st"], at["siv_st"] + n + 1)
                        alone(dve, s["dve_passed"], n + 1)
                        bn_join(ST1, MV1).then_inc(s["s_iv"], 1)
                    if t == 2 and live(4):
                        dve.wait_ge(s["scv_st"], n - 3)
                        alone(dve, s["dve_passed"], n - 3)
                        bn_join(ST3, MV3).then_inc(s["s_cv"], 1)
                    if t == 3 and live(5):
                        dve.wait_ge(s["cxv_st"], at["cxv_st"] + n - 4)
                        alone(dve, s["dve_passed"], n - 4)
                        bn_join(ST4, MV4).then_inc(s["c_xv"], 1)

                i = n - 3
                if live(3):
                    dve.wait_ge(s["s_y1"], i + 1)
                    if some(i):
                        dve.wait_ge(s["s_cnt"], at["s_cnt"] + i)
                mem = YM
                for t in range(STEPS):
                    if live(3):
                        if t:
                            dve.wait_ge(s["s_mem"], i * (STEPS - 1) + t)
                        ts(SPK[t][:, :], mem[:, :], 1.0, None, ALU.is_gt).then_inc(s["s_spk"], 1)
                        if t < STEPS - 1:
                            stt(out=ACC[:, :], in0=mem[:, :], scalar=BETA, in1=YM[:, :], op0=ALU.mult,
                                op1=ALU.add).then_inc(s["s_acc"], 1)
                    joined(t)
                    parts(t, 0)
                    if live(3) and t < STEPS - 1:
                        dve.wait_ge(s["s_spk"], i * STEPS + t + 1)
                        dve.wait_ge(s["s_acc"], i * (STEPS - 1) + t + 1)
                        mem = MEM
                        tt(MEM[:, :], ACC[:, :], SPK[t][:, :], ALU.subtract).then_inc(s["s_mem"], 1)
                    parts(t, 1)
                    if t == 3 and live(1):
                        dve.wait_ge(s["s_hi"], at["s_hi"] + n)
                        tt(X2L[:, :], pX2[:, :], X2H[:, :].bitcast(FP32), ALU.subtract).then_inc(s["s_lo"], 1)
                if live(6):
                    i = n - 6
                    dve.wait_ge(s["c_u_ps"], at["c_u_ps"] + i + 1)
                    tt(tiles(U[:, :]), tiles(pK[:, :]), BIN[:, :].unsqueeze(1).broadcast_to([P, TILES, P]),
                       ALU.add).then_inc(s["c_ub"], 1)
                    dve.wait_ge(s["c_ub"], i + 1)
                    butterfly(U, lambda q: V[:, bass.ds(q * (BATCH * P) + i * P, P)], i + 2).then_inc(s["c_u"], 1)

            pipeline(dve, 6, spiking)

            def forward(g, k):
                dve.wait_ge(s["c_f_ps"], at["c_f_ps"] + g * TILES + k + 1)
                if g and k == 0:
                    dve.wait_ge(s["c_y_ps"], g * GROUP)
                if some(g * TILES + k):
                    dve.wait_ge(s["c_yf"], g * TILES + k)
                pr, pi = PS[4 + (k % 2) * 2], PS[5 + (k % 2) * 2]
                kr = KRE[:, k * P:(k + 1) * P].unsqueeze(1).broadcast_to([P, GROUP, P])
                ki = KIM[:, k * P:(k + 1) * P].unsqueeze(1).broadcast_to([P, GROUP, P])
                kr2 = (KRE2[:, :] if k == 0 else KRE[:, k * P:(k + 1) * P]).unsqueeze(1).broadcast_to([P, GROUP, P])
                yr, yi = YF[:, k * SEQ:(k + 1) * SEQ], YF[:, (TILES + k) * SEQ:(TILES + k + 1) * SEQ]
                tt(tiles(HA[0][:, :]), tiles(pi[:, :]), ki, ALU.mult).then_inc(s["c_m"], 1)
                tt(tiles(HA[1][:, :]), tiles(pi[:, :]), kr2, ALU.mult).then_inc(s["c_m"], 1)
                tt(tiles(yr), tiles(pr[:, :]), kr, ALU.mult).then_inc(s["c_m"], 1)
                tt(tiles(yi), tiles(pr[:, :]), ki, ALU.mult).then_inc(s["c_m"], 1)
                dve.wait_ge(s["c_m"], (g * TILES + k) * 4 + 4)
                tt(yr, yr, HA[0][:, :], ALU.subtract)
                tt(yi, yi, HA[1][:, :], ALU.add).then_inc(s["c_yf"], 1)

            def inverse(item):
                dve.wait_ge(s["c_second"], item + 1)
                if some(item):
                    dve.wait_ge(s["c_o_ps"], item)
                a, c = PS[(4, 7)[item % 2]], PS[5]
                root = 0.5 ** 0.5
                tt(YAC[:, :], c[:, 0:2 * P], YR[:, :], ALU.add)
                tt(YBD[:, :], c[:, 0:2 * P], YR[:, :], ALU.subtract).then_inc(s["c_rot"], 1)
                tt(YE[:, :], a[:, 0:2 * P], YS[:, :], ALU.add)
                tt(YG[:, :], a[:, 0:2 * P], YS[:, :], ALU.subtract)
                dve.wait_ge(s["c_rot"], item + 1)
                tt(YBC[:, 0:P], YBD[:, 0:P], YAC[:, P:2 * P], ALU.subtract)
                tt(YBC[:, P:2 * P], YBD[:, 0:P], YAC[:, P:2 * P], ALU.add).then_inc(s["c_halves"], 1)
                dve.wait_ge(s["c_halves"], item + 1)
                tt(XTF[:, 0:P], YE[:, 0:P], YAC[:, 0:P], ALU.add)
                tt(XTF[:, 2 * P:3 * P], YG[:, 0:P], YBD[:, P:2 * P], ALU.subtract)
                stt(out=XTF[:, P:2 * P], in0=YBC[:, 0:P], scalar=root, in1=YG[:, P:2 * P], op0=ALU.mult, op1=ALU.add)
                stt(out=XTF[:, 3 * P:4 * P], in0=YBC[:, P:2 * P], scalar=-root, in1=YE[:, P:2 * P], op0=ALU.mult,
                    op1=ALU.add).then_inc(s["c_yT"], 1)

            def project(item):
                dve.wait_ge(s["c_o_ps"], item + 1)
                if some(item):
                    dve.wait_ge(s["c_zo"], item)
                tt(tiles(EKT[:, :]), tiles(pY[:, :]), BOUT[:, :].unsqueeze(1).broadcast_to([P, TILES, P]), ALU.add).then_inc(s["c_z"], 1)
                dve.wait_ge(s["c_z"], item + 1)
                stats(lambda j: EKT[:, j * P:(j + 1) * P], ST3, MV3, s["cov_st"], at["cov_st"] + item + 1).then_inc(s["c_ov"], 1)

            dve.wait_ge(s["sh0"], 1)

            for k in range(TILES):
                forward(0, k)

            def slot(item, early, late):
                if item[LN] is not None:
                    i = item[LN]
                    dve.wait_ge(s["c_x"], i + 1)
                    if some(i):
                        dve.wait_ge(s["d_xs"], at["d_xs"] + i)
                    stats(lambda j: tile(X, i, j), ST1, MV1, s["dxv_st"], at["dxv_st"] + i + 1).then_inc(s["d_xv"], 1)
                if item[MIX] is not None:
                    i = item[MIX]
                    dve.wait_ge(s["d_xT"], at["d_xT"] + i + 1)
                    tt(YM[:, :], SH[:, 1:1 + SEQ], SH[:, 0:SEQ], ALU.subtract).then_inc(s["d_diff"], 1)
                    dve.wait_ge(s["d_diff"], i + 1)
                    if some(i):
                        dve.wait_ge(s["d_r_ps"], at["d_r_ps"] + i)
                    stt(out=XR[:, :], in0=YM[:, :], scalar=MU[:, 0:1], in1=SH[:, 0:SEQ], op0=ALU.mult, op1=ALU.add)
                    stt(out=QS[:, :], in0=YM[:, :], scalar=MU[:, 1:2], in1=SH[:, 0:SEQ], op0=ALU.mult,
                        op1=ALU.add).then_inc(s["d_mix"], 1)
                if item[GATE] is not None:
                    i = item[GATE]
                    dve.wait_ge(s["d_sig"], i + 1)
                    dve.wait_ge(s["d_v_ps"], at["d_v_ps"] + i + 1)
                    if some(i):
                        dve.wait_ge(s["d_zo"], i)
                    tt(ACC[:, :], pXT[:, :], QB[:, :], ALU.mult).then_inc(s["d_rv"], 1)
                    dve.wait_ge(s["d_rv"], i + 1)
                    stats(lambda j: ACC[:, j * P:(j + 1) * P], ST2, MV2, s["dov_st"], at["dov_st"] + i + 1).then_inc(s["d_ov"], 1)
                if item[PROJECT] is not None:
                    project(item[PROJECT])
                if item[INVERSE] is not None:
                    inverse(item[INVERSE])
                for k in early + late:
                    forward(1, k)

            slots(slot)


_ARGS = ["x", "qkv", "wo", "w1", "w2", "lnc", "bo", "fcT", "proj", "winT", "woutT", "alog", "bmat", "cmat", "dtr", "dp",
         "bins", "bouts", "wrT", "wkT", "wvT", "mu", "ident", "cent", "hmask", "iota", "fwd", "fwdx", "inv"]


def spectrum_matrices():
    n = 2 * SEQ
    m = np.arange(P)
    bins = [np.where(m < P // 2, 8 * m, 8 * (m - P // 2) + 4)] + [8 * m + r for r in (1, 2, 3)]
    fwd = np.zeros((2, P, 2, TILES, P))
    for k, f in enumerate(bins):
        phase = (np.outer(m, f) % n) * (2 * np.pi / n)
        cos, sin = np.cos(phase), np.sin(phase)
        if k:
            fwd[0, :, 0, k], fwd[0, :, 1, k] = cos, -sin
            fwd[1, :, 0, k], fwd[1, :, 1, k] = -sin, -cos
        else:
            for j, rows in enumerate((m < P // 2, m >= P // 2)):
                fwd[j, :, 0, k], fwd[j, :, 1, k] = cos * rows, -sin * rows
    fwdx = fwd[:, :, ::-1, 0].copy()
    sign = 1.0 - 2.0 * (m % 2)
    fwdx[0, :, 1, 0] = fwd[0, :, 1, 0, 0] = sign
    inv = np.zeros((2, TILES, P, 2, P))
    for k, f in enumerate(bins):
        phase = (np.outer(f, m) % n) * (2 * np.pi / n)
        cos, sin = np.cos(phase), np.sin(phase)
        if k:
            inv[0, k, :, 0], inv[0, k, :, 1] = cos, sin
            inv[1, k, :, 0], inv[1, k, :, 1] = -sin, cos
        else:
            odd = np.where(m < P // 2, 1.0, -1.0)[:, None]
            inv[0, k, :, 0], inv[0, k, :, 1] = cos, cos * odd
            inv[1, k, :, 0], inv[1, k, :, 1] = -sin, -sin * odd
    inv[0, 0, 0] /= 2
    inv[1, 0, 0] = sign / 2
    inv *= 2.0 / n
    return (fwd.reshape(2, P, 2 * SEQ).astype(np.float32), fwdx.reshape(2, P, 2 * P).astype(np.float32),
            inv.reshape(2 * SEQ, 2 * P).astype(np.float32))


def kernel(**inputs):
    import concourse.bacc as bacc
    from concourse.bass_utils import run_bass_kernel_spmd

    a = {k: np.asarray(v) for k, v in inputs.items()}

    def state_rows(m):
        return m.T.reshape(STATES, 2, PAIRS).transpose(1, 0, 2).reshape(P, PAIRS)

    fwd, fwdx, inv = spectrum_matrices()
    head = np.arange(P) // DH
    lay = {
        "x": a["L0_attn_x"],
        "qkv": np.concatenate([a["L0_attn_wq"], a["L0_attn_wk"], a["L0_attn_wv"]], axis=2),
        "wo": a["L0_attn_wo"],
        "w1": a["L0_attn_w1"],
        "w2": a["L0_attn_w2"],
        "lnc": np.stack([a["L0_attn_ln1_w"], a["L0_attn_ln1_b"], a["L0_attn_ln2_w"], a["L0_attn_ln2_b"]], axis=2),
        "bo": a["L0_attn_bo"],
        "fcT": a["L0_ffn_W_fc"].T,
        "proj": a["L0_ffn_W_proj"].T,
        "winT": a["L1_attn_Win"].T,
        "woutT": a["L1_attn_Wout"].T,
        "alog": state_rows(a["L1_attn_A_log"]),
        "bmat": state_rows(a["L1_attn_B"]),
        "cmat": state_rows(a["L1_attn_C"]),
        "dtr": np.repeat(a["L1_attn_dt"].reshape(2, PAIRS), STATES, axis=0),
        "dp": a["L1_attn_Dp"].reshape(1, P),
        "bins": a["L1_attn_bin_"].reshape(1, P),
        "bouts": a["L1_attn_bout"].reshape(1, P),
        "wrT": a["L1_ffn_W_r"].T,
        "wkT": a["L1_ffn_W_k"].T,
        "wvT": a["L1_ffn_W_v"].T,
        "mu": np.stack([a["L1_ffn_mu_r"], a["L1_ffn_mu_k"]], axis=1),
        "ident": np.eye(P, dtype=np.float32),
        "cent": np.eye(P, dtype=np.float32) - np.float32(1.0 / P),
        "hmask": (head[:, None] == head[None, :]).astype(np.float32),
        "iota": np.ascontiguousarray(np.broadcast_to(np.arange(P, dtype=np.float32), (P, P))),
        "fwd": fwd, "fwdx": fwdx, "inv": inv,
    }
    nc = bacc.Bacc("TRN2", target_bir_lowering=False, num_devices=1)
    arrays, args = {}, []
    for name in _ARGS:
        v = np.ascontiguousarray(lay[name])
        arrays[f"in_{name}"] = v
        args.append(nc.dram_tensor(f"in_{name}", v.shape, mybir.dt.from_np(v.dtype), kind="ExternalInput").ap())
    args.append(nc.dram_tensor("out_0", (BATCH, SEQ, P), FP32, kind="ExternalOutput").ap())
    build(nc, *args)
    r = run_bass_kernel_spmd(nc, [arrays], core_ids=[0])
    return r.results[0]["out_0"]
```
